# Optimizing a Trainium2 kernel written in Bass

```python
import numpy as np
import jax
import jax.numpy as jnp

def _softmax(x, axis=-1):
    return jax.nn.softmax(x, axis=axis)

def _gelu(x):
    return jax.nn.gelu(x, approximate=True)

def _silu(x):
    return jax.nn.silu(x)

def _sigmoid(x):
    return jax.nn.sigmoid(x)

def _layernorm(x, axis=-1, eps=1e-05):
    m = jnp.mean(x, axis=axis, keepdims=True)
    v = jnp.var(x, axis=axis, keepdims=True)
    return (x - m) / jnp.sqrt(v + eps)

def _scatter_add(tgt, idx, src, axis=0):
    return tgt.at[idx].add(src)

def _segment_sum(src, seg, n):
    return jax.ops.segment_sum(src, seg, n)
kernel_name = 'mk_adj_seq_d4_adj_r2_2ee3d8'

def setup_inputs(seed: int=0):
    np.random.seed(seed)
    _w = jnp.asarray

    def _rec_inputs():
        import jax
        import jax.numpy as jnp
        _gk = jax.random.key(seed)
        x = -0.0002928 + 1 * jax.random.normal(jax.random.fold_in(_gk, 1), (8, 1024, 256), jnp.float32)
        _w = (1.0 + jnp.arange(1024, dtype=jnp.float32)) ** (-0.5)
        _w = _w / _w.mean()
        _pij = jnp.clip(0.0078125 * _w[:, None] * _w[None, :], 0.0, 1.0)
        _a = jax.random.uniform(jax.random.fold_in(_gk, 2), (8, 1024, 1024)) < _pij
        _af = _a.astype(jnp.float32)
        adj = _af
        return (x, adj)
    x, adj = _rec_inputs()

    def _L0_gnn_setup():
        import jax, jax.numpy as jnp
        import numpy as np
        import math
        D_MODEL = 256
        NHEAD = 8
        HEAD_DIM = D_MODEL // NHEAD
        LN_EPS = 1e-05

        def _layernorm(x, g, b):
            mu = jnp.mean(x, axis=-1, keepdims=True)
            var = jnp.mean(jnp.square(x - mu), axis=-1, keepdims=True)
            return (x - mu) * jax.lax.rsqrt(var + LN_EPS) * g + b
        key = jax.random.key(seed)
        ks = jax.random.split(key, 12)
        B, N, D = (4, 1024, D_MODEL)
        s = 1.0 / math.sqrt(D)
        inp = {'hidden': jax.random.normal(ks[0], (B, N, D), jnp.float32), 'adjacency': (jax.random.uniform(ks[1], (B, N, N)) > 0.98).astype(jnp.float32), 'Wq': jax.random.normal(ks[2], (D, D), jnp.float32) * s, 'bq': jnp.zeros((D,), jnp.float32), 'Wk': jax.random.normal(ks[3], (D, D), jnp.float32) * s, 'bk': jnp.zeros((D,), jnp.float32), 'Wv': jax.random.normal(ks[4], (D, D), jnp.float32) * s, 'bv': jnp.zeros((D,), jnp.float32), 'Wo': jax.random.normal(ks[5], (D, D), jnp.float32) * s, 'bo': jnp.zeros((D,), jnp.float32), 'g1': jnp.ones((D,), jnp.float32), 'b1': jnp.zeros((D,), jnp.float32), 'g2': jnp.ones((D,), jnp.float32), 'b2': jnp.zeros((D,), jnp.float32), 'Wf1': jax.random.normal(ks[6], (D, 4 * D), jnp.float32) * s, 'bf1': jnp.zeros((4 * D,), jnp.float32), 'Wf2': jax.random.normal(ks[7], (4 * D, D), jnp.float32) * (1.0 / math.sqrt(4 * D)), 'bf2': jnp.zeros((D,), jnp.float32)}
        return inp
    _L0_gnn_all = _L0_gnn_setup()
    _L0_gnn_in = {k: v for k, v in _L0_gnn_all.items() if k in ('Wq', 'bq', 'Wk', 'bk', 'Wv', 'bv', 'Wo', 'bo', 'g1', 'b1', 'g2', 'b2', 'Wf1', 'bf1', 'Wf2', 'bf2')}
    del _L0_gnn_all

    def _L1_gnn_setup():
        import jax, jax.numpy as jnp
        import numpy as np
        NUM_HEADS = 8
        EPS = 1e-09
        key = jax.random.key(seed)
        ks = jax.random.split(key, 8)
        B, N, D = (2, 1024, 256)
        s = 1.0 / np.sqrt(D)
        x = jax.random.normal(ks[0], (B, N, D), dtype=jnp.float32)
        adjacency = jax.random.uniform(ks[1], (B, N, N), dtype=jnp.float32)
        W_q = jax.random.normal(ks[2], (D, D), dtype=jnp.float32) * s
        W_k = jax.random.normal(ks[3], (D, D), dtype=jnp.float32) * s
        W_v = jax.random.normal(ks[4], (D, D), dtype=jnp.float32) * s
        b_q = jnp.zeros((D,), jnp.float32)
        b_k = jnp.zeros((D,), jnp.float32)
        b_v = jnp.zeros((D,), jnp.float32)
        w_g = jax.random.normal(ks[5], (2 * D,), dtype=jnp.float32) * (1.0 / np.sqrt(2 * D))
        b_g = jnp.zeros((), jnp.float32)
        return {'x': x, 'adjacency': adjacency, 'W_q': W_q, 'b_q': b_q, 'W_k': W_k, 'b_k': b_k, 'W_v': W_v, 'b_v': b_v, 'w_g': w_g, 'b_g': b_g}
    _L1_gnn_all = _L1_gnn_setup()
    _L1_gnn_in = {k: v for k, v in _L1_gnn_all.items() if k in ('W_q', 'b_q', 'W_k', 'b_k', 'W_v', 'b_v', 'w_g', 'b_g')}
    del _L1_gnn_all

    def _L2_gnn_setup():
        import jax, jax.numpy as jnp
        import numpy as np
        NUM_HID = 256
        BS, N = (8, 1024)
        NEG_BIG = -1000000000.0
        LEAKY_SLOPE = 0.01
        key = jax.random.key(seed)
        k_feats, k_adj, k_w, k_wq, k_wk = jax.random.split(key, 5)
        feats = jax.random.normal(k_feats, (BS, N, NUM_HID), dtype=jnp.float32)
        adj = (jax.random.uniform(k_adj, (BS, N, N)) < 0.05).astype(jnp.float32)
        eye = jnp.eye(N, dtype=jnp.float32)[None]
        adj_mat = jnp.maximum(adj, eye)
        s = 1.0 / np.sqrt(NUM_HID)
        W_fc = jax.random.uniform(k_w, (NUM_HID, NUM_HID), minval=-s, maxval=s, dtype=jnp.float32)
        b_fc = jnp.zeros((NUM_HID,), dtype=jnp.float32)
        w_q = jax.random.uniform(k_wq, (NUM_HID, 1), minval=-s, maxval=s, dtype=jnp.float32)
        b_q = jnp.zeros((1,), dtype=jnp.float32)
        w_k = jax.random.uniform(k_wk, (NUM_HID, 1), minval=-s, maxval=s, dtype=jnp.float32)
        b_k = jnp.zeros((1,), dtype=jnp.float32)
        return {'feats': feats, 'adj_mat': adj_mat, 'W_fc': W_fc, 'b_fc': b_fc, 'w_q': w_q, 'b_q': b_q, 'w_k': w_k, 'b_k': b_k}
    _L2_gnn_all = _L2_gnn_setup()
    _L2_gnn_in = {k: v for k, v in _L2_gnn_all.items() if k in ('W_fc', 'b_fc', 'w_q', 'b_q', 'w_k', 'b_k')}
    del _L2_gnn_all

    def _L3_gnn_setup():
        import jax, jax.numpy as jnp
        import numpy as np
        B, N, D, H = (8, 512, 256, 8)
        DK = D // H
        LN_EPS = 1e-05
        ADJ_MIN = 1e-08

        def _layer_norm(x, gamma, beta):
            mu = jnp.mean(x, axis=-1, keepdims=True)
            var = jnp.mean(jnp.square(x - mu), axis=-1, keepdims=True)
            return (x - mu) * jax.lax.rsqrt(var + LN_EPS) * gamma + beta
        key = jax.random.key(seed)
        ks = jax.random.split(key, 12)
        x = jax.random.normal(ks[0], (B, N, D), dtype=jnp.float32)
        adj = jax.random.uniform(ks[1], (B, N, N), dtype=jnp.float32)
        adj = adj / jnp.sum(adj, axis=-1, keepdims=True)
        s = 1.0 / np.sqrt(D)
        Wq = jax.random.normal(ks[2], (D, D), dtype=jnp.float32) * s
        bq = jnp.zeros((D,), dtype=jnp.float32)
        Wk = jax.random.normal(ks[3], (D, D), dtype=jnp.float32) * s
        bk = jnp.zeros((D,), dtype=jnp.float32)
        Wv = jax.random.normal(ks[4], (D, D), dtype=jnp.float32) * s
        bv = jnp.zeros((D,), dtype=jnp.float32)
        Wo = jax.random.normal(ks[5], (D, D), dtype=jnp.float32) * s
        bo = jnp.zeros((D,), dtype=jnp.float32)
        gamma = jnp.ones((D,), dtype=jnp.float32)
        beta = jnp.zeros((D,), dtype=jnp.float32)
        return {'x': x, 'adj': adj, 'Wq': Wq, 'bq': bq, 'Wk': Wk, 'bk': bk, 'Wv': Wv, 'bv': bv, 'Wo': Wo, 'bo': bo, 'gamma': gamma, 'beta': beta}
    _L3_gnn_all = _L3_gnn_setup()
    _L3_gnn_in = {k: v for k, v in _L3_gnn_all.items() if k in ('Wq', 'bq', 'Wk', 'bk', 'Wv', 'bv', 'Wo', 'bo', 'gamma', 'beta')}
    del _L3_gnn_all
    return {'x': x, 'adj': adj, 'L0_gnn_Wq': _L0_gnn_in['Wq'], 'L0_gnn_bq': _L0_gnn_in['bq'], 'L0_gnn_Wk': _L0_gnn_in['Wk'], 'L0_gnn_bk': _L0_gnn_in['bk'], 'L0_gnn_Wv': _L0_gnn_in['Wv'], 'L0_gnn_bv': _L0_gnn_in['bv'], 'L0_gnn_Wo': _L0_gnn_in['Wo'], 'L0_gnn_bo': _L0_gnn_in['bo'], 'L0_gnn_g1': _L0_gnn_in['g1'], 'L0_gnn_b1': _L0_gnn_in['b1'], 'L0_gnn_g2': _L0_gnn_in['g2'], 'L0_gnn_b2': _L0_gnn_in['b2'], 'L0_gnn_Wf1': _L0_gnn_in['Wf1'], 'L0_gnn_bf1': _L0_gnn_in['bf1'], 'L0_gnn_Wf2': _L0_gnn_in['Wf2'], 'L0_gnn_bf2': _L0_gnn_in['bf2'], 'L1_gnn_W_q': _L1_gnn_in['W_q'], 'L1_gnn_b_q': _L1_gnn_in['b_q'], 'L1_gnn_W_k': _L1_gnn_in['W_k'], 'L1_gnn_b_k': _L1_gnn_in['b_k'], 'L1_gnn_W_v': _L1_gnn_in['W_v'], 'L1_gnn_b_v': _L1_gnn_in['b_v'], 'L1_gnn_w_g': _L1_gnn_in['w_g'], 'L1_gnn_b_g': _L1_gnn_in['b_g'], 'L2_gnn_W_fc': _L2_gnn_in['W_fc'], 'L2_gnn_b_fc': _L2_gnn_in['b_fc'], 'L2_gnn_w_q': _L2_gnn_in['w_q'], 'L2_gnn_b_q': _L2_gnn_in['b_q'], 'L2_gnn_w_k': _L2_gnn_in['w_k'], 'L2_gnn_b_k': _L2_gnn_in['b_k'], 'L3_gnn_Wq': _L3_gnn_in['Wq'], 'L3_gnn_bq': _L3_gnn_in['bq'], 'L3_gnn_Wk': _L3_gnn_in['Wk'], 'L3_gnn_bk': _L3_gnn_in['bk'], 'L3_gnn_Wv': _L3_gnn_in['Wv'], 'L3_gnn_bv': _L3_gnn_in['bv'], 'L3_gnn_Wo': _L3_gnn_in['Wo'], 'L3_gnn_bo': _L3_gnn_in['bo'], 'L3_gnn_gamma': _L3_gnn_in['gamma'], 'L3_gnn_beta': _L3_gnn_in['beta']}

def reference(x, adj, L0_gnn_Wq, L0_gnn_bq, L0_gnn_Wk, L0_gnn_bk, L0_gnn_Wv, L0_gnn_bv, L0_gnn_Wo, L0_gnn_bo, L0_gnn_g1, L0_gnn_b1, L0_gnn_g2, L0_gnn_b2, L0_gnn_Wf1, L0_gnn_bf1, L0_gnn_Wf2, L0_gnn_bf2, L1_gnn_W_q, L1_gnn_b_q, L1_gnn_W_k, L1_gnn_b_k, L1_gnn_W_v, L1_gnn_b_v, L1_gnn_w_g, L1_gnn_b_g, L2_gnn_W_fc, L2_gnn_b_fc, L2_gnn_w_q, L2_gnn_b_q, L2_gnn_w_k, L2_gnn_b_k, L3_gnn_Wq, L3_gnn_bq, L3_gnn_Wk, L3_gnn_bk, L3_gnn_Wv, L3_gnn_bv, L3_gnn_Wo, L3_gnn_bo, L3_gnn_gamma, L3_gnn_beta):
    import jax
    import jax.numpy as jnp

    def _L0_gnn_ref(hidden, adjacency, Wq, bq, Wk, bk, Wv, bv, Wo, bo, g1, b1, g2, b2, Wf1, bf1, Wf2, bf2):
        import jax, jax.numpy as jnp
        import numpy as np
        import math
        D_MODEL = 256
        NHEAD = 8
        HEAD_DIM = D_MODEL // NHEAD
        LN_EPS = 1e-05

        def _layernorm(x, g, b):
            mu = jnp.mean(x, axis=-1, keepdims=True)
            var = jnp.mean(jnp.square(x - mu), axis=-1, keepdims=True)
            return (x - mu) * jax.lax.rsqrt(var + LN_EPS) * g + b
        B, N, D = hidden.shape
        H, Hd = (NHEAD, HEAD_DIM)
        normed = _layernorm(hidden, g1, b1)
        q = (normed @ Wq + bq).reshape(B, N, H, Hd).transpose(0, 2, 1, 3)
        k = (normed @ Wk + bk).reshape(B, N, H, Hd).transpose(0, 2, 1, 3)
        v = (normed @ Wv + bv).reshape(B, N, H, Hd).transpose(0, 2, 1, 3)
        logits = jnp.einsum('bhnd,bhmd->bhnm', q, k) / math.sqrt(Hd)
        adj = adjacency[:, None, :, :]
        logits = logits + (2.0 * adj - 1.0)
        weights = jax.nn.softmax(logits, axis=-1)
        weights = weights * (0.25 + 0.75 * adj)
        weights = weights / jnp.maximum(weights.sum(axis=-1, keepdims=True), 1e-06)
        attended = jnp.einsum('bhnm,bhmd->bhnd', weights, v)
        attended = attended.transpose(0, 2, 1, 3).reshape(B, N, D)
        hidden = hidden + attended @ Wo + bo
        h2 = _layernorm(hidden, g2, b2)
        ff = jax.nn.gelu(h2 @ Wf1 + bf1, approximate=False) @ Wf2 + bf2
        return hidden + ff

    def _L1_gnn_ref(x, adjacency, W_q, b_q, W_k, b_k, W_v, b_v, w_g, b_g):
        import jax, jax.numpy as jnp
        import numpy as np
        NUM_HEADS = 8
        EPS = 1e-09
        B, N, D = x.shape
        H = NUM_HEADS
        hd = D // H
        Q = (x @ W_q + b_q).reshape(B, N, H, hd)
        K = (x @ W_k + b_k).reshape(B, N, H, hd)
        V = (x @ W_v + b_v).reshape(B, N, H, hd)
        scores = jnp.einsum('bihd,bjhd->bhij', Q, K) / jnp.sqrt(jnp.float32(hd))
        a = x @ w_g[:D]
        c = x @ w_g[D:]
        soul_bias = a[:, :, None] + c[:, None, :] + b_g
        scores = scores + (soul_bias + jnp.log(adjacency + EPS))[:, None, :, :]
        attn = jax.nn.softmax(scores, axis=-1)
        out = jnp.einsum('bhij,bjhd->bihd', attn, V).reshape(B, N, D)
        return out + x

    def _L2_gnn_ref(feats, adj_mat, W_fc, b_fc, w_q, b_q, w_k, b_k):
        import jax, jax.numpy as jnp
        import numpy as np
        NUM_HID = 256
        BS, N = (8, 1024)
        NEG_BIG = -1000000000.0
        LEAKY_SLOPE = 0.01
        feat_proj = jnp.einsum('bnd,de->bne', feats, W_fc) + b_fc
        q = jnp.einsum('bnd,do->bno', feat_proj, w_q) + b_q
        k = jnp.einsum('bnd,do->bno', feat_proj, w_k) + b_k
        logits = q + jnp.swapaxes(k, 2, 1)
        masked = logits + (1.0 - adj_mat) * NEG_BIG
        masked = jnp.where(masked >= 0, masked, LEAKY_SLOPE * masked)
        atten = jax.nn.softmax(masked, axis=-1)
        out = jnp.einsum('bnm,bmd->bnd', atten, feat_proj)
        return out + feats

    def _L3_gnn_ref(x, adj, Wq, bq, Wk, bk, Wv, bv, Wo, bo, gamma, beta):
        import jax, jax.numpy as jnp
        import numpy as np
        B, N, D, H = (8, 512, 256, 8)
        DK = D // H
        LN_EPS = 1e-05
        ADJ_MIN = 1e-08

        def _layer_norm(x, gamma, beta):
            mu = jnp.mean(x, axis=-1, keepdims=True)
            var = jnp.mean(jnp.square(x - mu), axis=-1, keepdims=True)
            return (x - mu) * jax.lax.rsqrt(var + LN_EPS) * gamma + beta
        b, n, d = x.shape
        q = (x @ Wq.T + bq).reshape(b, n, H, DK).transpose(0, 2, 1, 3)
        k = (x @ Wk.T + bk).reshape(b, n, H, DK).transpose(0, 2, 1, 3)
        v = (x @ Wv.T + bv).reshape(b, n, H, DK).transpose(0, 2, 1, 3)
        logits = jnp.einsum('bhqd,bhkd->bhqk', q, k) / np.sqrt(DK)
        logits = logits + jnp.log(jnp.clip(adj, ADJ_MIN, None))[:, None, :, :]
        attn = jax.nn.softmax(logits, axis=-1)
        out = jnp.einsum('bhqk,bhkd->bhqd', attn, v)
        out = out.transpose(0, 2, 1, 3).reshape(b, n, d)
        out = out @ Wo.T + bo
        return _layer_norm(x + out, gamma, beta)
    x = _L0_gnn_ref(x, adj, L0_gnn_Wq, L0_gnn_bq, L0_gnn_Wk, L0_gnn_bk, L0_gnn_Wv, L0_gnn_bv, L0_gnn_Wo, L0_gnn_bo, L0_gnn_g1, L0_gnn_b1, L0_gnn_g2, L0_gnn_b2, L0_gnn_Wf1, L0_gnn_bf1, L0_gnn_Wf2, L0_gnn_bf2)
    x = _L1_gnn_ref(x, adj, L1_gnn_W_q, L1_gnn_b_q, L1_gnn_W_k, L1_gnn_b_k, L1_gnn_W_v, L1_gnn_b_v, L1_gnn_w_g, L1_gnn_b_g)
    x = _L2_gnn_ref(x, adj, L2_gnn_W_fc, L2_gnn_b_fc, L2_gnn_w_q, L2_gnn_b_q, L2_gnn_w_k, L2_gnn_b_k)
    x = _L3_gnn_ref(x, adj, L3_gnn_Wq, L3_gnn_bq, L3_gnn_Wk, L3_gnn_bk, L3_gnn_Wv, L3_gnn_bv, L3_gnn_Wo, L3_gnn_bo, L3_gnn_gamma, L3_gnn_beta)
    return x

_drawn_inputs = setup_inputs


def setup_inputs(seed=0):
    import zlib

    import numpy as np

    out = dict(_drawn_inputs(seed))
    spreads = {'L0_gnn_bq': (0.0, 0.381),
     'L0_gnn_bk': (0.0, 0.8),
     'L0_gnn_bv': (0.0, 0.1),
     'L0_gnn_bo': (0.0, 0.1),
     'L0_gnn_g1': (1.0, 0.2),
     'L0_gnn_b1': (0.0, 0.1),
     'L0_gnn_g2': (1.0, 0.2),
     'L0_gnn_b2': (0.0, 0.1),
     'L0_gnn_bf1': (0.0, 0.1),
     'L0_gnn_bf2': (0.0, 0.1),
     'L1_gnn_b_q': (0.0, 0.1),
     'L1_gnn_b_k': (0.0, 0.8),
     'L1_gnn_b_v': (0.0, 0.1),
     'L2_gnn_b_fc': (0.0, 0.1),
     'L3_gnn_bq': (0.0, 0.1),
     'L3_gnn_bk': (0.0, 0.8),
     'L3_gnn_bv': (0.0, 0.1),
     'L3_gnn_bo': (0.0, 0.1),
     'L3_gnn_gamma': (1.0, 0.2),
     'L3_gnn_beta': (0.0, 0.1)}
    factors = {}
    for name, (base, spread) in spreads.items():
        noise = np.random.default_rng([zlib.crc32(name.encode()), seed]).standard_normal(out[name].shape)
        drawn = base * np.exp(spread * noise) if base else spread * noise
        out[name] = jnp.asarray(drawn.astype(out[name].dtype))
    for name, factor in factors.items():
        out[name] = (out[name] * factor).astype(out[name].dtype)
    return out
```

```python
import math
from contextlib import ExitStack

import concourse.bass as bass
from concourse import mybir

F32 = mybir.dt.float32
F32R = mybir.dt.float32r
ALU = mybir.AluOpType
ACT = mybir.ActivationFunctionType
AX = mybir.AxisListType

P = 128
BATCH, N, D = 8, 1024, 256
HEADS = 8
HD = D // HEADS
GH = P // HD
G = HEADS // GH
KC = D // P
NC = N // P
HALF = 512
HC = HALF // P
FF = 4 * D
FC = FF // P
LN_EPS = 1e-5
SCALE = float(HD) ** -0.5

STEPS = 2 * NC
MAX_FROM = 3
MAX_UNITS = GH * NC * 2
MAX_PER_STEP = 5
LAG = 2
P_SLOTS = 3
DMA = 16


def et_job(job):
    return job // 2, job % 2


X_TURN_STEPS = {8: (0, 0), 9: (0, 1), 13: (1, 0), 14: (1, 1)}
WEIGHT_LOADS = {"L0": 16, "L1": 9, "L3": 6}


def wait_from(eng, sem, count):
    if not isinstance(count, int) or count > 0:
        eng.wait_ge(sem, count)


def p_slot(s):
    return s % P_SLOTS


def edge_jobs(g, s, last):
    if g == 0:
        return [(0, 1, s + 1)] if s < 7 else []
    return [(1, 0, s - 7)] if 7 <= s < 15 and not last else []


def attention_layer(nc, sems, name, x_in, x_out, adj, w, ident, ones, sums_d, recips_d):
    is_l0, is_l1, is_l3 = name == "L0", name == "L1", name == "L3"
    n_bias = 4 if is_l1 else 0
    k_max = 3 * HD + n_bias
    k_all = k_max + 2
    stack_dmas = 2 * 3 * GH + n_bias
    last_b = BATCH - 1

    with ExitStack() as ctx:
        def sb(what, shape, dt=F32):
            return ctx.enter_context(nc.sbuf_tensor(f"{name}_{what}", shape, dt))

        def ps(what, shape):
            return ctx.enter_context(nc.psum_tensor(f"{name}_{what}", shape, F32))

        def sem(what):
            sems.append(nc.alloc_semaphore(f"{name}_{what}"))
            return sems[-1]

        qs = [sb(f"q_stack{g}", [P, GH, N], F32R) for g in range(G)]
        ks = [sb(f"k_stack{g}", [P, GH, N], F32R) for g in range(G)]
        et = sb("edge_t", [P, NC, N])
        v_sb = sb("v", [P, NC, D])
        xt = sb("x_t", [P, KC, N])
        xbuf = sb("x_rows", [P, HC, D])
        adj_sb = [sb(f"adj{i}", [P, HALF]) for i in range(2)]
        split_hi = [sb(f"split_hi{i}", [P, N], F32R) for i in range(2)]
        split_lo = [sb(f"split_lo{i}", [P, N], F32R) for i in range(2)]
        probs = sb("probs", [P, P_SLOTS, 2, 2, HALF])
        ot = sb("attended_t", [P, G, N])
        y = sb("y", [P, HC, D])
        sums = sb("sums", [P, HALF])
        sums_col = sb("sums_col", [P, 16])
        recip_col = sb("recip_col", [P, 16])
        recip_bc = sb("recip_bc", [P, HALF])
        max_part = sb("max_part", [P, GH * NC, 2])
        neg_max = sb("neg_max", [P, GH * NC])
        max_hi = sb("max_hi", [GH * NC, P], F32R)
        max_lo = sb("max_lo", [GH * NC, P], F32R)
        wq, wk, wv = (sb(f"w{c}", [P, KC, D]) for c in "qkv")
        bq, bk = sb("bq", [P, G]), sb("bk", [P, G])
        bv_bc = sb("bv_bc", [P, D])
        if is_l1:
            wg = sb("wg", [P, KC, 2])
            bg = sb("bg", [2, 1])
            ca_hi, ca_lo = sb("ca_hi", [2, N], F32R), sb("ca_lo", [2, N], F32R)
        else:
            wo = sb("wo", [P, KC, D])
            bo_bc = sb("bo_bc", [P, D])
            ln_raw, ln_mv = sb("ln_raw", [P, HC, 6]), sb("ln_mv", [P, HC, 2])
            ln_var, ln_rstd = sb("ln_var", [P, HC]), sb("ln_rstd", [P, HC])
            minus_half, ln_eps = sb("minus_half", [P, HC]), sb("ln_eps", [P, HC])
        if is_l0:
            g1, b1, g2, b2 = (sb(c, [P, KC]) for c in ("g1", "b1", "g2", "b2"))
            wf1, wf2 = sb("wf1", [P, KC, FF]), sb("wf2", [P, FC, D])
            bf1, bf2_bc = sb("bf1", [P, FC]), sb("bf2_bc", [P, D])
            edge_exp, edge_bias = sb("edge_exp", [P, HALF]), sb("edge_bias", [P, 1])
            flat = probs[:, :, :, :, :].rearrange("p s t h n -> p (s t h n)")
            hid = flat[:, 0:FC * HALF].rearrange("p (f n) -> p f n", n=HALF)
            h2t = flat[:, FC * HALF:(FC + KC) * HALF].rearrange("p (k n) -> p k n", n=HALF)
            xhat = flat[:, (FC + KC) * HALF:(FC + 2 * KC) * HALF].rearrange("p (c d) -> p c d", d=D)
        if is_l3:
            gamma_bc, beta_bc = sb("gamma_bc", [P, D]), sb("beta_bc", [P, D])
            xhat = y

        big = [ps(f"big{i}", [P, N]) for i in range(2)]
        small = [ps(f"small{i}", [P, HALF]) for i in range(2)]
        pv = ps("pv", [P, HALF])
        rowsum = ps("rowsum", [P, HALF])

        weights_loaded, w_raw_loaded, w_turned = sem("weights_loaded"), sem("w_raw_loaded"), sem("w_turned")
        w_copied, w_scaled, bg_cleared = sem("w_copied"), sem("w_scaled"), sem("bg_cleared")
        consts_ready = sem("consts_ready")
        x_loaded, res_loaded, stored = sem("x_loaded"), sem("res_loaded"), sem("stored")
        adj_loaded = [sem(f"adj_loaded{i}") for i in range(2)]
        adj_exp, adj_ready = sem("adj_exp"), sem("adj_ready")
        et_turned, et_ready = sem("et_turned"), sem("et_ready")
        xln_mv, xln_var, xln_rstd, xln_done = (sem(f"xln_{c}") for c in ("mv", "var", "rstd", "done"))
        cln_mv, cln_var, cln_rstd, cln_done = (sem(f"cln_{c}") for c in ("mv", "var", "rstd", "done"))
        x_turned, xt_ready = sem("x_turned"), sem("xt_ready")
        ca_made, ca_copied, ca_hi_ready, ca_ready = sem("ca_made"), sem("ca_copied"), sem("ca_hi_ready"), sem("ca_ready")
        qk_made, split_copied, split_ready = sem("qk_made"), sem("split_copied"), sem("split_ready")
        stack_loaded = [sem(f"stack_loaded{g}") for g in range(G)]
        v_made, v_copied, v_ready = sem("v_made"), sem("v_copied"), sem("v_ready")
        max_scored, max_taken = sem("max_scored"), sem("max_taken")
        neg_max_ready, max_turned, max_hi_ready, max_rows_ready = (
            sem(c) for c in ("neg_max_ready", "max_turned", "max_hi_ready", "max_rows_ready"))
        max_loaded = [sem(f"max_loaded{g}") for g in range(G)]
        scored, exp_done, pv_done, pv_copied = sem("scored"), sem("exp_done"), sem("pv_done"), sem("pv_copied")
        probs_ready = [sem(f"probs_ready{t}") for t in range(2)]
        sums_out, sums_in, recip_ready, recip_out, recip_in = (
            sem(c) for c in ("sums_out", "sums_in", "recip_ready", "recip_out", "recip_in"))
        ot_ready = sem("ot_ready")
        c_made, c_copied, c_biased, y_ready, gelu_done, out_ready, out_mid = (
            sem(c) for c in ("c_made", "c_copied", "c_biased", "y_ready", "gelu_done", "out_ready", "out_mid"))

        def step_no(b, g, s):
            return b * (G * STEPS) + g * STEPS + s

        def unit_no(b, g, u):
            return b * (G * MAX_UNITS) + g * MAX_UNITS + u

        def et_no(b, nh, job):
            return b * 16 + nh * 8 + job

        C_TILES = 7 if is_l0 else 1

        def jobs_at(g, s, last):
            jobs = []
            if g == 0:
                if s < 8:
                    jobs.append(("et", 0, 1, s))
                nb, ng = 0, 1
            else:
                if last:
                    return jobs
                nb, ng = 1, 0
            for u in range(max(0, (s - MAX_FROM) * MAX_PER_STEP), min(MAX_UNITS, (s - MAX_FROM + 1) * MAX_PER_STEP)):
                jobs.append(("max", nb, ng, u))
            if g == 1 and s >= 8:
                jobs.append(("et", 1, 0, s - 8))
            if g == 0 and s in X_TURN_STEPS and not last:
                jobs.append(("xt", 1, *X_TURN_STEPS[s]))
            return jobs

        n_weights = WEIGHT_LOADS[name]
        n_consts = 4 + 2 * (not is_l1) + is_l0
        block = ctx.enter_context(nc.Block())

        def rows_of(t, b, hf):
            return t[bass.ds(b, 1), hf * HALF:(hf + 1) * HALF, :].rearrange("o (c p) d -> p (o c) d", p=P)

        @block.sync
        def _(sp):
            n_w = 0

            def load(dst, src):
                nonlocal n_w
                sp.dma_start(dst, src, allow_slow_non_contiguous=True).then_inc(weights_loaded, DMA)
                n_w += DMA

            def load_x(b, hf):
                if hf == 0:
                    wait_from(sp, stored, (b - 1) * (2 * DMA))
                else:
                    sp.wait_ge(xt_ready, b * 4 + 2)
                sp.dma_start(xbuf[:, :, :], rows_of(x_in, b, hf)).then_inc(x_loaded, DMA)

            def load_adj(b, nh, job):
                c, mh = et_job(job)
                wait_from(sp, et_ready, et_no(b, nh, job) - 1)
                r0 = (nh * HC + c) * P
                sp.dma_start(adj_sb[job % 2][:, :],
                             adj[bass.ds(b, 1), r0:r0 + P, mh * HALF:(mh + 1) * HALF].rearrange("o p m -> (o p) m")
                             ).then_inc(adj_loaded[job % 2], DMA)

            def stack(b, g, which):
                sp.wait_ge(split_ready, (b * G + g) * 2 + which + 1)
                dst = (qs if which == 0 else ks)[g]
                hi, lo = split_hi[which], split_lo[which]
                parts = (hi, hi, lo) if which == 0 else (hi, lo, hi)
                for i, part in enumerate(parts):
                    for h in range(GH):
                        sp.dma_start(dst[i * HD:(i + 1) * HD, h, :].bitcast(F32),
                                     part[h * HD:(h + 1) * HD, :].bitcast(F32)).then_inc(stack_loaded[g], DMA)
                if is_l1 and which == 0:
                    sp.wait_ge(ca_ready, (b + 1) * 2)
                    for i, part in enumerate((ca_hi, ca_lo)):
                        r = 3 * HD + i
                        sp.dma_start(ks[g][r:r + 1, :, :].bitcast(F32),
                                     part[0:1, None, :].bitcast(F32).to_broadcast([1, GH, N])).then_inc(stack_loaded[g], DMA)
                        sp.dma_start(qs[g][r + 2:r + 3, :, :].bitcast(F32),
                                     part[1:2, None, :].bitcast(F32).to_broadcast([1, GH, N])).then_inc(stack_loaded[g], DMA)

            def max_rows(b, g):
                sp.wait_ge(max_rows_ready, b * G + g + 1)
                for i, part in enumerate((max_hi, max_lo)):
                    sp.dma_start(qs[g][k_max + i:k_max + i + 1, :, :].rearrange("p h (c n) -> p (h c) n", n=P).bitcast(F32),
                                 part[:, :].bitcast(F32)).then_inc(max_loaded[g], DMA)

            def norm_dma(b, q, part):
                n = b * 4 + q
                if part == 0:
                    sp.wait_ge(pv_copied, 2 * n + 2)
                    sp.dma_start(sums_d[q, :, :], sums[0:P:HD, :]).then_inc(sums_out, DMA)
                elif part == 1:
                    sp.wait_ge(sums_out, (n + 1) * DMA)
                    sp.dma_start(sums_col[:, :], sums_d[q, :, :].rearrange("h (j f) -> (h j) f", f=16)).then_inc(sums_in, DMA)
                elif part == 2:
                    sp.wait_ge(recip_ready, n + 1)
                    sp.dma_start(recips_d[q, :, :].rearrange("h (j f) -> (h j) f", f=16), recip_col[:, :]).then_inc(recip_out, DMA)
                else:
                    sp.wait_ge(recip_out, (n + 1) * DMA)
                    wait_from(sp, ot_ready, n)
                    sp.dma_start(recip_bc[:, :], recips_d[q, :, None, :].to_broadcast([GH, HD, HALF])).then_inc(recip_in, DMA)

            def close(b, last):
                for j in range(2):
                    if j == 0:
                        if last:
                            sp.wait_ge(xt_ready, BATCH * 4)
                        else:
                            sp.wait_ge(xt_ready, (b + 2) * 4)
                    else:
                        sp.wait_ge(stored, (b * 2 + 1) * DMA)
                    sp.dma_start(xbuf[:, :, :], rows_of(x_in, b, j)).then_inc(res_loaded, DMA)
                    if j == 0:
                        norm_dma(b, 3, 2)
                        norm_dma(b, 3, 3)
                    sp.wait_ge(out_ready, b * 2 + j + 1)
                    sp.dma_start(rows_of(x_out, b, j), (xbuf if is_l0 else y)[:, :, :]).then_inc(stored, DMA)

            load_x(0, 0)
            for t, n in ((wq, "Wq"), (wk, "Wk"), (wv, "Wv")) if not is_l3 else ():
                load(t[:, :, :], w[n].rearrange("(k p) o -> p k o", p=P))
            for t, n in ((bq, "bq"), (bk, "bk")):
                load(t[:, :], w[n].rearrange("(g p) -> p g", p=P))
            load(bv_bc[:, :], w["bv"][None, :].to_broadcast([P, D]))
            if is_l1:
                load(wg[:, :, 0:1], w["w_g"][D:2 * D].rearrange("(k p o) -> p k o", p=P, o=1))
                load(wg[:, :, 1:2], w["w_g"][0:D].rearrange("(k p o) -> p k o", p=P, o=1))
                sp.wait_ge(bg_cleared, 1)
                load(bg[0:1, :], w["b_g"])
            else:
                load(bo_bc[:, :], w["bo"][None, :].to_broadcast([P, D]))
            if is_l0:
                load(wo[:, :, :], w["Wo"].rearrange("(k p) o -> p k o", p=P))
                for t, n in ((g1, "g1"), (b1, "b1"), (g2, "g2"), (b2, "b2")):
                    load(t[:, :], w[n].rearrange("(k p) -> p k", p=P))
                load(wf1[:, :, :], w["Wf1"].rearrange("(k p) o -> p k o", p=P))
                load(wf2[:, :, :], w["Wf2"].rearrange("(k p) o -> p k o", p=P))
                load(bf1[:, :], w["bf1"].rearrange("(k p) -> p k", p=P))
                load(bf2_bc[:, :], w["bf2"][None, :].to_broadcast([P, D]))
            if is_l3:
                load(gamma_bc[:, :], w["gamma"][None, :].to_broadcast([P, D]))
                load(beta_bc[:, :], w["beta"][None, :].to_broadcast([P, D]))
                for i, n in enumerate(("Wq", "Wk", "Wv", "Wo")):
                    sp.dma_start(et[:, i, 0:2 * D].rearrange("p (k o) -> p k o", o=D),
                                 w[n].rearrange("(k p) i -> p k i", p=P)).then_inc(w_raw_loaded, DMA)
            assert n_w == n_weights * DMA
            load_adj(0, 0, 0)
            load_adj(0, 0, 1)
            load_x(0, 1)
            sp.wait_ge(consts_ready, n_consts)
            stack(0, 0, 0)
            stack(0, 0, 1)
            for job in range(2, 8):
                load_adj(0, 0, job)
            stack(0, 1, 0)
            stack(0, 1, 1)
            load_adj(0, 1, 0)
            load_adj(0, 1, 1)
            max_rows(0, 0)

            def graph(b, last):
                for s in range(STEPS):
                    if 1 <= s < 7:
                        load_adj(b, 1, s + 1)
                    if s == 3 and not last:
                        load_x(b + 1, 0)
                    if s == 10 and not last:
                        load_x(b + 1, 1)
                    if s in (11, 12):
                        norm_dma(b, 0, s - 11)
                    if s in (14, 15):
                        norm_dma(b, 0, s - 12)
                max_rows(b, 1)
                if not last:
                    stack(b + 1, 0, 0)
                    stack(b + 1, 0, 1)
                for s in range(STEPS):
                    if s in (0, 1):
                        norm_dma(b, 1, s)
                        if not last:
                            load_adj(b + 1, 0, s)
                    if s in (3, 4):
                        norm_dma(b, 1, s - 1)
                    if 9 <= s < 15 and not last:
                        load_adj(b + 1, 0, s - 7)
                    if s in (11, 12):
                        norm_dma(b, 2, s - 11)
                    if s in (14, 15):
                        norm_dma(b, 2, s - 12)
                norm_dma(b, 3, 0)
                norm_dma(b, 3, 1)
                if not last:
                    max_rows(b + 1, 0)
                    stack(b + 1, 1, 0)
                    stack(b + 1, 1, 1)
                    load_adj(b + 1, 1, 0)
                    load_adj(b + 1, 1, 1)
                close(b, last)

            graph(0, False)
            with sp.Fori(1, last_b) as b:
                graph(b, False)
            graph(last_b, True)
            sp.wait_ge(stored, BATCH * 2 * DMA)

        @block.tensor
        def _(pe):
            small_hist, big_hist = [None, None], [None, None]
            n_small = n_big = 0

            def small_slot(done_sem, done_value):
                nonlocal n_small
                if small_hist[-2] is not None:
                    pe.wait_ge(*small_hist[-2])
                small_hist.append((done_sem, done_value))
                n_small += 1
                return small[(n_small - 1) % 2]

            def big_slot(done_sem, done_value):
                nonlocal n_big
                if big_hist[-2] is not None:
                    pe.wait_ge(*big_hist[-2])
                big_hist.append((done_sem, done_value))
                n_big += 1
                return big[(n_big - 1) % 2]

            def turn_weights():
                pe.wait_ge(w_raw_loaded, 4 * DMA)
                for i in range(4):
                    tile = small_slot(w_copied, i + 1)
                    for k in range(KC):
                        for o in range(KC):
                            mm = pe.transpose(tile[:, k * D + o * P:k * D + (o + 1) * P],
                                              et[:, i, o * D + k * P:o * D + (k + 1) * P], ident[:, :])
                    mm.then_inc(w_turned, 1)

            def turn_x(b, hf, k):
                if is_l0:
                    pe.wait_ge(xln_done, b * 2 + hf + 1)
                else:
                    pe.wait_ge(x_loaded, (b * 2 + hf + 1) * DMA)
                tile = small_slot(xt_ready, b * 4 + hf * 2 + k + 1)
                for c in range(HC):
                    mm = pe.transpose(tile[:, c * P:(c + 1) * P], xbuf[:, c, k * P:(k + 1) * P], ident[:, :])
                mm.then_inc(x_turned, 1)

            def turn_adj(b, nh, job):
                if is_l0:
                    pe.wait_ge(adj_ready, et_no(b, nh, job) + 1)
                else:
                    pe.wait_ge(adj_loaded[job % 2], (b * 8 + nh * 4 + job // 2 + 1) * DMA)
                tile = small_slot(et_ready, et_no(b, nh, job) + 1)
                for c in range(HC):
                    mm = pe.transpose(tile[:, c * P:(c + 1) * P], adj_sb[job % 2][:, c * P:(c + 1) * P], ident[:, :])
                mm.then_inc(et_turned, 1)

            def project_ca(b):
                for hf in range(2):
                    tile = small_slot(ca_ready, b * 2 + hf + 1)
                    for k in range(KC):
                        mm = pe.matmul(tile[0:2, :], wg[:, k, :], xt[:, k, hf * HALF:(hf + 1) * HALF],
                                       start=k == 0, stop=k == KC - 1)
                    mm.then_inc(ca_made, 1)

            def project_qk(b, g, which):
                pe.wait_ge(xt_ready, (b + 1) * 4)
                tile = big_slot(split_copied, (b * G + g) * 4 + which * 2 + 2)
                wt = wq if which == 0 else wk
                for nh in range(2):
                    for k in range(KC):
                        mm = pe.matmul(tile[:, nh * HALF:(nh + 1) * HALF], wt[:, k, g * P:(g + 1) * P],
                                       xt[:, k, nh * HALF:(nh + 1) * HALF], start=k == 0, stop=k == KC - 1)
                mm.then_inc(qk_made, 1)

            def project_v(b):
                pe.wait_ge(xt_ready, (b + 1) * 4)
                for j in range(2):
                    tile = big_slot(v_copied, b * 2 + j + 1)
                    for c in range(HC):
                        for k in range(KC):
                            mm = pe.matmul(tile[:, c * D:(c + 1) * D], xt[:, k, (j * HC + c) * P:(j * HC + c + 1) * P],
                                           wv[:, k, :], start=k == 0, stop=k == KC - 1)
                    mm.then_inc(v_made, 1)

            def score_for_max(b, g, u):
                h, c, mh = u // (2 * NC), u // 2 % NC, u % 2
                if u == 0:
                    pe.wait_ge(stack_loaded[g], (b + 1) * (stack_dmas * DMA))
                tile = small_slot(max_taken, unit_no(b, g, u) + 1)
                pe.matmul(tile[:, :], qs[g][0:k_max, h, c * P:(c + 1) * P], ks[g][0:k_max, h, mh * HALF:(mh + 1) * HALF],
                          start=True, stop=True).then_inc(max_scored, 1)

            def turn_max(b, g):
                pe.wait_ge(neg_max_ready, b * G + g + 1)
                tile = small_slot(max_rows_ready, b * G + g + 1)
                pe.transpose(tile[0:GH * NC, 0:P], neg_max[:, :], ident[:, :]).then_inc(max_turned, 1)

            def job(b, j):
                kind, db, *rest = j
                {"et": turn_adj, "xt": turn_x, "max": score_for_max}[kind](b + db, *rest)

            def score(b, g, s):
                nh, mc = s // NC, s % NC
                for t in range(2):
                    tile = big_slot(exp_done, step_no(b, g, s) * 2 + t + 1)
                    for j in range(2):
                        h = 2 * t + j
                        mm = pe.matmul(tile[:, j * HALF:(j + 1) * HALF], ks[g][0:k_all, h, mc * P:(mc + 1) * P],
                                       qs[g][0:k_all, h, nh * HALF:(nh + 1) * HALF], start=True, stop=True)
                    mm.then_inc(scored, 1)

            def attend(b, g, s):
                mc = s % NC
                n = step_no(b, g, s)
                for t in range(2):
                    pe.wait_ge(probs_ready[t], n + 1)
                if mc == 0:
                    wait_from(pe, pv_copied, (b * 4 + g * 2 + s // NC) * 2)
                slot = p_slot(s)
                for h in range(GH):
                    pe.matmul(pv[h * HD:(h + 1) * HD, :], v_sb[:, mc, (g * GH + h) * HD:(g * GH + h + 1) * HD],
                              probs[:, slot, h // 2, h % 2, :], start=mc == 0, stop=mc == NC - 1)
                for h in range(GH):
                    mm = pe.matmul(rowsum[h * HD:(h + 1) * HD, :], ones[:, :], probs[:, slot, h // 2, h % 2, :],
                                   start=mc == 0, stop=mc == NC - 1)
                mm.then_inc(pv_done, 1)

            def phase(b, g, last):
                pe.wait_ge(max_loaded[g], (b + 1) * (2 * DMA))
                if g == 0:
                    pe.wait_ge(v_ready, (b + 1) * 2)
                    pe.wait_ge(split_copied, (b + 1) * (4 * G))
                    pe.wait_ge(stack_loaded[0], (b + 1) * (stack_dmas * DMA))
                for s in range(STEPS):
                    score(b, g, s)
                    for j in jobs_at(g, s, last):
                        job(b, j)
                    if s >= LAG:
                        attend(b, g, s - LAG)
                for s in range(STEPS - LAG, STEPS):
                    attend(b, g, s)

            def close(b):
                for j in range(2):
                    if j == 0:
                        pe.wait_ge(ot_ready, (b + 1) * 4)
                    tile0 = (b * 2 + j) * C_TILES
                    tile = big_slot(c_copied, tile0 + 1)
                    for c in range(HC):
                        for g in range(G):
                            o = ot[:, g, (j * HC + c) * P:(j * HC + c + 1) * P]
                            if is_l1:
                                mm = pe.transpose(tile[:, c * D + g * P:c * D + (g + 1) * P], o, ident[:, :])
                            else:
                                mm = pe.matmul(tile[:, c * D:(c + 1) * D], o, wo[:, g, :], start=g == 0, stop=g == G - 1)
                    mm.then_inc(c_made, 1)
                    if is_l0:
                        pe.wait_ge(cln_done, b * 2 + j + 1)
                        tile = big_slot(c_copied, tile0 + 2)
                        for k in range(KC):
                            for c in range(HC):
                                mm = pe.transpose(tile[:, k * HALF + c * P:k * HALF + (c + 1) * P],
                                                  xhat[:, c, k * P:(k + 1) * P], ident[:, :])
                        mm.then_inc(c_made, 1)
                        pe.wait_ge(c_copied, tile0 + 2)
                        for i in range(FC // 2):
                            tile = big_slot(c_copied, tile0 + 3 + i)
                            for jj in range(2):
                                f = 2 * i + jj
                                for k in range(KC):
                                    mm = pe.matmul(tile[:, jj * HALF:(jj + 1) * HALF], wf1[:, k, f * P:(f + 1) * P],
                                                   h2t[:, k, :], start=k == 0, stop=k == KC - 1)
                            mm.then_inc(c_made, 1)
                        tile = big_slot(c_copied, tile0 + 7)
                        pe.wait_ge(c_copied, tile0 + 6)
                        for c in range(HC):
                            for f in range(FC):
                                mm = pe.matmul(tile[:, c * D:(c + 1) * D], hid[:, f, c * P:(c + 1) * P], wf2[:, f, :],
                                               start=f == 0, stop=f == FC - 1)
                        mm.then_inc(c_made, 1)

            pe.wait_ge(consts_ready, n_consts)
            if is_l3:
                turn_weights()
                pe.wait_ge(w_copied, 4)
            for hf in range(2):
                for k in range(KC):
                    turn_x(0, hf, k)
            pe.wait_ge(weights_loaded, n_weights * DMA)
            if is_l1:
                pe.wait_ge(xt_ready, 4)
                project_ca(0)
            for g in range(G):
                for which in range(2):
                    project_qk(0, g, which)
                if g == 0:
                    for i in range(8):
                        turn_adj(0, 0, i)
            project_v(0)
            for u in range(MAX_UNITS):
                score_for_max(0, 0, u)
            turn_max(0, 0)

            def graph(b, last):
                phase(b, 0, last)
                if not last:
                    if is_l1:
                        pe.wait_ge(xt_ready, (b + 2) * 4)
                        project_ca(b + 1)
                    project_qk(b + 1, 0, 0)
                turn_max(b, 1)
                if not last:
                    project_qk(b + 1, 0, 1)
                phase(b, 1, last)
                if not last:
                    project_v(b + 1)
                    project_qk(b + 1, 1, 0)
                    turn_max(b + 1, 0)
                    project_qk(b + 1, 1, 1)
                close(b)

            def ring_readers(b):
                small_hist[:] = [(max_taken, unit_no(b, 0, MAX_UNITS - 1) + 1), (max_rows_ready, b * G + 1)]
                big_hist[:] = [(c_copied, b * (2 * C_TILES)), (c_copied, b * (2 * C_TILES))]

            first_small, first_big = n_small, n_big
            graph(0, False)
            assert (n_small - first_small) % 2 == 0 and (n_big - first_big) % 2 == 0
            with pe.Fori(1, last_b) as b:
                ring_readers(b)
                graph(b, False)
            ring_readers(last_b)
            graph(last_b, True)

        @block.scalar
        def _(act):
            def edge_nat(b, nh, job):
                act.wait_ge(adj_loaded[job % 2], (b * 8 + nh * 4 + job // 2 + 1) * DMA)
                wait_from(act, adj_ready, et_no(b, nh, job))
                act.activation(edge_exp[:, :], adj_sb[job % 2][:, :], ACT.Exp, bias=edge_bias[:, :], scale=2.0
                               ).then_inc(adj_exp, 1)

            def copy_qk(b, g, which):
                n = (b * G + g) * 2 + which
                act.wait_ge(qk_made, n + 1)
                if g == 1:
                    act.wait_ge(stack_loaded[0], (b + 1) * (stack_dmas * DMA))
                else:
                    wait_from(act, stack_loaded[1], b * (stack_dmas * DMA))
                tile = big[which]
                scale, bias = (SCALE, bq) if which == 0 else (1.0, bk)
                act.activation(split_lo[which][:, :].bitcast(F32), tile[:, :], ACT.Identity,
                               bias=bias[:, g:g + 1], scale=scale).then_inc(split_copied, 1)
                act.activation(split_hi[which][:, :], tile[:, :], ACT.Identity,
                               bias=bias[:, g:g + 1], scale=scale).then_inc(split_copied, 1)

            def copy_v(b):
                for j in range(2):
                    act.wait_ge(v_made, b * 2 + j + 1)
                    act.activation(v_sb[:, j * HC:(j + 1) * HC, :].rearrange("p c d -> p (c d)"), big[j][:, :], ACT.Copy
                                   ).then_inc(v_copied, 1)

            def exps(b, g, s):
                n = step_no(b, g, s)
                slot = p_slot(s)
                wait_from(act, pv_done, n - (P_SLOTS - 1) if s >= P_SLOTS else step_no(b, g, 0))
                for t in range(2):
                    act.wait_ge(scored, n * 2 + t + 1)
                    act.activation(probs[:, slot, t, :, :].rearrange("p h n -> p (h n)"), big[t][:, :], ACT.Exp
                                   ).then_inc(exp_done, 1)

            def copy_pv(b, q):
                n = b * 4 + q
                act.wait_ge(pv_done, (n + 1) * NC)
                wait_from(act, sums_out, n * DMA)
                act.activation(ot[:, q // 2, (q % 2) * HALF:(q % 2 + 1) * HALF], pv[:, :], ACT.Copy).then_inc(pv_copied, 1)
                act.activation(sums[:, :], rowsum[:, :], ACT.Copy).then_inc(pv_copied, 1)

            def phase(b, g, last):
                if is_l0 and g == 0:
                    edge_nat(b, 1, 0)
                for s in range(STEPS):
                    exps(b, g, s)
                    if is_l0:
                        for j in edge_jobs(g, s, last):
                            edge_nat(b + j[0], *j[1:])
                    if s == NC + LAG - 1:
                        copy_pv(b, 2 * g)
                copy_pv(b, 2 * g + 1)

            def close(b):
                for j in range(2):
                    tile0 = (b * 2 + j) * C_TILES
                    act.wait_ge(c_made, tile0 + 1)
                    wait_from(act, stored, (b * 2 + j) * DMA)
                    nb = j * C_TILES
                    act.activation(y[:, :, :].rearrange("p c d -> p (c d)"), big[nb % 2][:, :], ACT.Copy).then_inc(c_copied, 1)
                    if is_l0:
                        act.wait_ge(c_made, tile0 + 2)
                        t = big[(nb + 1) % 2]
                        for k in range(KC):
                            op = act.activation(h2t[:, k, :], t[:, k * HALF:(k + 1) * HALF], ACT.Identity,
                                                bias=b2[:, k:k + 1], scale=g2[:, k:k + 1])
                        op.then_inc(c_copied, 1)
                        for i in range(FC // 2):
                            act.wait_ge(c_made, tile0 + 3 + i)
                            t = big[(nb + 2 + i) % 2]
                            for jj in range(2):
                                f = 2 * i + jj
                                op = act.activation(hid[:, f, :], t[:, jj * HALF:(jj + 1) * HALF], ACT.Gelu, bias=bf1[:, f:f + 1])
                            op.then_inc(c_copied, 1)
                        act.wait_ge(c_made, tile0 + 7)
                        act.wait_ge(y_ready, b * 2 + j + 1)
                        act.activation(xbuf[:, :, :].rearrange("p c d -> p (c d)"), big[(nb + 6) % 2][:, :], ACT.Copy
                                       ).then_inc(c_copied, 1)

            act.wait_ge(consts_ready, n_consts)
            act.wait_ge(weights_loaded, n_weights * DMA)
            act.activation(bq[:, :], bq[:, :], ACT.Copy, scale=SCALE).then_inc(w_scaled, 1)
            act.wait_ge(w_scaled, 1)
            for g in range(G):
                for which in range(2):
                    copy_qk(0, g, which)
                if is_l0 and g == 0:
                    for i in range(8):
                        edge_nat(0, 0, i)
            copy_v(0)

            def graph(b, last):
                phase(b, 0, last)
                if not last:
                    copy_qk(b + 1, 0, 0)
                    copy_qk(b + 1, 0, 1)
                phase(b, 1, last)
                if not last:
                    copy_v(b + 1)
                    copy_qk(b + 1, 1, 0)
                    copy_qk(b + 1, 1, 1)
                close(b)

            graph(0, False)
            with act.Fori(1, last_b) as b:
                graph(b, False)
            graph(last_b, True)

        @block.vector
        def _(dve):
            n_small = 0

            def small_slot():
                nonlocal n_small
                n_small += 1
                return small[(n_small - 1) % 2]

            def layernorm_stats(src, mv_sem):
                for c in range(HC):
                    dve.bn_stats(ln_raw[:, c, :], src[:, c, :])
                dve.drain()
                for c in range(HC):
                    op = dve.bn_aggr(ln_mv[:, c, :], ln_raw[:, c, :])
                op.then_inc(mv_sem, 1)

            def layernorm_apply(dst, src, rstd_sem, done_sem, n):
                dve.wait_ge(rstd_sem, n + 1)
                for c in range(HC):
                    op = dve.tensor_scalar(dst[:, c, :], src[:, c, :], ln_mv[:, c, 0:1], ln_rstd[:, c:c + 1],
                                           ALU.subtract, ALU.mult)
                op.then_inc(done_sem, 1)

            def x_stats(b, hf):
                dve.wait_ge(x_loaded, (b * 2 + hf + 1) * DMA)
                layernorm_stats(xbuf, xln_mv)

            def x_norm(b, hf):
                layernorm_apply(xbuf, xbuf, xln_rstd, xln_done, b * 2 + hf)

            def x_to_t(b, hf, k):
                tile = small_slot()
                dve.wait_ge(x_turned, b * 4 + hf * 2 + k + 1)
                dst = xt[:, k, hf * HALF:(hf + 1) * HALF]
                if is_l0:
                    op = dve.tensor_scalar(dst, tile[:, :], g1[:, k:k + 1], b1[:, k:k + 1], ALU.mult, ALU.add)
                else:
                    op = dve.tensor_copy(dst, tile[:, :])
                op.then_inc(xt_ready, 1)

            def edge_mix(b, nh, job):
                n = et_no(b, nh, job)
                dve.wait_ge(adj_exp, n + 1)
                dve.scalar_tensor_tensor(out=adj_sb[job % 2][:, :], in0=adj_sb[job % 2][:, :], scalar=1.0 / 3.0,
                                         in1=edge_exp[:, :], op0=ALU.add, op1=ALU.mult).then_inc(adj_ready, 1)

            def edge_to_t(b, nh, job, read_until):
                c, mh = et_job(job)
                n = et_no(b, nh, job)
                tile = small_slot()
                dve.wait_ge(et_turned, n + 1)
                if read_until is not None:
                    for t in range(2):
                        wait_from(dve, probs_ready[t], read_until)
                q0 = (nh * HC + c) * P
                dst = et[:, mh * HC:(mh + 1) * HC, q0:q0 + P]
                src = tile[:, :].rearrange("p (c n) -> p c n", n=P)
                if is_l0:
                    op = dve.tensor_copy(dst, src)
                elif is_l1:
                    op = dve.tensor_scalar(dst, src, 1e-9, None, ALU.add)
                else:
                    op = dve.tensor_scalar(dst, src, 1e-8, None, ALU.max)
                op.then_inc(et_ready, 1)

            def take_max(b, g, u):
                h, c, mh = u // (2 * NC), u // 2 % NC, u % 2
                tile = small_slot()
                dve.wait_ge(max_scored, unit_no(b, g, u) + 1)
                dve.tensor_reduce(max_part[:, h * NC + c, mh:mh + 1], tile[:, :], AX.X, ALU.max).then_inc(max_taken, 1)

            def max_to_rows(b, g):
                n = b * G + g
                dve.wait_ge(max_taken, unit_no(b, g, MAX_UNITS - 1) + 1)
                dve.tensor_reduce(neg_max[:, :], max_part[:, :, :], AX.X, ALU.max, negate=True).then_inc(neg_max_ready, 1)
                tile = small_slot()[0:GH * NC, 0:P]
                dve.wait_ge(max_turned, n + 1)
                if g == 1:
                    dve.wait_ge(max_loaded[0], (b + 1) * (2 * DMA))
                else:
                    wait_from(dve, max_loaded[1], b * (2 * DMA))
                dve.tensor_copy(max_hi[:, :], tile).then_inc(max_hi_ready, 1)
                dve.wait_ge(max_hi_ready, n + 1)
                dve.tensor_tensor(max_lo[:, :], tile, max_hi[:, :].bitcast(F32), ALU.subtract).then_inc(max_rows_ready, 1)

            def take_ca(b):
                wait_from(dve, stack_loaded[1], b * (stack_dmas * DMA))
                for hf in range(2):
                    n = b * 2 + hf
                    tile = small_slot()[0:2, :]
                    cols = slice(hf * HALF, (hf + 1) * HALF)
                    dve.wait_ge(ca_made, n + 1)
                    dve.tensor_scalar(ca_lo[:, cols].bitcast(F32), tile, bg[:, 0:1], None, ALU.add).then_inc(ca_copied, 1)
                    dve.tensor_scalar(ca_hi[:, cols], tile, bg[:, 0:1], None, ALU.add).then_inc(ca_hi_ready, 1)
                    dve.wait_ge(ca_hi_ready, n + 1)
                    dve.wait_ge(ca_copied, n + 1)
                    dve.tensor_tensor(ca_lo[:, cols], ca_lo[:, cols].bitcast(F32), ca_hi[:, cols].bitcast(F32),
                                      ALU.subtract).then_inc(ca_ready, 1)

            def split(b, g, which):
                dve.wait_ge(split_copied, (b * G + g) * 4 + which * 2 + 2)
                lo, hi = split_lo[which], split_hi[which]
                dve.tensor_tensor(lo[:, :], lo[:, :].bitcast(F32), hi[:, :].bitcast(F32), ALU.subtract).then_inc(split_ready, 1)

            def weigh(b, g, s):
                n = step_no(b, g, s)
                nh, mc = s // NC, s % NC
                dve.wait_ge(et_ready, et_no(b, nh, 7) + 1)
                dve.wait_ge(exp_done, n * 2 + 2)
                pr = probs[:, p_slot(s), 1, :, :]
                dve.tensor_tensor(pr, pr, et[:, mc, None, nh * HALF:(nh + 1) * HALF].to_broadcast([P, 2, HALF]),
                                  ALU.mult).then_inc(probs_ready[1], 1)

            def recip(b, q):
                n = b * 4 + q
                dve.wait_ge(sums_in, (n + 1) * DMA)
                wait_from(dve, recip_out, n * DMA)
                dve.reciprocal(recip_col[:, :], sums_col[:, :]).then_inc(recip_ready, 1)

            def phase(b, g, last):
                if is_l0 and g == 0:
                    edge_mix(b, 1, 0)
                for s in range(STEPS):
                    for kind, db, *rest in jobs_at(g, s, last):
                        if kind == "max":
                            take_max(b + db, *rest)
                        elif kind == "xt":
                            x_to_t(b + db, *rest)
                        else:
                            edge_to_t(b + db, *rest, step_no(b, 1, 8) if db else step_no(b, 0, 0))
                    weigh(b, g, s)
                    if is_l0:
                        for db, nh, job in edge_jobs(g, s, last):
                            edge_mix(b + db, nh, job)
                        if g == 0 and not last:
                            if s in (5, 11):
                                x_stats(b + 1, s // 11)
                            if s in (6, 12):
                                x_norm(b + 1, s // 12)
                    if (g, s) == (1, 2):
                        recip(b, 1)
                    if s == 13:
                        recip(b, 2 * g)

            def close(b):
                if is_l1:
                    return
                for j in range(2):
                    n = b * 2 + j
                    dve.wait_ge(y_ready, n + 1)
                    layernorm_stats(y, cln_mv)
                    layernorm_apply(xhat, y, cln_rstd, cln_done, n)

            for g in range(G):
                dve.memset(ks[g][3 * HD:P, :, :].bitcast(F32), 1.0).then_inc(consts_ready, 1)
            if not is_l1:
                dve.memset(minus_half[:, :], -0.5).then_inc(consts_ready, 1)
                dve.memset(ln_eps[:, :], LN_EPS).then_inc(consts_ready, 1)
            if is_l0:
                dve.memset(edge_bias[:, :], math.log(0.75) - 1.0).then_inc(consts_ready, 1)
            if is_l1:
                dve.memset(bg[:, :], 0.0).then_inc(bg_cleared, 1)
            dve.wait_ge(consts_ready, n_consts)
            if is_l3:
                for i, t in enumerate((wq, wk, wv, wo)):
                    tile = small_slot()
                    dve.wait_ge(w_turned, i + 1)
                    dve.tensor_copy(t[:, :, :].rearrange("p k o -> p (k o)"), tile[:, :]).then_inc(w_copied, 1)
                dve.wait_ge(w_copied, 4)
            dve.wait_ge(weights_loaded, n_weights * DMA)
            for hf in range(2):
                if is_l0:
                    x_stats(0, hf)
                    x_norm(0, hf)
                for k in range(KC):
                    x_to_t(0, hf, k)
            if is_l1:
                take_ca(0)
            for g in range(G):
                split(0, g, 0)
                split(0, g, 1)
                if g == 0:
                    for job in range(8):
                        if is_l0:
                            edge_mix(0, 0, job)
                        edge_to_t(0, 0, job, None)
            for u in range(MAX_UNITS):
                take_max(0, 0, u)
            max_to_rows(0, 0)

            def graph(b, last):
                phase(b, 0, last)
                if not last and is_l1:
                    take_ca(b + 1)
                max_to_rows(b, 1)
                if not last:
                    split(b + 1, 0, 0)
                    split(b + 1, 0, 1)
                phase(b, 1, last)
                if not last:
                    max_to_rows(b + 1, 0)
                    split(b + 1, 1, 0)
                    split(b + 1, 1, 1)
                recip(b, 3)
                close(b)

            graph(0, False)
            with dve.Fori(1, last_b) as b:
                graph(b, False)
            graph(last_b, True)

        @block.gpsimd
        def _(pool):
            def rstd(mv_sem, var_sem, rstd_sem, n):
                pool.wait_ge(mv_sem, n + 1)
                pool.tensor_tensor(ln_var[:, :], ln_mv[:, :, 1], ln_eps[:, :], ALU.add).then_inc(var_sem, 1)
                pool.wait_ge(var_sem, n + 1)
                pool.tensor_tensor(ln_rstd[:, :], ln_var[:, :], minus_half[:, :], ALU.pow).then_inc(rstd_sem, 1)

            def rows(t):
                return t[:, None, :].to_broadcast([P, HC, D])

            def bias_v(b):
                for j in range(2):
                    pool.wait_ge(v_copied, b * 2 + j + 1)
                    part = v_sb[:, j * HC:(j + 1) * HC, :]
                    pool.tensor_tensor(part, part, rows(bv_bc), ALU.add).then_inc(v_ready, 1)

            def weigh(b, g, s):
                n = step_no(b, g, s)
                nh, mc = s // NC, s % NC
                pool.wait_ge(et_ready, et_no(b, nh, 7) + 1)
                pool.wait_ge(exp_done, n * 2 + 1)
                pr = probs[:, p_slot(s), 0, :, :]
                pool.tensor_tensor(pr, pr, et[:, mc, None, nh * HALF:(nh + 1) * HALF].to_broadcast([P, 2, HALF]),
                                   ALU.mult).then_inc(probs_ready[0], 1)

            def normalise(b, q):
                pool.wait_ge(recip_in, (b * 4 + q + 1) * DMA)
                part = ot[:, q // 2, (q % 2) * HALF:(q % 2 + 1) * HALF]
                pool.tensor_tensor(part, part, recip_bc[:, :], ALU.mult).then_inc(ot_ready, 1)

            def phase(b, g, last):
                for s in range(STEPS):
                    weigh(b, g, s)
                    if is_l0 and g == 0 and not last and s in (5, 11):
                        rstd(xln_mv, xln_var, xln_rstd, (b + 1) * 2 + s // 11)
                    if (g, s) == (1, 5):
                        normalise(b, 1)
                normalise(b, 2 * g)

            def close(b):
                for j in range(2):
                    n = b * 2 + j
                    pool.wait_ge(res_loaded, (n + 1) * DMA)
                    if not is_l1:
                        pool.tensor_tensor(xbuf[:, :, :], xbuf[:, :, :], rows(bo_bc), ALU.add).then_inc(c_biased, 1)
                        pool.wait_ge(c_biased, n + 1)
                    pool.wait_ge(c_copied, n * C_TILES + 1)
                    pool.tensor_tensor(y[:, :, :], y[:, :, :], xbuf[:, :, :], ALU.add).then_inc(out_ready if is_l1 else y_ready, 1)
                    if is_l1:
                        continue
                    rstd(cln_mv, cln_var, cln_rstd, n)
                    if is_l0:
                        pool.wait_ge(c_copied, (n + 1) * C_TILES)
                        pool.tensor_tensor(xbuf[:, :, :], xbuf[:, :, :], y[:, :, :], ALU.add).then_inc(out_mid, 1)
                        pool.wait_ge(out_mid, n + 1)
                        pool.tensor_tensor(xbuf[:, :, :], xbuf[:, :, :], rows(bf2_bc), ALU.add).then_inc(out_ready, 1)
                    else:
                        pool.wait_ge(cln_done, n + 1)
                        pool.tensor_tensor(y[:, :, :], y[:, :, :], rows(gamma_bc), ALU.mult).then_inc(out_mid, 1)
                        pool.wait_ge(out_mid, n + 1)
                        pool.tensor_tensor(y[:, :, :], y[:, :, :], rows(beta_bc), ALU.add).then_inc(out_ready, 1)

            for g in range(G):
                pool.memset(qs[g][3 * HD:P, :, :].bitcast(F32), 1.0).then_inc(consts_ready, 1)
            pool.wait_ge(consts_ready, n_consts)
            pool.wait_ge(weights_loaded, n_weights * DMA)
            if is_l0:
                for hf in range(2):
                    rstd(xln_mv, xln_var, xln_rstd, hf)
            bias_v(0)

            def graph(b, last):
                phase(b, 0, last)
                phase(b, 1, last)
                if not last:
                    bias_v(b + 1)
                normalise(b, 3)
                close(b)

            graph(0, False)
            with pool.Fori(1, last_b) as b:
                graph(b, False)
            graph(last_b, True)


def constants(nc, sems, ident, ones):
    with ExitStack() as ctx:
        cleared, made = nc.alloc_semaphore("ident_cleared"), nc.alloc_semaphore("ident_made")
        sems.extend((cleared, made))
        block = ctx.enter_context(nc.Block())

        @block.gpsimd
        def _(pool):
            pool.memset(ident[:, :], 0.0).then_inc(cleared, 1)
            pool.wait_ge(cleared, 1)
            pool.affine_select(out=ident[:, :], in_=ident[:, :], compare_op=ALU.not_equal, fill=1.0,
                               base=0, pattern=[[-1, P]], channel_multiplier=1).then_inc(made, 1)
            pool.memset(ones[:, :], 1.0).then_inc(made, 1)
            pool.wait_ge(made, 2)


def single_head_layer(nc, sems, x_in, x_out, adj, w, ident):
    NEG_BIG = -1e9
    SLOPE = 0.01
    X_STEPS, F_STEPS, QK_STEP, K_ROW_STEP, K_COPY_STEP = (3, 4), (5, 6), 7, 7, 7
    A_SLOTS = 4

    with ExitStack() as ctx:
        def sb(what, shape, dt=F32):
            return ctx.enter_context(nc.sbuf_tensor(f"L2_{what}", shape, dt))

        def sem(what):
            sems.append(nc.alloc_semaphore(f"L2_{what}"))
            return sems[-1]

        x_rows = [sb(f"x_rows{i}", [P, NC, D]) for i in range(2)]
        feat = [sb(f"feat{i}", [P, NC, D]) for i in range(2)]
        q_col = [sb(f"q_col{i}", [P, NC]) for i in range(2)]
        k_col = [sb(f"k_col{i}", [P, NC]) for i in range(2)]
        k_row = [sb(f"k_row{i}", [P, N]) for i in range(2)]
        xt = sb("x_t", [P, KC, N])
        adj_sb = [sb(f"adj{i}", [P, N]) for i in range(A_SLOTS)]
        logit = [sb(f"logit{i}", [P, N]) for i in range(2)]
        prob = [sb(f"prob{i}", [P, N]) for i in range(2)]
        prob_t = [sb(f"prob_t{i}", [P, NC, P]) for i in range(2)]
        neg_max, total, inv = sb("neg_max", [P, 4]), sb("total", [P, 4]), sb("inv", [P, 4])
        y = [sb(f"y{i}", [P, HC, D]) for i in range(2)]
        wfc, b_bc = sb("wfc", [P, KC, D]), sb("b_bc", [P, D])
        wq_bc, wk_bc, bq, bk = sb("wq_bc", [P, D]), sb("wk_bc", [P, D]), sb("bq", [P, 1]), sb("bk", [P, 1])
        minus_big = sb("minus_big", [P, 1])
        products = sb("products", [P, NC, D])

        turned = [ctx.enter_context(nc.psum_tensor(f"L2_turned{i}", [P, N], F32)) for i in range(2)]
        small = [ctx.enter_context(nc.psum_tensor(f"L2_small{i}", [P, HALF], F32)) for i in range(2)]
        out_ps = [ctx.enter_context(nc.psum_tensor(f"L2_out{i}", [P, HALF], F32)) for i in range(2)]

        weights_loaded, minus_big_ready = sem("weights_loaded"), sem("minus_big_ready")
        x_loaded = [sem(f"x_loaded{i}") for i in range(2)]
        adj_loaded = [sem(f"adj_loaded{i}") for i in range(A_SLOTS)]
        x_turned, xt_ready = sem("x_turned"), sem("xt_ready")
        f_made, f_copied, f_ready = sem("f_made"), sem("f_copied"), sem("f_ready")
        qk_ready, k_row_made, k_row_ready = sem("qk_ready"), sem("k_row_made"), sem("k_row_ready")
        mask_ready, masked, leaked, max_ready = sem("mask_ready"), sem("masked"), sem("leaked"), sem("max_ready")
        exp_done, p_turned, pt_ready = sem("exp_done"), sem("p_turned"), sem("pt_ready")
        attended, inv_ready, y_ready = sem("attended"), sem("inv_ready"), sem("y_ready")
        stored = [sem(f"stored{i}") for i in range(2)]
        n_weights = 6

        block = ctx.enter_context(nc.Block())

        def run(eng, graph):
            graph(0, 0, True, False)
            graph(1, 1, False, False)
            with eng.Fori(2, BATCH - 2, 2) as b:
                graph(b, 0, False, False)
                graph(b + 1, 1, False, False)
            graph(BATCH - 2, 0, False, False)
            graph(BATCH - 1, 1, False, True)

        @block.sync
        def _(sp):
            def load_adj(b, c, skip_wait=False):
                if not skip_wait:
                    sp.wait_ge(masked, b * NC + c - A_SLOTS + 1)
                sp.dma_start(adj_sb[c % A_SLOTS][:, :], adj[bass.ds(b, 1), c * P:(c + 1) * P, :].rearrange("o p m -> (o p) m")
                             ).then_inc(adj_loaded[c % A_SLOTS], DMA)

            def load_x(b, par):
                sp.dma_start(x_rows[par][:, :, :], x_in[bass.ds(b, 1), :, :].rearrange("o (c p) d -> p (o c) d", p=P)
                             ).then_inc(x_loaded[par], DMA)

            load_x(0, 0)
            for dst, src in ((wfc[:, :, :], w["W_fc"].rearrange("(k p) o -> p k o", p=P)),
                             (b_bc[:, :], w["b_fc"][None, :].to_broadcast([P, D])),
                             (wq_bc[:, :], w["w_q"].rearrange("d o -> o d").to_broadcast([P, D])),
                             (wk_bc[:, :], w["w_k"].rearrange("d o -> o d").to_broadcast([P, D])),
                             (bq[:, :], w["b_q"][None, :].to_broadcast([P, 1])),
                             (bk[:, :], w["b_k"][None, :].to_broadcast([P, 1]))):
                sp.dma_start(dst, src, allow_slow_non_contiguous=True).then_inc(weights_loaded, DMA)
            for c in range(A_SLOTS - 1):
                load_adj(0, c, True)

            def graph(b, par, first, last):
                for c in range(NC):
                    ahead = c + A_SLOTS - 1
                    if ahead < NC:
                        load_adj(b, ahead, first and ahead < A_SLOTS)
                    elif not last:
                        load_adj(b + 1, ahead - NC)
                    if c == 1 and not last:
                        if not first:
                            wait_from(sp, y_ready, (b + 1) * NC - NC)
                        load_x(b + 1, 1 - par)
                    if c == 2 and not first:
                        store(b - 1, 1)
                    if c == 6:
                        store(b, 0)
                if last:
                    store(b, 1)

            def store(b, hf):
                sp.wait_ge(y_ready, b * NC + hf * HC + HC)
                sp.dma_start(x_out[bass.ds(b, 1), hf * HALF:(hf + 1) * HALF, :].rearrange("o (c p) d -> p (o c) d", p=P),
                             y[hf][:, :, :]).then_inc(stored[hf], DMA)

            run(sp, graph)
            for hf in range(2):
                sp.wait_ge(stored[hf], BATCH * DMA)

        @block.tensor
        def _(pe):
            hist = [None, None]
            n_small = 0

            def small_slot(done_sem, done_value):
                nonlocal n_small
                if hist[-2] is not None:
                    pe.wait_ge(*hist[-2])
                hist.append((done_sem, done_value))
                n_small += 1
                return small[(n_small - 1) % 2]

            def turn_x(b, par, hf):
                pe.wait_ge(x_loaded[par], (b - par) * (DMA // 2) + DMA)
                for k in range(KC):
                    tile = small_slot(xt_ready, b * 4 + hf * 2 + k + 1)
                    for c in range(HC):
                        mm = pe.transpose(tile[:, c * P:(c + 1) * P], x_rows[par][:, hf * HC + c, k * P:(k + 1) * P], ident[:, :])
                    mm.then_inc(x_turned, 1)

            def project(b, hf):
                pe.wait_ge(xt_ready, (b + 1) * 4)
                for j in range(2):
                    tile = small_slot(f_copied, b * 4 + hf * 2 + j + 1)
                    for i in range(2):
                        c = hf * HC + j * 2 + i
                        for k in range(KC):
                            mm = pe.matmul(tile[:, i * D:(i + 1) * D], xt[:, k, c * P:(c + 1) * P], wfc[:, k, :],
                                           start=k == 0, stop=k == KC - 1)
                    mm.then_inc(f_made, 1)

            def spread_k(b, par):
                pe.wait_ge(qk_ready, (b + 1) * 2)
                for hf in range(2):
                    tile = small_slot(k_row_ready, b * 2 + hf + 1)
                    for i in range(HC):
                        c = hf * HC + i
                        mm = pe.matmul(tile[:, i * P:(i + 1) * P], k_col[par][:, c:c + 1].to_broadcast([P, P]), ident[:, :],
                                       start=True, stop=True)
                    mm.then_inc(k_row_made, 1)

            def turn_p(b, c):
                n = b * NC + c
                pe.wait_ge(exp_done, n + 1)
                wait_from(pe, pt_ready, n - 1)
                for m in range(NC):
                    mm = pe.transpose(turned[c % 2][:, m * P:(m + 1) * P], prob[c % 2][:, m * P:(m + 1) * P], ident[:, :])
                mm.then_inc(p_turned, 1)

            def attend(b, par, c):
                n = b * NC + c
                pe.wait_ge(pt_ready, n + 1)
                wait_from(pe, y_ready, n - 1)
                for m in range(NC):
                    mm = pe.matmul(out_ps[c % 2][:, 0:D], prob_t[c % 2][:, m, :], feat[par][:, m, :],
                                   start=m == 0, stop=m == NC - 1)
                mm.then_inc(attended, 1)

            pe.wait_ge(weights_loaded, n_weights * DMA)
            for hf in range(2):
                turn_x(0, 0, hf)
            for hf in range(2):
                project(0, hf)
            spread_k(0, 0)

            def graph(b, par, first, last):
                hist[:] = [(k_row_ready, b * 2 + 1), (k_row_ready, b * 2 + 2)]
                for c in range(NC):
                    turn_p(b, c)
                    if c:
                        attend(b, par, c - 1)
                    elif not first:
                        attend(b - 1, 1 - par, NC - 1)
                    if not last:
                        if c in X_STEPS:
                            turn_x(b + 1, 1 - par, c - X_STEPS[0])
                        if c in F_STEPS:
                            project(b + 1, c - F_STEPS[0])
                        if c == K_ROW_STEP:
                            spread_k(b + 1, 1 - par)
                if last:
                    attend(b, par, NC - 1)

            run(pe, graph)

        @block.scalar
        def _(act):
            n_small = 0

            def small_slot():
                nonlocal n_small
                n_small += 1
                return small[(n_small - 1) % 2]

            def copy_xt(b, hf):
                for k in range(KC):
                    tile = small_slot()
                    act.wait_ge(x_turned, b * 4 + hf * 2 + k + 1)
                    act.activation(xt[:, k, hf * HALF:(hf + 1) * HALF], tile[:, :], ACT.Copy).then_inc(xt_ready, 1)

            def copy_f(b, par, hf):
                for j in range(2):
                    tile = small_slot()
                    c = hf * HC + j * 2
                    act.wait_ge(f_made, b * 4 + hf * 2 + j + 1)
                    act.activation(feat[par][:, c:c + 2, :].rearrange("p c d -> p (c d)"), tile[:, :], ACT.Copy).then_inc(f_copied, 1)

            def copy_k(b, par):
                for hf in range(2):
                    tile = small_slot()
                    act.wait_ge(k_row_made, b * 2 + hf + 1)
                    act.activation(k_row[par][:, hf * HALF:(hf + 1) * HALF], tile[:, :], ACT.Copy).then_inc(k_row_ready, 1)

            def mask(b, c):
                act.wait_ge(adj_loaded[c % A_SLOTS], (b * 2 + c // A_SLOTS + 1) * DMA)
                t = adj_sb[c % A_SLOTS]
                act.activation(t[:, :], t[:, :], ACT.Identity, bias=minus_big[:, :], scale=-NEG_BIG).then_inc(mask_ready, 1)

            def exp(b, c):
                n = b * NC + c
                act.wait_ge(max_ready, n + 1)
                wait_from(act, p_turned, n - 1)
                wait_from(act, inv_ready, n - 3)
                act.activation(prob[c % 2][:, :], logit[c % 2][:, :], ACT.Exp, bias=neg_max[:, c % 4:c % 4 + 1],
                               accum_out=total[:, c % 4:c % 4 + 1]).then_inc(exp_done, 1)

            def copy_pt(b, c):
                n = b * NC + c
                act.wait_ge(p_turned, n + 1)
                wait_from(act, attended, n - 1)
                act.activation(prob_t[c % 2][:, :, :].rearrange("p m n -> p (m n)"), turned[c % 2][:, :], ACT.Copy
                               ).then_inc(pt_ready, 1)

            act.wait_ge(minus_big_ready, 1)
            mask(0, 0)
            mask(0, 1)
            for hf in range(2):
                copy_xt(0, hf)
            for hf in range(2):
                copy_f(0, 0, hf)
            copy_k(0, 0)

            def graph(b, par, first, last):
                for c in range(NC):
                    exp(b, c)
                    if c + 2 < NC:
                        mask(b, c + 2)
                    elif not last:
                        mask(b + 1, c + 2 - NC)
                    copy_pt(b, c)
                    if not last:
                        if c in X_STEPS:
                            copy_xt(b + 1, c - X_STEPS[0])
                        if c in F_STEPS:
                            copy_f(b + 1, 1 - par, c - F_STEPS[0])
                        if c == K_COPY_STEP:
                            copy_k(b + 1, 1 - par)

            run(act, graph)

        @block.vector
        def _(dve):
            def numbers(b, par):
                dve.wait_ge(f_ready, (b + 1) * 2)
                for i, (col, wt, bias) in enumerate(((q_col, wq_bc, bq), (k_col, wk_bc, bk))):
                    wait_from(dve, qk_ready, b * 2 + i)
                    for c in range(NC):
                        op = dve.tensor_tensor_reduce(products[:, c, :], feat[par][:, c, :], wt[:, :], 1.0, bias[:, 0:1], ALU.mult, ALU.add,
                                                      col[par][:, c:c + 1])
                    op.then_inc(qk_ready, 1)

            def logits(b, par, c):
                n = b * NC + c
                z = logit[c % 2]
                if c == 0:
                    dve.wait_ge(k_row_ready, (b + 1) * 2)
                    dve.wait_ge(qk_ready, (b + 1) * 2)
                dve.wait_ge(mask_ready, n + 1)
                wait_from(dve, exp_done, n - 1)
                dve.scalar_tensor_tensor(out=z[:, :], in0=k_row[par][:, :], scalar=q_col[par][:, c:c + 1],
                                         in1=adj_sb[c % A_SLOTS][:, :], op0=ALU.add, op1=ALU.add).then_inc(masked, 1)
                dve.wait_ge(masked, n + 1)
                dve.scalar_tensor_tensor(out=z[:, :], in0=z[:, :], scalar=SLOPE, in1=z[:, :], op0=ALU.mult, op1=ALU.max
                                         ).then_inc(leaked, 1)
                dve.wait_ge(leaked, n + 1)
                dve.tensor_reduce(neg_max[:, c % 4:c % 4 + 1], z[:, :], AX.X, ALU.max, negate=True).then_inc(max_ready, 1)

            def finish(b, par, c):
                n = b * NC + c
                dve.wait_ge(exp_done, n + 1)
                dve.reciprocal(inv[:, c % 4:c % 4 + 1], total[:, c % 4:c % 4 + 1]).then_inc(inv_ready, 1)
                dve.wait_ge(inv_ready, n + 1)
                dve.wait_ge(attended, n + 1)
                if c % HC == 0:
                    wait_from(dve, stored[c // HC], b * DMA)
                dve.scalar_tensor_tensor(out=y[c // HC][:, c % HC, :], in0=out_ps[c % 2][:, 0:D], scalar=inv[:, c % 4:c % 4 + 1],
                                         in1=x_rows[par][:, c, :], op0=ALU.mult, op1=ALU.add).then_inc(y_ready, 1)

            dve.memset(minus_big[:, :], NEG_BIG).then_inc(minus_big_ready, 1)
            dve.wait_ge(weights_loaded, n_weights * DMA)
            numbers(0, 0)

            def graph(b, par, first, last):
                for c in range(NC):
                    logits(b, par, c)
                    if c >= 2:
                        finish(b, par, c - 2)
                    elif not first:
                        finish(b - 1, 1 - par, NC - 2 + c)
                    if c == QK_STEP and not last:
                        numbers(b + 1, 1 - par)
                if last:
                    finish(b, par, NC - 2)
                    finish(b, par, NC - 1)

            run(dve, graph)

        @block.gpsimd
        def _(pool):
            def bias_f(b, par):
                for hf in range(2):
                    pool.wait_ge(f_copied, b * 4 + hf * 2 + 2)
                    part = feat[par][:, hf * HC:(hf + 1) * HC, :]
                    pool.tensor_tensor(part, part, b_bc[:, None, :].to_broadcast([P, HC, D]), ALU.add).then_inc(f_ready, 1)

            pool.wait_ge(weights_loaded, n_weights * DMA)
            bias_f(0, 0)

            def graph(b, par, first, last):
                if not last:
                    bias_f(b + 1, 1 - par)

            run(pool, graph)


def clear(nc, sems):
    nc.clear_and_free_semaphores(sems)
    sems.clear()
    with nc.Block():
        pass


def program(nc, x, adj, weights, out):
    between = [nc.dram_tensor(f"x_after_{n}", [BATCH, N, D], F32).ap() for n in ("L0", "L1", "L2")]
    sums_d = nc.dram_tensor("sums_by_row", [4, GH, HALF], F32).ap()
    recips_d = nc.dram_tensor("recips_by_row", [4, GH, HALF], F32).ap()
    with ExitStack() as ctx:
        ident = ctx.enter_context(nc.sbuf_tensor("ident", [P, P], F32))
        ones = ctx.enter_context(nc.sbuf_tensor("ones", [P, HD], F32))
        sems = []
        constants(nc, sems, ident, ones)
        attention_layer(nc, sems, "L0", x, between[0], adj, weights["L0"], ident, ones, sums_d, recips_d)
        clear(nc, sems)
        attention_layer(nc, sems, "L1", between[0], between[1], adj, weights["L1"], ident, ones, sums_d, recips_d)
        clear(nc, sems)
        single_head_layer(nc, sems, between[1], between[2], adj, weights["L2"], ident)
        clear(nc, sems)
        attention_layer(nc, sems, "L3", between[2], out, adj, weights["L3"], ident, ones, sums_d, recips_d)


_SAME = {n: n for n in ("Wq", "bq", "Wk", "bk", "Wv", "bv", "Wo", "bo")}
_WEIGHTS = {
    "L0": {**_SAME, **{n: n for n in ("g1", "b1", "g2", "b2", "Wf1", "bf1", "Wf2", "bf2")}},
    "L1": {"Wq": "W_q", "bq": "b_q", "Wk": "W_k", "bk": "b_k", "Wv": "W_v", "bv": "b_v", "w_g": "w_g", "b_g": "b_g"},
    "L2": {n: n for n in ("W_fc", "b_fc", "w_q", "b_q", "w_k", "b_k")},
    "L3": {**_SAME, "gamma": "gamma", "beta": "beta"},
}


def kernel(**inputs):
    import numpy as _np
    import concourse.bacc as _bacc
    from concourse import mybir as _mybir
    from concourse.bass_utils import run_bass_kernel_spmd as _run

    nc = _bacc.Bacc("TRN2", target_bir_lowering=False, num_devices=1)
    arrays = {}

    def declare(name):
        a = _np.ascontiguousarray(inputs[name])
        a = a.reshape(1, 1) if a.size == 1 and a.ndim == 0 else a
        arrays[f"in_{name}"] = a
        return nc.dram_tensor(f"in_{name}", list(a.shape), _mybir.dt.from_np(a.dtype), kind="ExternalInput").ap()

    x, adj = declare("x"), declare("adj")
    weights = {layer: {own: declare(f"{layer}_gnn_{n}") for own, n in names.items()} for layer, names in _WEIGHTS.items()}
    out = nc.dram_tensor("out", [BATCH, N, D], F32, kind="ExternalOutput").ap()
    program(nc, x, adj, weights, out)
    r = _run(nc, [arrays], core_ids=[0])
    return r.results[0]["out"]
```

```python
import math
from contextlib import ExitStack

import concourse.bass as bass
from concourse import mybir

F32 = mybir.dt.float32
F32R = mybir.dt.float32r
ALU = mybir.AluOpType
ACT = mybir.ActivationFunctionType
AX = mybir.AxisListType

P = 128
BATCH, N, D = 8, 1024, 256
HEADS = 8
HD = D // HEADS
GH = P // HD
G = HEADS // GH
KC = D // P
NC = N // P
HALF = 512
HC = HALF // P
FF = 4 * D
FC = FF // P
LN_EPS = 1e-5
SCALE = float(HD) ** -0.5

STEPS = 2 * NC
MAX_FROM, MAX_TO = 1, 15
MAX_UNITS = GH * NC * 2
LAG = 2
P_SLOTS = 3
DMA = 16


def et_job(job):
    return job // 2, job % 2


X_TURN_STEPS = {5: (0, 0), 6: (0, 1), 11: (1, 0), 12: (1, 1)}
QK_STEP = 13
CLOSE_STEPS = (6, 10)
WEIGHT_LOADS = {"L0": 16, "L1": 9, "L3": 6}


def wait_from(eng, sem, count):
    if not isinstance(count, int) or count > 0:
        eng.wait_ge(sem, count)


def p_slot(s):
    return s % P_SLOTS


def edge_jobs(g, s, last):
    if g == 0:
        return [(0, 1, s + 1)] if s < 7 else []
    return [(1, 0, s - 7)] if 7 <= s < 15 and not last else []


def attention_layer(nc, sems, name, x_in, x_out, adj, w, ident, ones, sums_d, recips_d):
    is_l0, is_l1, is_l3 = name == "L0", name == "L1", name == "L3"
    n_bias = 4 if is_l1 else 0
    k_max = 3 * HD + n_bias
    k_all = k_max + 2
    head_dmas = 2 * 3
    last_b = BATCH - 1

    with ExitStack() as ctx:
        def sb(what, shape, dt=F32):
            return ctx.enter_context(nc.sbuf_tensor(f"{name}_{what}", shape, dt))

        def ps(what, shape):
            return ctx.enter_context(nc.psum_tensor(f"{name}_{what}", shape, F32))

        def sem(what):
            sems.append(nc.alloc_semaphore(f"{name}_{what}"))
            return sems[-1]

        qs = [sb(f"q_stack{g}", [P, GH, N], F32R) for g in range(G)]
        ks = [sb(f"k_stack{g}", [P, GH, N], F32R) for g in range(G)]
        et = sb("edge_t", [P, NC, N])
        v_sb = sb("v", [P, NC, D])
        xt = sb("x_t", [P, KC, N])
        xbuf = sb("x_rows", [P, HC, D])
        adj_sb = [sb(f"adj{i}", [P, HALF]) for i in range(2)]
        split_hi = [sb(f"split_hi{i}", [P, N], F32R) for i in range(2)]
        split_lo = [sb(f"split_lo{i}", [P, N], F32R) for i in range(2)]
        probs = sb("probs", [P, P_SLOTS, 2, 2, HALF])
        ot = sb("attended_t", [P, G, N])
        y = [sb(f"y{i}", [P, HC, D]) for i in range(1 if is_l0 else 2)]
        sums = sb("sums", [P, HALF])
        sums_col = sb("sums_col", [P, 16])
        recip_col = sb("recip_col", [P, 16])
        recip_bc = sb("recip_bc", [P, HALF])
        max_part = sb("max_part", [P, GH * NC, 2])
        neg_max = sb("neg_max", [P, GH * NC])
        max_hi = sb("max_hi", [GH * NC, P], F32R)
        max_lo = sb("max_lo", [GH * NC, P], F32R)
        wq, wk, wv = (sb(f"w{c}", [P, KC, D]) for c in "qkv")
        bq, bk = sb("bq", [P, G]), sb("bk", [P, G])
        bv_bc = sb("bv_bc", [P, D])
        if not is_l0:
            res = sb("residual", [P, NC, D])
        if is_l1:
            wg = sb("wg", [P, KC, 2])
            bg = sb("bg", [2, 1])
            ca_hi, ca_lo = sb("ca_hi", [2, N], F32R), sb("ca_lo", [2, N], F32R)
        else:
            wo = sb("wo", [P, KC, D])
            bo_bc = sb("bo_bc", [P, D])
            ln_raw, ln_mv = sb("ln_raw", [P, HC, 6]), sb("ln_mv", [P, HC, 2])
            ln_var, ln_rstd = sb("ln_var", [P, HC]), sb("ln_rstd", [P, HC])
            minus_half, ln_eps = sb("minus_half", [P, HC]), sb("ln_eps", [P, HC])
        if is_l0:
            g1, b1, g2, b2 = (sb(c, [P, KC]) for c in ("g1", "b1", "g2", "b2"))
            wf1, wf2 = sb("wf1", [P, KC, FF]), sb("wf2", [P, FC, D])
            bf1, bf2_bc = sb("bf1", [P, FC]), sb("bf2_bc", [P, D])
            edge_exp, edge_bias = sb("edge_exp", [P, HALF]), sb("edge_bias", [P, 1])
            flat = probs[:, :, :, :, :].rearrange("p s t h n -> p (s t h n)")
            hid = flat[:, 0:FC * HALF].rearrange("p (f n) -> p f n", n=HALF)
            h2t = flat[:, FC * HALF:(FC + KC) * HALF].rearrange("p (k n) -> p k n", n=HALF)
            xhat = flat[:, (FC + KC) * HALF:(FC + 2 * KC) * HALF].rearrange("p (c d) -> p c d", d=D)
        if is_l3:
            gamma_bc, beta_bc = sb("gamma_bc", [P, D]), sb("beta_bc", [P, D])

        big = [ps(f"big{i}", [P, N]) for i in range(2)]
        small = [ps(f"small{i}", [P, HALF]) for i in range(2)]
        pv = ps("pv", [P, HALF])
        rowsum = ps("rowsum", [P, HALF])

        weights_loaded, w_raw_loaded, w_turned = sem("weights_loaded"), sem("w_raw_loaded"), sem("w_turned")
        w_copied, w_scaled, bg_cleared = sem("w_copied"), sem("w_scaled"), sem("bg_cleared")
        consts_ready = sem("consts_ready")
        x_loaded, res_loaded, stored = sem("x_loaded"), sem("res_loaded"), sem("stored")
        adj_loaded = [sem(f"adj_loaded{i}") for i in range(2)]
        adj_exp, adj_ready = sem("adj_exp"), sem("adj_ready")
        et_turned, et_ready = sem("et_turned"), sem("et_ready")
        xln_mv, xln_var, xln_rstd, xln_done = (sem(f"xln_{c}") for c in ("mv", "var", "rstd", "done"))
        cln_mv, cln_var, cln_rstd, cln_done = (sem(f"cln_{c}") for c in ("mv", "var", "rstd", "done"))
        x_turned, xt_ready = sem("x_turned"), sem("xt_ready")
        ca_made, ca_copied, ca_hi_ready, ca_ready = sem("ca_made"), sem("ca_copied"), sem("ca_hi_ready"), sem("ca_ready")
        qk_made, split_copied, split_ready = sem("qk_made"), sem("split_copied"), sem("split_ready")
        stack_loaded = [[sem(f"stack_loaded{g}_{h}") for h in range(GH)] for g in range(G)]
        bias_loaded = [sem(f"bias_loaded{g}") for g in range(G)]
        v_made, v_copied, v_ready = sem("v_made"), sem("v_copied"), sem("v_ready")
        max_scored, max_taken = sem("max_scored"), sem("max_taken")
        neg_max_ready, max_turned, max_hi_ready, max_rows_ready = (
            sem(c) for c in ("neg_max_ready", "max_turned", "max_hi_ready", "max_rows_ready"))
        max_loaded = [sem(f"max_loaded{g}") for g in range(G)]
        scored, exp_done, pv_done, pv_copied = sem("scored"), sem("exp_done"), sem("pv_done"), sem("pv_copied")
        probs_ready = [sem(f"probs_ready{t}") for t in range(2)]
        sums_out, sums_in, recip_ready, recip_out, recip_in = (
            sem(c) for c in ("sums_out", "sums_in", "recip_ready", "recip_out", "recip_in"))
        ot_ready = sem("ot_ready")
        c_made, c_copied, c_biased, y_ready, gelu_done, out_ready, out_mid = (
            sem(c) for c in ("c_made", "c_copied", "c_biased", "y_ready", "gelu_done", "out_ready", "out_mid"))

        def step_no(b, g, s):
            return b * (G * STEPS) + g * STEPS + s

        def unit_no(b, g, u):
            return b * (G * MAX_UNITS) + g * MAX_UNITS + u

        def et_no(b, nh, job):
            return b * 16 + nh * 8 + job

        C_TILES = 7 if is_l0 else 1

        def wait_stacks(eng, g, count):
            for h in range(GH):
                wait_from(eng, stack_loaded[g][h], count * (head_dmas * DMA))
            if is_l1:
                wait_from(eng, bias_loaded[g], count * (n_bias * DMA))

        def jobs_at(g, s, last):
            maxima, others = [], []
            if g == 0:
                if s < 8:
                    others.append(("et", 0, 1, s))
                nb, ng = 0, 1
            else:
                if last:
                    return maxima, others
                nb, ng = 1, 0
            span = MAX_TO - MAX_FROM
            if MAX_FROM <= s < MAX_TO:
                maxima = [("max", nb, ng, u) for u in range(MAX_UNITS * (s - MAX_FROM) // span,
                                                            MAX_UNITS * (s - MAX_FROM + 1) // span)]
            if g == 1 and s >= 8:
                others.append(("et", 1, 0, s - 8))
            if g == 0 and s in X_TURN_STEPS and not last:
                others.append(("xt", 1, *X_TURN_STEPS[s]))
            if is_l1 and (g, s) == (0, QK_STEP) and not last:
                others += [("ca", 1, 0), ("ca", 1, 1)]
            if s == STEPS - 1:
                others.append(("max_rows", nb, ng))
            return maxima, others

        n_weights = WEIGHT_LOADS[name]
        n_consts = 4 + 2 * (not is_l1) + is_l0
        block = ctx.enter_context(nc.Block())

        def rows_of(t, b, hf):
            return t[bass.ds(b, 1), hf * HALF:(hf + 1) * HALF, :].rearrange("o (c p) d -> p (o c) d", p=P)

        @block.sync
        def _(sp):
            n_w = 0

            def load(dst, src):
                nonlocal n_w
                sp.dma_start(dst, src, allow_slow_non_contiguous=True).then_inc(weights_loaded, DMA)
                n_w += DMA

            def load_x(b, hf):
                if is_l0 and hf == 0 and not (isinstance(b, int) and b < 2):
                    sp.wait_ge(stored, (b - 1) * (2 * DMA))
                else:
                    wait_from(sp, xt_ready, b * 4 + 2 * hf)
                sp.dma_start(xbuf[:, :, :], rows_of(x_in, b, hf)).then_inc(x_loaded, DMA)

            def load_adj(b, nh, job):
                c, mh = et_job(job)
                wait_from(sp, et_ready, et_no(b, nh, job) - 1)
                r0 = (nh * HC + c) * P
                sp.dma_start(adj_sb[job % 2][:, :],
                             adj[bass.ds(b, 1), r0:r0 + P, mh * HALF:(mh + 1) * HALF].rearrange("o p m -> (o p) m")
                             ).then_inc(adj_loaded[job % 2], DMA)

            def stack_biases(b, g):
                if is_l1:
                    for i, part in enumerate((ca_hi, ca_lo)):
                        r = 3 * HD + i
                        sp.dma_start(ks[g][r:r + 1, :, :].bitcast(F32),
                                     part[0:1, None, :].bitcast(F32).to_broadcast([1, GH, N])).then_inc(bias_loaded[g], DMA)
                        sp.dma_start(qs[g][r + 2:r + 3, :, :].bitcast(F32),
                                     part[1:2, None, :].bitcast(F32).to_broadcast([1, GH, N])).then_inc(bias_loaded[g], DMA)

            def stack(b, g, h):
                if h == 0:
                    splits, ca_halves, scores_before = (b * G + g) * 2 + 2, (b + 1) * 2, step_no(b - 1, g, STEPS) * 2
                    sp.wait_ge(split_ready, splits)
                    if is_l1:
                        sp.wait_ge(ca_ready, ca_halves)
                    wait_from(sp, scored, scores_before)
                    stack_biases(b, g)
                for which, dst in ((0, qs[g]), (1, ks[g])):
                    hi, lo = split_hi[which], split_lo[which]
                    for i, part in enumerate((hi, hi, lo) if which == 0 else (hi, lo, hi)):
                        sp.dma_start(dst[i * HD:(i + 1) * HD, h, :].bitcast(F32),
                                     part[h * HD:(h + 1) * HD, :].bitcast(F32)).then_inc(stack_loaded[g][h], DMA)

            def max_rows(b, g):
                sp.wait_ge(max_rows_ready, b * G + g + 1)
                for i, part in enumerate((max_hi, max_lo)):
                    sp.dma_start(qs[g][k_max + i:k_max + i + 1, :, :].rearrange("p h (c n) -> p (h c) n", n=P).bitcast(F32),
                                 part[:, :].bitcast(F32)).then_inc(max_loaded[g], DMA)

            def norm_dma(b, q, part):
                n = b * 4 + q
                if part == 0:
                    pv_copies, stores_before = 2 * n + 2, b * (2 * DMA)
                    if q == 2 and not is_l0:
                        wait_from(sp, stored, stores_before)
                    sp.wait_ge(pv_copied, pv_copies)
                    sp.dma_start(sums_d[q, :, :], sums[0:P:HD, :]).then_inc(sums_out, DMA)
                elif part == 1:
                    sp.wait_ge(sums_out, (n + 1) * DMA)
                    sp.dma_start(sums_col[:, :], sums_d[q, :, :].rearrange("h (j f) -> (h j) f", f=16)).then_inc(sums_in, DMA)
                elif part == 2:
                    sp.wait_ge(recip_ready, n + 1)
                    sp.dma_start(recips_d[q, :, :].rearrange("h (j f) -> (h j) f", f=16), recip_col[:, :]).then_inc(recip_out, DMA)
                else:
                    sp.wait_ge(recip_out, (n + 1) * DMA)
                    wait_from(sp, ot_ready, n)
                    sp.dma_start(recip_bc[:, :], recips_d[q, :, None, :].to_broadcast([GH, HD, HALF])).then_inc(recip_in, DMA)

            def load_residual(b):
                sp.dma_start(res[:, :, :], x_in[bass.ds(b, 1), :, :].rearrange("o (c p) d -> p (o c) d", p=P)
                             ).then_inc(res_loaded, DMA)

            def store(b, j):
                sp.wait_ge(out_ready, b * 2 + j + 1)
                sp.dma_start(rows_of(x_out, b, j), (xbuf if is_l0 else y[j])[:, :, :]).then_inc(stored, DMA)

            def close_l0(b, last):
                for j in range(2):
                    if j == 0:
                        sp.wait_ge(xt_ready, BATCH * 4 if last else (b + 2) * 4)
                    else:
                        sp.wait_ge(stored, (b * 2 + 1) * DMA)
                    sp.dma_start(xbuf[:, :, :], rows_of(x_in, b, j)).then_inc(res_loaded, DMA)
                    store(b, j)

            load_x(0, 0)
            for t, n in ((wq, "Wq"), (wk, "Wk"), (wv, "Wv")) if not is_l3 else ():
                load(t[:, :, :], w[n].rearrange("(k p) o -> p k o", p=P))
            for t, n in ((bq, "bq"), (bk, "bk")):
                load(t[:, :], w[n].rearrange("(g p) -> p g", p=P))
            load(bv_bc[:, :], w["bv"][None, :].to_broadcast([P, D]))
            if is_l1:
                load(wg[:, :, 0:1], w["w_g"][D:2 * D].rearrange("(k p o) -> p k o", p=P, o=1))
                load(wg[:, :, 1:2], w["w_g"][0:D].rearrange("(k p o) -> p k o", p=P, o=1))
                sp.wait_ge(bg_cleared, 1)
                load(bg[0:1, :], w["b_g"])
            else:
                load(bo_bc[:, :], w["bo"][None, :].to_broadcast([P, D]))
            if is_l0:
                load(wo[:, :, :], w["Wo"].rearrange("(k p) o -> p k o", p=P))
                for t, n in ((g1, "g1"), (b1, "b1"), (g2, "g2"), (b2, "b2")):
                    load(t[:, :], w[n].rearrange("(k p) -> p k", p=P))
                load(wf1[:, :, :], w["Wf1"].rearrange("(k p) o -> p k o", p=P))
                load(wf2[:, :, :], w["Wf2"].rearrange("(k p) o -> p k o", p=P))
                load(bf1[:, :], w["bf1"].rearrange("(k p) -> p k", p=P))
                load(bf2_bc[:, :], w["bf2"][None, :].to_broadcast([P, D]))
            if is_l3:
                load(gamma_bc[:, :], w["gamma"][None, :].to_broadcast([P, D]))
                load(beta_bc[:, :], w["beta"][None, :].to_broadcast([P, D]))
                for i, n in enumerate(("Wq", "Wk", "Wv", "Wo")):
                    sp.dma_start(et[:, i, 0:2 * D].rearrange("p (k o) -> p k o", o=D),
                                 w[n].rearrange("(k p) i -> p k i", p=P)).then_inc(w_raw_loaded, DMA)
            assert n_w == n_weights * DMA
            load_adj(0, 0, 0)
            load_adj(0, 0, 1)
            load_x(0, 1)
            sp.wait_ge(consts_ready, n_consts)
            for h in range(GH):
                stack(0, 0, h)
            for job in range(2, 8):
                load_adj(0, 0, job)
            load_adj(0, 1, 0)
            load_adj(0, 1, 1)
            max_rows(0, 0)

            def graph(b, first, last):
                stack(b, 1, 0)
                stack(b, 1, 1)
                if not (first or is_l0):
                    norm_dma(b - 1, 3, 0)
                load_adj(b, 1, 2)
                stack(b, 1, 2)
                if not (first or is_l0):
                    norm_dma(b - 1, 3, 1)
                    load_residual(b - 1)
                load_adj(b, 1, 3)
                stack(b, 1, 3)
                if not (first or is_l0):
                    norm_dma(b - 1, 3, 2)
                if not last:
                    load_x(b + 1, 0)
                load_adj(b, 1, 4)
                if not (first or is_l0):
                    norm_dma(b - 1, 3, 3)
                for s in range(5, STEPS):
                    if s < 8:
                        load_adj(b, 1, s)
                    if s == 8 and not last:
                        load_x(b + 1, 1)
                    if s == 11 and not (first or is_l0):
                        store(b - 1, 0)
                    if s in (11, 12):
                        norm_dma(b, 0, s - 11)
                    if s in (14, 15):
                        norm_dma(b, 0, s - 12)
                max_rows(b, 1)
                if not (first or is_l0):
                    store(b - 1, 1)
                if not last:
                    stack(b + 1, 0, 0)
                    stack(b + 1, 0, 1)
                norm_dma(b, 1, 0)
                if not last:
                    stack(b + 1, 0, 2)
                norm_dma(b, 1, 1)
                if not last:
                    stack(b + 1, 0, 3)
                    load_adj(b + 1, 0, 0)
                    load_adj(b + 1, 0, 1)
                norm_dma(b, 1, 2)
                norm_dma(b, 1, 3)
                for s in range(8, STEPS):
                    if 9 <= s < 15 and not last:
                        load_adj(b + 1, 0, s - 7)
                    if s in (11, 12):
                        norm_dma(b, 2, s - 11)
                    if s in (14, 15):
                        norm_dma(b, 2, s - 12)
                if not last:
                    load_adj(b + 1, 1, 0)
                    load_adj(b + 1, 1, 1)
                    max_rows(b + 1, 0)
                if is_l0 or last:
                    for part in range(4):
                        norm_dma(b, 3, part)
                if is_l0:
                    close_l0(b, last)
                elif last:
                    load_residual(b)
                    store(b, 0)
                    store(b, 1)

            graph(0, True, False)
            with sp.Fori(1, last_b) as b:
                graph(b, False, False)
            graph(last_b, False, True)
            sp.wait_ge(stored, BATCH * 2 * DMA)

        @block.tensor
        def _(pe):
            small_hist, big_hist = [None, None], [None, None]
            n_small = n_big = 0

            def small_slot(done_sem, done_value):
                nonlocal n_small
                if small_hist[-2] is not None:
                    pe.wait_ge(*small_hist[-2])
                small_hist.append((done_sem, done_value))
                n_small += 1
                return small[(n_small - 1) % 2]

            def big_slot(done_sem, done_value):
                nonlocal n_big
                if big_hist[-2] is not None:
                    pe.wait_ge(*big_hist[-2])
                big_hist.append((done_sem, done_value))
                n_big += 1
                return big[(n_big - 1) % 2]

            def turn_weights():
                pe.wait_ge(w_raw_loaded, 4 * DMA)
                for i in range(4):
                    tile = small_slot(w_copied, i + 1)
                    for k in range(KC):
                        for o in range(KC):
                            mm = pe.transpose(tile[:, k * D + o * P:k * D + (o + 1) * P],
                                              et[:, i, o * D + k * P:o * D + (k + 1) * P], ident[:, :])
                    mm.then_inc(w_turned, 1)

            def turn_x(b, hf, k):
                if is_l0:
                    pe.wait_ge(xln_done, b * 2 + hf + 1)
                else:
                    pe.wait_ge(x_loaded, (b * 2 + hf + 1) * DMA)
                tile = small_slot(xt_ready, b * 4 + hf * 2 + k + 1)
                for c in range(HC):
                    mm = pe.transpose(tile[:, c * P:(c + 1) * P], xbuf[:, c, k * P:(k + 1) * P], ident[:, :])
                mm.then_inc(x_turned, 1)

            def turn_adj(b, nh, job):
                if is_l0:
                    pe.wait_ge(adj_ready, et_no(b, nh, job) + 1)
                else:
                    pe.wait_ge(adj_loaded[job % 2], (b * 8 + nh * 4 + job // 2 + 1) * DMA)
                tile = small_slot(et_ready, et_no(b, nh, job) + 1)
                for c in range(HC):
                    mm = pe.transpose(tile[:, c * P:(c + 1) * P], adj_sb[job % 2][:, c * P:(c + 1) * P], ident[:, :])
                mm.then_inc(et_turned, 1)

            def project_ca(b, hf):
                pe.wait_ge(xt_ready, (b + 1) * 4)
                tile = small_slot(ca_ready, b * 2 + hf + 1)
                for k in range(KC):
                    mm = pe.matmul(tile[0:2, :], wg[:, k, :], xt[:, k, hf * HALF:(hf + 1) * HALF],
                                   start=k == 0, stop=k == KC - 1)
                mm.then_inc(ca_made, 1)

            def project_qk(b, g, which):
                pe.wait_ge(xt_ready, (b + 1) * 4)
                tile = big_slot(split_copied, (b * G + g) * 4 + which * 2 + 2)
                wt = wq if which == 0 else wk
                for nh in range(2):
                    for k in range(KC):
                        mm = pe.matmul(tile[:, nh * HALF:(nh + 1) * HALF], wt[:, k, g * P:(g + 1) * P],
                                       xt[:, k, nh * HALF:(nh + 1) * HALF], start=k == 0, stop=k == KC - 1)
                mm.then_inc(qk_made, 1)

            def project_v(b, j):
                pe.wait_ge(xt_ready, (b + 1) * 4)
                tile = big_slot(v_copied, b * 2 + j + 1)
                for c in range(HC):
                    for k in range(KC):
                        mm = pe.matmul(tile[:, c * D:(c + 1) * D], xt[:, k, (j * HC + c) * P:(j * HC + c + 1) * P],
                                       wv[:, k, :], start=k == 0, stop=k == KC - 1)
                mm.then_inc(v_made, 1)

            def score_for_max(b, g, u):
                h, c, mh = u // (2 * NC), u // 2 % NC, u % 2
                if u % (2 * NC) == 0:
                    pe.wait_ge(stack_loaded[g][h], (b + 1) * (head_dmas * DMA))
                if is_l1 and u == 0:
                    pe.wait_ge(bias_loaded[g], (b + 1) * (n_bias * DMA))
                tile = small_slot(max_taken, unit_no(b, g, u) + 1)
                pe.matmul(tile[:, :], qs[g][0:k_max, h, c * P:(c + 1) * P], ks[g][0:k_max, h, mh * HALF:(mh + 1) * HALF],
                          start=True, stop=True).then_inc(max_scored, 1)

            def turn_max(b, g):
                pe.wait_ge(neg_max_ready, b * G + g + 1)
                tile = small_slot(max_rows_ready, b * G + g + 1)
                pe.transpose(tile[0:GH * NC, 0:P], neg_max[:, :], ident[:, :]).then_inc(max_turned, 1)

            def do_job(b, j):
                kind, db, *rest = j
                {"et": turn_adj, "xt": turn_x, "ca": project_ca, "max": score_for_max, "max_rows": turn_max}[kind](b + db, *rest)

            def score(b, g, s, t):
                nh, mc = s // NC, s % NC
                tile = big_slot(exp_done, step_no(b, g, s) * 2 + t + 1)
                for j in range(2):
                    h = 2 * t + j
                    mm = pe.matmul(tile[:, j * HALF:(j + 1) * HALF], ks[g][0:k_all, h, mc * P:(mc + 1) * P],
                                   qs[g][0:k_all, h, nh * HALF:(nh + 1) * HALF], start=True, stop=True)
                mm.then_inc(scored, 1)

            def attend(b, g, s):
                mc = s % NC
                n = step_no(b, g, s)
                if s == 0:
                    pe.wait_ge(v_ready, (b + 1) * 2)
                for t in range(2):
                    pe.wait_ge(probs_ready[t], n + 1)
                if mc == 0:
                    wait_from(pe, pv_copied, (b * 4 + g * 2 + s // NC) * 2)
                for h in range(GH):
                    pe.matmul(pv[h * HD:(h + 1) * HD, :], v_sb[:, mc, (g * GH + h) * HD:(g * GH + h + 1) * HD],
                              probs[:, p_slot(s), h // 2, h % 2, :], start=mc == 0, stop=mc == NC - 1)

            def sum_probs(b, g, s):
                mc = s % NC
                for h in range(GH):
                    mm = pe.matmul(rowsum[h * HD:(h + 1) * HD, :], ones[:, :], probs[:, p_slot(s), h // 2, h % 2, :],
                                   start=mc == 0, stop=mc == NC - 1)
                mm.then_inc(pv_done, 1)

            def phase(b, g, first, last):
                pe.wait_ge(max_loaded[g], (b + 1) * (2 * DMA))
                for s in range(STEPS):
                    maxima, others = jobs_at(g, s, last)
                    score(b, g, s, 0)
                    for j in maxima[0:1]:
                        do_job(b, j)
                    score(b, g, s, 1)
                    for j in maxima[1:2] + others:
                        do_job(b, j)
                    if s == QK_STEP and not last:
                        project_qk(b + 1, g, 0)
                        project_qk(b + 1, g, 1)
                    if g == 0 and not (first or is_l0) and s in CLOSE_STEPS:
                        close_half(b - 1, CLOSE_STEPS.index(s))
                    if s >= LAG:
                        attend(b, g, s - LAG)
                    for j in maxima[2:4]:
                        do_job(b, j)
                    if s >= LAG:
                        sum_probs(b, g, s - LAG)
                    for j in maxima[4:]:
                        do_job(b, j)
                attend(b, g, STEPS - 2)
                sum_probs(b, g, STEPS - 2)
                if g == 1 and not last:
                    project_v(b + 1, 0)
                attend(b, g, STEPS - 1)
                sum_probs(b, g, STEPS - 1)
                if g == 1 and not last:
                    project_v(b + 1, 1)

            def close_half(b, j):
                if j == 0:
                    pe.wait_ge(ot_ready, (b + 1) * 4)
                tile0 = (b * 2 + j) * C_TILES
                tile = big_slot(c_copied, tile0 + 1)
                for c in range(HC):
                    for g in range(G):
                        o = ot[:, g, (j * HC + c) * P:(j * HC + c + 1) * P]
                        if is_l1:
                            mm = pe.transpose(tile[:, c * D + g * P:c * D + (g + 1) * P], o, ident[:, :])
                        else:
                            mm = pe.matmul(tile[:, c * D:(c + 1) * D], o, wo[:, g, :], start=g == 0, stop=g == G - 1)
                mm.then_inc(c_made, 1)
                if is_l0:
                    pe.wait_ge(cln_done, b * 2 + j + 1)
                    tile = big_slot(c_copied, tile0 + 2)
                    for k in range(KC):
                        for c in range(HC):
                            mm = pe.transpose(tile[:, k * HALF + c * P:k * HALF + (c + 1) * P],
                                              xhat[:, c, k * P:(k + 1) * P], ident[:, :])
                    mm.then_inc(c_made, 1)
                    pe.wait_ge(c_copied, tile0 + 2)
                    for i in range(FC // 2):
                        tile = big_slot(c_copied, tile0 + 3 + i)
                        for jj in range(2):
                            f = 2 * i + jj
                            for k in range(KC):
                                mm = pe.matmul(tile[:, jj * HALF:(jj + 1) * HALF], wf1[:, k, f * P:(f + 1) * P],
                                               h2t[:, k, :], start=k == 0, stop=k == KC - 1)
                        mm.then_inc(c_made, 1)
                    tile = big_slot(c_copied, tile0 + 7)
                    pe.wait_ge(c_copied, tile0 + 6)
                    for c in range(HC):
                        for f in range(FC):
                            mm = pe.matmul(tile[:, c * D:(c + 1) * D], hid[:, f, c * P:(c + 1) * P], wf2[:, f, :],
                                           start=f == 0, stop=f == FC - 1)
                    mm.then_inc(c_made, 1)

            pe.wait_ge(consts_ready, n_consts)
            if is_l3:
                turn_weights()
                pe.wait_ge(w_copied, 4)
            for hf in range(2):
                for k in range(KC):
                    turn_x(0, hf, k)
            pe.wait_ge(weights_loaded, n_weights * DMA)
            if is_l1:
                project_ca(0, 0)
                project_ca(0, 1)
            for g in range(G):
                for which in range(2):
                    project_qk(0, g, which)
                if g == 0:
                    for i in range(8):
                        turn_adj(0, 0, i)
            project_v(0, 0)
            project_v(0, 1)
            for u in range(MAX_UNITS):
                score_for_max(0, 0, u)
            turn_max(0, 0)

            def graph(b, first, last):
                phase(b, 0, first, last)
                phase(b, 1, first, last)
                if is_l0 or last:
                    close_half(b, 0)
                    close_half(b, 1)

            def ring_readers(b):
                small_hist[:] = [(et_ready, et_no(b, 0, 7) + 1), (max_rows_ready, b * G + 1)]
                if is_l0:
                    big_hist[:] = [(c_copied, b * (2 * C_TILES))] * 2
                else:
                    big_hist[:] = [(v_copied, b * 2 + 1), (v_copied, b * 2 + 2)]

            first_small, first_big = n_small, n_big
            graph(0, True, False)
            assert (n_small - first_small) % 2 == 0 and (n_big - first_big) % 2 == 0
            with pe.Fori(1, last_b) as b:
                ring_readers(b)
                graph(b, False, False)
            assert (n_small - first_small) % 2 == 0 and (n_big - first_big) % 2 == 0
            ring_readers(last_b)
            graph(last_b, False, True)

        @block.scalar
        def _(act):
            n_big = 0

            def big_slot():
                nonlocal n_big
                n_big += 1
                return big[(n_big - 1) % 2]

            def edge_nat(b, nh, job):
                act.wait_ge(adj_loaded[job % 2], (b * 8 + nh * 4 + job // 2 + 1) * DMA)
                wait_from(act, adj_ready, et_no(b, nh, job))
                act.activation(edge_exp[:, :], adj_sb[job % 2][:, :], ACT.Exp, bias=edge_bias[:, :], scale=2.0
                               ).then_inc(adj_exp, 1)

            def copy_qk(b, g, which):
                n = (b * G + g) * 2 + which
                act.wait_ge(qk_made, n + 1)
                wait_stacks(act, 1 - g, b + g)
                tile = big_slot()
                scale, bias = (SCALE, bq) if which == 0 else (1.0, bk)
                act.activation(split_lo[which][:, :].bitcast(F32), tile[:, :], ACT.Identity,
                               bias=bias[:, g:g + 1], scale=scale).then_inc(split_copied, 1)
                act.activation(split_hi[which][:, :], tile[:, :], ACT.Identity,
                               bias=bias[:, g:g + 1], scale=scale).then_inc(split_copied, 1)

            def copy_v(b, j):
                act.wait_ge(v_made, b * 2 + j + 1)
                wait_from(act, pv_done, step_no(b, 0, 0))
                act.activation(v_sb[:, j * HC:(j + 1) * HC, :].rearrange("p c d -> p (c d)"), big_slot()[:, :], ACT.Copy
                               ).then_inc(v_copied, 1)

            def exps(b, g, s):
                n = step_no(b, g, s)
                slot = p_slot(s)
                wait_from(act, pv_done, n - (P_SLOTS - 1) if s >= P_SLOTS else step_no(b, g, 0))
                for t in range(2):
                    act.wait_ge(scored, n * 2 + t + 1)
                    act.activation(probs[:, slot, t, :, :].rearrange("p h n -> p (h n)"), big_slot()[:, :], ACT.Exp
                                   ).then_inc(exp_done, 1)

            def copy_pv(b, q):
                n = b * 4 + q
                act.wait_ge(pv_done, (n + 1) * NC)
                wait_from(act, sums_out, n * DMA)
                act.activation(ot[:, q // 2, (q % 2) * HALF:(q % 2 + 1) * HALF], pv[:, :], ACT.Copy).then_inc(pv_copied, 1)
                act.activation(sums[:, :], rowsum[:, :], ACT.Copy).then_inc(pv_copied, 1)

            def phase(b, g, first, last):
                if is_l0 and g == 0:
                    edge_nat(b, 1, 0)
                for s in range(STEPS):
                    exps(b, g, s)
                    if is_l0:
                        for j in edge_jobs(g, s, last):
                            edge_nat(b + j[0], *j[1:])
                    if s == QK_STEP and not last:
                        copy_qk(b + 1, g, 0)
                        copy_qk(b + 1, g, 1)
                    if g == 0 and not (first or is_l0) and s in CLOSE_STEPS:
                        close_half(b - 1, CLOSE_STEPS.index(s))
                    if s == NC + LAG - 1:
                        copy_pv(b, 2 * g)
                if g == 1 and not last:
                    copy_v(b + 1, 0)
                copy_pv(b, 2 * g + 1)
                if g == 1 and not last:
                    copy_v(b + 1, 1)

            def close_half(b, j):
                tile0 = (b * 2 + j) * C_TILES
                act.wait_ge(c_made, tile0 + 1)
                if is_l0:
                    wait_from(act, stored, (b * 2 + j) * DMA)
                act.activation(y[j % len(y)][:, :, :].rearrange("p c d -> p (c d)"), big_slot()[:, :], ACT.Copy).then_inc(c_copied, 1)
                if is_l0:
                    act.wait_ge(c_made, tile0 + 2)
                    t = big_slot()
                    for k in range(KC):
                        op = act.activation(h2t[:, k, :], t[:, k * HALF:(k + 1) * HALF], ACT.Identity,
                                            bias=b2[:, k:k + 1], scale=g2[:, k:k + 1])
                    op.then_inc(c_copied, 1)
                    for i in range(FC // 2):
                        act.wait_ge(c_made, tile0 + 3 + i)
                        t = big_slot()
                        for jj in range(2):
                            f = 2 * i + jj
                            op = act.activation(hid[:, f, :], t[:, jj * HALF:(jj + 1) * HALF], ACT.Gelu, bias=bf1[:, f:f + 1])
                        op.then_inc(c_copied, 1)
                    act.wait_ge(c_made, tile0 + 7)
                    act.wait_ge(y_ready, b * 2 + j + 1)
                    act.activation(xbuf[:, :, :].rearrange("p c d -> p (c d)"), big_slot()[:, :], ACT.Copy
                                   ).then_inc(c_copied, 1)

            act.wait_ge(consts_ready, n_consts)
            act.wait_ge(weights_loaded, n_weights * DMA)
            act.activation(bq[:, :], bq[:, :], ACT.Copy, scale=SCALE).then_inc(w_scaled, 1)
            act.wait_ge(w_scaled, 1)
            for g in range(G):
                for which in range(2):
                    copy_qk(0, g, which)
                if is_l0 and g == 0:
                    for i in range(8):
                        edge_nat(0, 0, i)
            copy_v(0, 0)
            copy_v(0, 1)

            def graph(b, first, last):
                phase(b, 0, first, last)
                phase(b, 1, first, last)
                if is_l0 or last:
                    close_half(b, 0)
                    close_half(b, 1)

            graph(0, True, False)
            with act.Fori(1, last_b) as b:
                graph(b, False, False)
            graph(last_b, False, True)

        @block.vector
        def _(dve):
            n_small = 0

            def small_slot():
                nonlocal n_small
                n_small += 1
                return small[(n_small - 1) % 2]

            def layernorm_stats(src, mv_sem):
                for c in range(HC):
                    dve.bn_stats(ln_raw[:, c, :], src[:, c, :])
                dve.drain()
                for c in range(HC):
                    op = dve.bn_aggr(ln_mv[:, c, :], ln_raw[:, c, :])
                op.then_inc(mv_sem, 1)

            def layernorm_apply(dst, src, rstd_sem, done_sem, n):
                dve.wait_ge(rstd_sem, n + 1)
                for c in range(HC):
                    op = dve.tensor_scalar(dst[:, c, :], src[:, c, :], ln_mv[:, c, 0:1], ln_rstd[:, c:c + 1],
                                           ALU.subtract, ALU.mult)
                op.then_inc(done_sem, 1)

            def x_stats(b, hf):
                dve.wait_ge(x_loaded, (b * 2 + hf + 1) * DMA)
                layernorm_stats(xbuf, xln_mv)

            def x_norm(b, hf):
                layernorm_apply(xbuf, xbuf, xln_rstd, xln_done, b * 2 + hf)

            def x_to_t(b, hf, k):
                tile = small_slot()
                dve.wait_ge(x_turned, b * 4 + hf * 2 + k + 1)
                dst = xt[:, k, hf * HALF:(hf + 1) * HALF]
                if is_l0:
                    op = dve.tensor_scalar(dst, tile[:, :], g1[:, k:k + 1], b1[:, k:k + 1], ALU.mult, ALU.add)
                else:
                    op = dve.tensor_copy(dst, tile[:, :])
                op.then_inc(xt_ready, 1)

            def edge_mix(b, nh, job):
                n = et_no(b, nh, job)
                dve.wait_ge(adj_exp, n + 1)
                dve.scalar_tensor_tensor(out=adj_sb[job % 2][:, :], in0=adj_sb[job % 2][:, :], scalar=1.0 / 3.0,
                                         in1=edge_exp[:, :], op0=ALU.add, op1=ALU.mult).then_inc(adj_ready, 1)

            def edge_to_t(b, nh, job, read_until):
                c, mh = et_job(job)
                n = et_no(b, nh, job)
                tile = small_slot()
                dve.wait_ge(et_turned, n + 1)
                if read_until is not None:
                    for t in range(2):
                        wait_from(dve, probs_ready[t], read_until)
                q0 = (nh * HC + c) * P
                dst = et[:, mh * HC:(mh + 1) * HC, q0:q0 + P]
                src = tile[:, :].rearrange("p (c n) -> p c n", n=P)
                if is_l0:
                    op = dve.tensor_copy(dst, src)
                elif is_l1:
                    op = dve.tensor_scalar(dst, src, 1e-9, None, ALU.add)
                else:
                    op = dve.tensor_scalar(dst, src, 1e-8, None, ALU.max)
                op.then_inc(et_ready, 1)

            def take_max(b, g, u):
                h, c, mh = u // (2 * NC), u // 2 % NC, u % 2
                tile = small_slot()
                dve.wait_ge(max_scored, unit_no(b, g, u) + 1)
                dve.tensor_reduce(max_part[:, h * NC + c, mh:mh + 1], tile[:, :], AX.X, ALU.max).then_inc(max_taken, 1)

            def negate_max(b, g):
                dve.wait_ge(max_taken, unit_no(b, g, MAX_UNITS - 1) + 1)
                dve.tensor_reduce(neg_max[:, :], max_part[:, :, :], AX.X, ALU.max, negate=True).then_inc(neg_max_ready, 1)

            def max_to_rows(b, g):
                n = b * G + g
                tile = small_slot()[0:GH * NC, 0:P]
                dve.wait_ge(max_turned, n + 1)
                wait_from(dve, max_loaded[1 - g], (b + g) * (2 * DMA))
                dve.tensor_copy(max_hi[:, :], tile).then_inc(max_hi_ready, 1)
                dve.wait_ge(max_hi_ready, n + 1)
                dve.tensor_tensor(max_lo[:, :], tile, max_hi[:, :].bitcast(F32), ALU.subtract).then_inc(max_rows_ready, 1)

            def take_ca(b, hf):
                if hf == 0:
                    wait_from(dve, bias_loaded[1], b * (n_bias * DMA))
                n = b * 2 + hf
                tile = small_slot()[0:2, :]
                cols = slice(hf * HALF, (hf + 1) * HALF)
                dve.wait_ge(ca_made, n + 1)
                dve.tensor_scalar(ca_lo[:, cols].bitcast(F32), tile, bg[:, 0:1], None, ALU.add).then_inc(ca_copied, 1)
                dve.tensor_scalar(ca_hi[:, cols], tile, bg[:, 0:1], None, ALU.add).then_inc(ca_hi_ready, 1)
                dve.wait_ge(ca_hi_ready, n + 1)
                dve.wait_ge(ca_copied, n + 1)
                dve.tensor_tensor(ca_lo[:, cols], ca_lo[:, cols].bitcast(F32), ca_hi[:, cols].bitcast(F32),
                                  ALU.subtract).then_inc(ca_ready, 1)

            def split(b, g, which):
                dve.wait_ge(split_copied, (b * G + g) * 4 + which * 2 + 2)
                lo, hi = split_lo[which], split_hi[which]
                dve.tensor_tensor(lo[:, :], lo[:, :].bitcast(F32), hi[:, :].bitcast(F32), ALU.subtract).then_inc(split_ready, 1)

            def weigh(b, g, s):
                n = step_no(b, g, s)
                nh, mc = s // NC, s % NC
                dve.wait_ge(et_ready, et_no(b, nh, 7) + 1)
                dve.wait_ge(exp_done, n * 2 + 2)
                pr = probs[:, p_slot(s), 1, :, :]
                dve.tensor_tensor(pr, pr, et[:, mc, None, nh * HALF:(nh + 1) * HALF].to_broadcast([P, 2, HALF]),
                                  ALU.mult).then_inc(probs_ready[1], 1)

            def recip(b, q):
                n = b * 4 + q
                dve.wait_ge(sums_in, (n + 1) * DMA)
                wait_from(dve, recip_out, n * DMA)
                dve.reciprocal(recip_col[:, :], sums_col[:, :]).then_inc(recip_ready, 1)

            def do_job(b, j):
                kind, db, *rest = j
                if kind == "et":
                    edge_to_t(b + db, *rest, step_no(b, 1, 8) if db else step_no(b, 0, 0))
                else:
                    {"xt": x_to_t, "ca": take_ca, "max": take_max, "max_rows": max_to_rows}[kind](b + db, *rest)

            def phase(b, g, first, last):
                if is_l0 and g == 0:
                    edge_mix(b, 1, 0)
                for s in range(STEPS):
                    maxima, others = jobs_at(g, s, last)
                    if s == MAX_TO and not (g == 1 and last):
                        negate_max(b + g, 1 - g)
                    for j in maxima[:2]:
                        do_job(b, j)
                    if s > 0:
                        weigh(b, g, s - 1)
                    for j in others + maxima[2:]:
                        do_job(b, j)
                    if is_l0:
                        for db, nh, j in edge_jobs(g, s, last):
                            edge_mix(b + db, nh, j)
                        if g == 0 and not last:
                            if s in (4, 10):
                                x_stats(b + 1, s // 10)
                                x_norm(b + 1, s // 10)
                    if s == QK_STEP + 1 and not last:
                        split(b + 1, g, 0)
                        split(b + 1, g, 1)
                    if g == 0 and not (first or is_l0):
                        if is_l3 and s - 2 in CLOSE_STEPS:
                            y_stats(b - 1, CLOSE_STEPS.index(s - 2))
                        if is_l3 and s - 3 in CLOSE_STEPS:
                            y_norm(b - 1, CLOSE_STEPS.index(s - 3))
                        if s == 3:
                            recip(b - 1, 3)
                    if (g, s) == (1, 3):
                        recip(b, 1)
                    if s == 13:
                        recip(b, 2 * g)
                weigh(b, g, STEPS - 1)

            def y_stats(b, j):
                dve.wait_ge(y_ready, b * 2 + j + 1)
                layernorm_stats(y[j % len(y)], cln_mv)

            def y_norm(b, j):
                layernorm_apply(xhat if is_l0 else y[j], y[j % len(y)], cln_rstd, cln_done, b * 2 + j)

            for g in range(G):
                dve.memset(ks[g][3 * HD:P, :, :].bitcast(F32), 1.0).then_inc(consts_ready, 1)
            if not is_l1:
                dve.memset(minus_half[:, :], -0.5).then_inc(consts_ready, 1)
                dve.memset(ln_eps[:, :], LN_EPS).then_inc(consts_ready, 1)
            if is_l0:
                dve.memset(edge_bias[:, :], math.log(0.75) - 1.0).then_inc(consts_ready, 1)
            if is_l1:
                dve.memset(bg[:, :], 0.0).then_inc(bg_cleared, 1)
            dve.wait_ge(consts_ready, n_consts)
            if is_l3:
                for i, t in enumerate((wq, wk, wv, wo)):
                    tile = small_slot()
                    dve.wait_ge(w_turned, i + 1)
                    dve.tensor_copy(t[:, :, :].rearrange("p k o -> p (k o)"), tile[:, :]).then_inc(w_copied, 1)
                dve.wait_ge(w_copied, 4)
            dve.wait_ge(weights_loaded, n_weights * DMA)
            for hf in range(2):
                if is_l0:
                    x_stats(0, hf)
                    x_norm(0, hf)
                for k in range(KC):
                    x_to_t(0, hf, k)
            if is_l1:
                take_ca(0, 0)
                take_ca(0, 1)
            for g in range(G):
                split(0, g, 0)
                split(0, g, 1)
                if g == 0:
                    for job in range(8):
                        if is_l0:
                            edge_mix(0, 0, job)
                        edge_to_t(0, 0, job, None)
            for u in range(MAX_UNITS):
                take_max(0, 0, u)
            negate_max(0, 0)
            max_to_rows(0, 0)

            def graph(b, first, last):
                phase(b, 0, first, last)
                phase(b, 1, first, last)
                if is_l0 or last:
                    recip(b, 3)
                    for j in range(2 if not is_l1 else 0):
                        y_stats(b, j)
                        y_norm(b, j)

            graph(0, True, False)
            with dve.Fori(1, last_b) as b:
                graph(b, False, False)
            graph(last_b, False, True)

        @block.gpsimd
        def _(pool):
            def rstd(mv_sem, var_sem, rstd_sem, n):
                pool.wait_ge(mv_sem, n + 1)
                pool.tensor_tensor(ln_var[:, :], ln_mv[:, :, 1], ln_eps[:, :], ALU.add).then_inc(var_sem, 1)
                pool.wait_ge(var_sem, n + 1)
                pool.tensor_tensor(ln_rstd[:, :], ln_var[:, :], minus_half[:, :], ALU.pow).then_inc(rstd_sem, 1)

            def rows(t):
                return t[:, None, :].to_broadcast([P, HC, D])

            def bias_v(b, j):
                pool.wait_ge(v_copied, b * 2 + j + 1)
                part = v_sb[:, j * HC:(j + 1) * HC, :]
                pool.tensor_tensor(part, part, rows(bv_bc), ALU.add).then_inc(v_ready, 1)

            def weigh(b, g, s):
                n = step_no(b, g, s)
                nh, mc = s // NC, s % NC
                pool.wait_ge(et_ready, et_no(b, nh, 7) + 1)
                pool.wait_ge(exp_done, n * 2 + 1)
                pr = probs[:, p_slot(s), 0, :, :]
                pool.tensor_tensor(pr, pr, et[:, mc, None, nh * HALF:(nh + 1) * HALF].to_broadcast([P, 2, HALF]),
                                   ALU.mult).then_inc(probs_ready[0], 1)

            def normalise(b, q):
                pool.wait_ge(recip_in, (b * 4 + q + 1) * DMA)
                part = ot[:, q // 2, (q % 2) * HALF:(q % 2 + 1) * HALF]
                pool.tensor_tensor(part, part, recip_bc[:, :], ALU.mult).then_inc(ot_ready, 1)

            def phase(b, g, first, last):
                for s in range(STEPS):
                    weigh(b, g, s)
                    if is_l0 and g == 0 and not last and s in (4, 10):
                        rstd(xln_mv, xln_var, xln_rstd, (b + 1) * 2 + s // 10)
                    if g == 0 and not (first or is_l0):
                        if s == 5:
                            normalise(b - 1, 3)
                        if s - 1 in CLOSE_STEPS:
                            add_residual(b - 1, CLOSE_STEPS.index(s - 1))
                        if is_l3 and s - 2 in CLOSE_STEPS:
                            rstd(cln_mv, cln_var, cln_rstd, (b - 1) * 2 + CLOSE_STEPS.index(s - 2))
                        if is_l3 and s - 3 in CLOSE_STEPS:
                            scale_y(b - 1, CLOSE_STEPS.index(s - 3))
                        if is_l3 and s - 4 in CLOSE_STEPS:
                            shift_y(b - 1, CLOSE_STEPS.index(s - 4))
                    if (g, s) == (1, 5):
                        normalise(b, 1)
                normalise(b, 2 * g)

            def add_residual(b, j):
                n = b * 2 + j
                x_res = xbuf[:, :, :] if is_l0 else res[:, j * HC:(j + 1) * HC, :]
                pool.wait_ge(res_loaded, (n + 1) * DMA if is_l0 else (b + 1) * DMA)
                if not is_l1:
                    pool.tensor_tensor(x_res, x_res, rows(bo_bc), ALU.add).then_inc(c_biased, 1)
                    pool.wait_ge(c_biased, n + 1)
                pool.wait_ge(c_copied, n * C_TILES + 1)
                yj = y[j % len(y)]
                pool.tensor_tensor(yj[:, :, :], yj[:, :, :], x_res, ALU.add).then_inc(out_ready if is_l1 else y_ready, 1)

            def scale_y(b, j):
                pool.wait_ge(cln_done, b * 2 + j + 1)
                pool.tensor_tensor(y[j][:, :, :], y[j][:, :, :], rows(gamma_bc), ALU.mult).then_inc(out_mid, 1)

            def shift_y(b, j):
                pool.wait_ge(out_mid, b * 2 + j + 1)
                pool.tensor_tensor(y[j][:, :, :], y[j][:, :, :], rows(beta_bc), ALU.add).then_inc(out_ready, 1)

            def close_half(b, j):
                n = b * 2 + j
                add_residual(b, j)
                if is_l1:
                    return
                rstd(cln_mv, cln_var, cln_rstd, n)
                if is_l0:
                    pool.wait_ge(c_copied, (n + 1) * C_TILES)
                    pool.tensor_tensor(xbuf[:, :, :], xbuf[:, :, :], y[0][:, :, :], ALU.add).then_inc(out_mid, 1)
                    pool.wait_ge(out_mid, n + 1)
                    pool.tensor_tensor(xbuf[:, :, :], xbuf[:, :, :], rows(bf2_bc), ALU.add).then_inc(out_ready, 1)
                else:
                    scale_y(b, j)
                    shift_y(b, j)

            for g in range(G):
                pool.memset(qs[g][3 * HD:P, :, :].bitcast(F32), 1.0).then_inc(consts_ready, 1)
            pool.wait_ge(consts_ready, n_consts)
            pool.wait_ge(weights_loaded, n_weights * DMA)
            if is_l0:
                for hf in range(2):
                    rstd(xln_mv, xln_var, xln_rstd, hf)
            bias_v(0, 0)
            bias_v(0, 1)

            def graph(b, first, last):
                phase(b, 0, first, last)
                phase(b, 1, first, last)
                if not last:
                    bias_v(b + 1, 0)
                    bias_v(b + 1, 1)
                if is_l0 or last:
                    normalise(b, 3)
                    close_half(b, 0)
                    close_half(b, 1)

            graph(0, True, False)
            with pool.Fori(1, last_b) as b:
                graph(b, False, False)
            graph(last_b, False, True)


def constants(nc, sems, ident, ones):
    with ExitStack() as ctx:
        cleared, made = nc.alloc_semaphore("ident_cleared"), nc.alloc_semaphore("ident_made")
        sems.extend((cleared, made))
        block = ctx.enter_context(nc.Block())

        @block.gpsimd
        def _(pool):
            pool.memset(ident[:, :], 0.0).then_inc(cleared, 1)
            pool.wait_ge(cleared, 1)
            pool.affine_select(out=ident[:, :], in_=ident[:, :], compare_op=ALU.not_equal, fill=1.0,
                               base=0, pattern=[[-1, P]], channel_multiplier=1).then_inc(made, 1)
            pool.memset(ones[:, :], 1.0).then_inc(made, 1)
            pool.wait_ge(made, 2)


def single_head_layer(nc, sems, x_in, x_out, adj, w, ident):
    NEG_BIG = -1e9
    SLOPE = 0.01
    X_STEPS, F_STEPS, QK_STEP, K_ROW_STEP, K_COPY_STEP = (3, 4), (5, 6), 7, 7, 7
    A_SLOTS = 4

    with ExitStack() as ctx:
        def sb(what, shape, dt=F32):
            return ctx.enter_context(nc.sbuf_tensor(f"L2_{what}", shape, dt))

        def sem(what):
            sems.append(nc.alloc_semaphore(f"L2_{what}"))
            return sems[-1]

        x_rows = [sb(f"x_rows{i}", [P, NC, D]) for i in range(2)]
        feat = [sb(f"feat{i}", [P, NC, D]) for i in range(2)]
        q_col = [sb(f"q_col{i}", [P, NC]) for i in range(2)]
        k_col = [sb(f"k_col{i}", [P, NC]) for i in range(2)]
        k_row = [sb(f"k_row{i}", [P, N]) for i in range(2)]
        xt = sb("x_t", [P, KC, N])
        adj_sb = [sb(f"adj{i}", [P, N]) for i in range(A_SLOTS)]
        logit = [sb(f"logit{i}", [P, N]) for i in range(2)]
        prob = [sb(f"prob{i}", [P, N]) for i in range(2)]
        prob_t = [sb(f"prob_t{i}", [P, NC, P]) for i in range(2)]
        neg_max, total, inv = sb("neg_max", [P, 4]), sb("total", [P, 4]), sb("inv", [P, 4])
        y = [sb(f"y{i}", [P, HC, D]) for i in range(2)]
        wfc, b_bc = sb("wfc", [P, KC, D]), sb("b_bc", [P, D])
        wq_bc, wk_bc, bq, bk = sb("wq_bc", [P, D]), sb("wk_bc", [P, D]), sb("bq", [P, 1]), sb("bk", [P, 1])
        minus_big = sb("minus_big", [P, 1])
        products = sb("products", [P, NC, D])

        turned = [ctx.enter_context(nc.psum_tensor(f"L2_turned{i}", [P, N], F32)) for i in range(2)]
        small = [ctx.enter_context(nc.psum_tensor(f"L2_small{i}", [P, HALF], F32)) for i in range(2)]
        out_ps = [ctx.enter_context(nc.psum_tensor(f"L2_out{i}", [P, HALF], F32)) for i in range(2)]

        weights_loaded, minus_big_ready = sem("weights_loaded"), sem("minus_big_ready")
        x_loaded = [sem(f"x_loaded{i}") for i in range(2)]
        adj_loaded = [sem(f"adj_loaded{i}") for i in range(A_SLOTS)]
        x_turned, xt_ready = sem("x_turned"), sem("xt_ready")
        f_made, f_copied, f_ready = sem("f_made"), sem("f_copied"), sem("f_ready")
        qk_ready, k_row_made, k_row_ready = sem("qk_ready"), sem("k_row_made"), sem("k_row_ready")
        mask_ready, masked, leaked, max_ready = sem("mask_ready"), sem("masked"), sem("leaked"), sem("max_ready")
        exp_done, p_turned, pt_ready = sem("exp_done"), sem("p_turned"), sem("pt_ready")
        attended, inv_ready, y_ready = sem("attended"), sem("inv_ready"), sem("y_ready")
        stored = [sem(f"stored{i}") for i in range(2)]
        n_weights = 6

        block = ctx.enter_context(nc.Block())

        def run(eng, graph):
            graph(0, 0, True, False)
            graph(1, 1, False, False)
            with eng.Fori(2, BATCH - 2, 2) as b:
                graph(b, 0, False, False)
                graph(b + 1, 1, False, False)
            graph(BATCH - 2, 0, False, False)
            graph(BATCH - 1, 1, False, True)

        @block.sync
        def _(sp):
            def load_adj(b, c, skip_wait=False):
                if not skip_wait:
                    sp.wait_ge(masked, b * NC + c - A_SLOTS + 1)
                sp.dma_start(adj_sb[c % A_SLOTS][:, :], adj[bass.ds(b, 1), c * P:(c + 1) * P, :].rearrange("o p m -> (o p) m")
                             ).then_inc(adj_loaded[c % A_SLOTS], DMA)

            def load_x(b, par):
                sp.dma_start(x_rows[par][:, :, :], x_in[bass.ds(b, 1), :, :].rearrange("o (c p) d -> p (o c) d", p=P)
                             ).then_inc(x_loaded[par], DMA)

            load_x(0, 0)
            for dst, src in ((wfc[:, :, :], w["W_fc"].rearrange("(k p) o -> p k o", p=P)),
                             (b_bc[:, :], w["b_fc"][None, :].to_broadcast([P, D])),
                             (wq_bc[:, :], w["w_q"].rearrange("d o -> o d").to_broadcast([P, D])),
                             (wk_bc[:, :], w["w_k"].rearrange("d o -> o d").to_broadcast([P, D])),
                             (bq[:, :], w["b_q"][None, :].to_broadcast([P, 1])),
                             (bk[:, :], w["b_k"][None, :].to_broadcast([P, 1]))):
                sp.dma_start(dst, src, allow_slow_non_contiguous=True).then_inc(weights_loaded, DMA)
            for c in range(A_SLOTS - 1):
                load_adj(0, c, True)

            def graph(b, par, first, last):
                for c in range(NC):
                    ahead = c + A_SLOTS - 1
                    if ahead < NC:
                        load_adj(b, ahead, first and ahead < A_SLOTS)
                    elif not last:
                        load_adj(b + 1, ahead - NC)
                    if c == 1 and not last:
                        if not first:
                            wait_from(sp, y_ready, (b + 1) * NC - NC)
                        load_x(b + 1, 1 - par)
                    if c == 2 and not first:
                        store(b - 1, 1)
                    if c == 6:
                        store(b, 0)
                if last:
                    store(b, 1)

            def store(b, hf):
                sp.wait_ge(y_ready, b * NC + hf * HC + HC)
                sp.dma_start(x_out[bass.ds(b, 1), hf * HALF:(hf + 1) * HALF, :].rearrange("o (c p) d -> p (o c) d", p=P),
                             y[hf][:, :, :]).then_inc(stored[hf], DMA)

            run(sp, graph)
            for hf in range(2):
                sp.wait_ge(stored[hf], BATCH * DMA)

        @block.tensor
        def _(pe):
            hist = [None, None]
            n_small = 0

            def small_slot(done_sem, done_value):
                nonlocal n_small
                if hist[-2] is not None:
                    pe.wait_ge(*hist[-2])
                hist.append((done_sem, done_value))
                n_small += 1
                return small[(n_small - 1) % 2]

            def turn_x(b, par, hf):
                pe.wait_ge(x_loaded[par], (b - par) * (DMA // 2) + DMA)
                for k in range(KC):
                    tile = small_slot(xt_ready, b * 4 + hf * 2 + k + 1)
                    for c in range(HC):
                        mm = pe.transpose(tile[:, c * P:(c + 1) * P], x_rows[par][:, hf * HC + c, k * P:(k + 1) * P], ident[:, :])
                    mm.then_inc(x_turned, 1)

            def project(b, hf):
                pe.wait_ge(xt_ready, (b + 1) * 4)
                for j in range(2):
                    tile = small_slot(f_copied, b * 4 + hf * 2 + j + 1)
                    for i in range(2):
                        c = hf * HC + j * 2 + i
                        for k in range(KC):
                            mm = pe.matmul(tile[:, i * D:(i + 1) * D], xt[:, k, c * P:(c + 1) * P], wfc[:, k, :],
                                           start=k == 0, stop=k == KC - 1)
                    mm.then_inc(f_made, 1)

            def spread_k(b, par):
                pe.wait_ge(qk_ready, (b + 1) * 2)
                for hf in range(2):
                    tile = small_slot(k_row_ready, b * 2 + hf + 1)
                    for i in range(HC):
                        c = hf * HC + i
                        mm = pe.matmul(tile[:, i * P:(i + 1) * P], k_col[par][:, c:c + 1].to_broadcast([P, P]), ident[:, :],
                                       start=True, stop=True)
                    mm.then_inc(k_row_made, 1)

            def turn_p(b, c):
                n = b * NC + c
                pe.wait_ge(exp_done, n + 1)
                wait_from(pe, pt_ready, n - 1)
                for m in range(NC):
                    mm = pe.transpose(turned[c % 2][:, m * P:(m + 1) * P], prob[c % 2][:, m * P:(m + 1) * P], ident[:, :])
                mm.then_inc(p_turned, 1)

            def attend(b, par, c):
                n = b * NC + c
                pe.wait_ge(pt_ready, n + 1)
                wait_from(pe, y_ready, n - 1)
                for m in range(NC):
                    mm = pe.matmul(out_ps[c % 2][:, 0:D], prob_t[c % 2][:, m, :], feat[par][:, m, :],
                                   start=m == 0, stop=m == NC - 1)
                mm.then_inc(attended, 1)

            pe.wait_ge(weights_loaded, n_weights * DMA)
            for hf in range(2):
                turn_x(0, 0, hf)
            for hf in range(2):
                project(0, hf)
            spread_k(0, 0)

            def graph(b, par, first, last):
                hist[:] = [(k_row_ready, b * 2 + 1), (k_row_ready, b * 2 + 2)]
                for c in range(NC):
                    turn_p(b, c)
                    if c:
                        attend(b, par, c - 1)
                    elif not first:
                        attend(b - 1, 1 - par, NC - 1)
                    if not last:
                        if c in X_STEPS:
                            turn_x(b + 1, 1 - par, c - X_STEPS[0])
                        if c in F_STEPS:
                            project(b + 1, c - F_STEPS[0])
                        if c == K_ROW_STEP:
                            spread_k(b + 1, 1 - par)
                if last:
                    attend(b, par, NC - 1)

            run(pe, graph)

        @block.scalar
        def _(act):
            n_small = 0

            def small_slot():
                nonlocal n_small
                n_small += 1
                return small[(n_small - 1) % 2]

            def copy_xt(b, hf):
                for k in range(KC):
                    tile = small_slot()
                    act.wait_ge(x_turned, b * 4 + hf * 2 + k + 1)
                    act.activation(xt[:, k, hf * HALF:(hf + 1) * HALF], tile[:, :], ACT.Copy).then_inc(xt_ready, 1)

            def copy_f(b, par, hf):
                for j in range(2):
                    tile = small_slot()
                    c = hf * HC + j * 2
                    act.wait_ge(f_made, b * 4 + hf * 2 + j + 1)
                    act.activation(feat[par][:, c:c + 2, :].rearrange("p c d -> p (c d)"), tile[:, :], ACT.Copy).then_inc(f_copied, 1)

            def copy_k(b, par):
                for hf in range(2):
                    tile = small_slot()
                    act.wait_ge(k_row_made, b * 2 + hf + 1)
                    act.activation(k_row[par][:, hf * HALF:(hf + 1) * HALF], tile[:, :], ACT.Copy).then_inc(k_row_ready, 1)

            def mask(b, c):
                act.wait_ge(adj_loaded[c % A_SLOTS], (b * 2 + c // A_SLOTS + 1) * DMA)
                t = adj_sb[c % A_SLOTS]
                act.activation(t[:, :], t[:, :], ACT.Identity, bias=minus_big[:, :], scale=-NEG_BIG).then_inc(mask_ready, 1)

            def exp(b, c):
                n = b * NC + c
                act.wait_ge(max_ready, n + 1)
                wait_from(act, p_turned, n - 1)
                wait_from(act, inv_ready, n - 3)
                act.activation(prob[c % 2][:, :], logit[c % 2][:, :], ACT.Exp, bias=neg_max[:, c % 4:c % 4 + 1],
                               accum_out=total[:, c % 4:c % 4 + 1]).then_inc(exp_done, 1)

            def copy_pt(b, c):
                n = b * NC + c
                act.wait_ge(p_turned, n + 1)
                wait_from(act, attended, n - 1)
                act.activation(prob_t[c % 2][:, :, :].rearrange("p m n -> p (m n)"), turned[c % 2][:, :], ACT.Copy
                               ).then_inc(pt_ready, 1)

            act.wait_ge(minus_big_ready, 1)
            mask(0, 0)
            mask(0, 1)
            for hf in range(2):
                copy_xt(0, hf)
            for hf in range(2):
                copy_f(0, 0, hf)
            copy_k(0, 0)

            def graph(b, par, first, last):
                for c in range(NC):
                    exp(b, c)
                    if c + 2 < NC:
                        mask(b, c + 2)
                    elif not last:
                        mask(b + 1, c + 2 - NC)
                    copy_pt(b, c)
                    if not last:
                        if c in X_STEPS:
                            copy_xt(b + 1, c - X_STEPS[0])
                        if c in F_STEPS:
                            copy_f(b + 1, 1 - par, c - F_STEPS[0])
                        if c == K_COPY_STEP:
                            copy_k(b + 1, 1 - par)

            run(act, graph)

        @block.vector
        def _(dve):
            def numbers(b, par):
                dve.wait_ge(f_ready, (b + 1) * 2)
                for i, (col, wt, bias) in enumerate(((q_col, wq_bc, bq), (k_col, wk_bc, bk))):
                    wait_from(dve, qk_ready, b * 2 + i)
                    for c in range(NC):
                        op = dve.tensor_tensor_reduce(products[:, c, :], feat[par][:, c, :], wt[:, :], 1.0, bias[:, 0:1], ALU.mult, ALU.add,
                                                      col[par][:, c:c + 1])
                    op.then_inc(qk_ready, 1)

            def logits(b, par, c):
                n = b * NC + c
                z = logit[c % 2]
                if c == 0:
                    dve.wait_ge(k_row_ready, (b + 1) * 2)
                    dve.wait_ge(qk_ready, (b + 1) * 2)
                dve.wait_ge(mask_ready, n + 1)
                wait_from(dve, exp_done, n - 1)
                dve.scalar_tensor_tensor(out=z[:, :], in0=k_row[par][:, :], scalar=q_col[par][:, c:c + 1],
                                         in1=adj_sb[c % A_SLOTS][:, :], op0=ALU.add, op1=ALU.add).then_inc(masked, 1)
                dve.wait_ge(masked, n + 1)
                dve.scalar_tensor_tensor(out=z[:, :], in0=z[:, :], scalar=SLOPE, in1=z[:, :], op0=ALU.mult, op1=ALU.max
                                         ).then_inc(leaked, 1)
                dve.wait_ge(leaked, n + 1)
                dve.tensor_reduce(neg_max[:, c % 4:c % 4 + 1], z[:, :], AX.X, ALU.max, negate=True).then_inc(max_ready, 1)

            def finish(b, par, c):
                n = b * NC + c
                dve.wait_ge(exp_done, n + 1)
                dve.reciprocal(inv[:, c % 4:c % 4 + 1], total[:, c % 4:c % 4 + 1]).then_inc(inv_ready, 1)
                dve.wait_ge(inv_ready, n + 1)
                dve.wait_ge(attended, n + 1)
                if c % HC == 0:
                    wait_from(dve, stored[c // HC], b * DMA)
                dve.scalar_tensor_tensor(out=y[c // HC][:, c % HC, :], in0=out_ps[c % 2][:, 0:D], scalar=inv[:, c % 4:c % 4 + 1],
                                         in1=x_rows[par][:, c, :], op0=ALU.mult, op1=ALU.add).then_inc(y_ready, 1)

            dve.memset(minus_big[:, :], NEG_BIG).then_inc(minus_big_ready, 1)
            dve.wait_ge(weights_loaded, n_weights * DMA)
            numbers(0, 0)

            def graph(b, par, first, last):
                for c in range(NC):
                    logits(b, par, c)
                    if c >= 2:
                        finish(b, par, c - 2)
                    elif not first:
                        finish(b - 1, 1 - par, NC - 2 + c)
                    if c == QK_STEP and not last:
                        numbers(b + 1, 1 - par)
                if last:
                    finish(b, par, NC - 2)
                    finish(b, par, NC - 1)

            run(dve, graph)

        @block.gpsimd
        def _(pool):
            def bias_f(b, par):
                for hf in range(2):
                    pool.wait_ge(f_copied, b * 4 + hf * 2 + 2)
                    part = feat[par][:, hf * HC:(hf + 1) * HC, :]
                    pool.tensor_tensor(part, part, b_bc[:, None, :].to_broadcast([P, HC, D]), ALU.add).then_inc(f_ready, 1)

            pool.wait_ge(weights_loaded, n_weights * DMA)
            bias_f(0, 0)

            def graph(b, par, first, last):
                if not last:
                    bias_f(b + 1, 1 - par)

            run(pool, graph)


def clear(nc, sems):
    nc.clear_and_free_semaphores(sems)
    sems.clear()
    with nc.Block():
        pass


def program(nc, x, adj, weights, out):
    between = [nc.dram_tensor(f"x_after_{n}", [BATCH, N, D], F32).ap() for n in ("L0", "L1", "L2")]
    sums_d = nc.dram_tensor("sums_by_row", [4, GH, HALF], F32).ap()
    recips_d = nc.dram_tensor("recips_by_row", [4, GH, HALF], F32).ap()
    with ExitStack() as ctx:
        ident = ctx.enter_context(nc.sbuf_tensor("ident", [P, P], F32))
        ones = ctx.enter_context(nc.sbuf_tensor("ones", [P, HD], F32))
        sems = []
        constants(nc, sems, ident, ones)
        attention_layer(nc, sems, "L0", x, between[0], adj, weights["L0"], ident, ones, sums_d, recips_d)
        clear(nc, sems)
        attention_layer(nc, sems, "L1", between[0], between[1], adj, weights["L1"], ident, ones, sums_d, recips_d)
        clear(nc, sems)
        single_head_layer(nc, sems, between[1], between[2], adj, weights["L2"], ident)
        clear(nc, sems)
        attention_layer(nc, sems, "L3", between[2], out, adj, weights["L3"], ident, ones, sums_d, recips_d)


_SAME = {n: n for n in ("Wq", "bq", "Wk", "bk", "Wv", "bv", "Wo", "bo")}
_WEIGHTS = {
    "L0": {**_SAME, **{n: n for n in ("g1", "b1", "g2", "b2", "Wf1", "bf1", "Wf2", "bf2")}},
    "L1": {"Wq": "W_q", "bq": "b_q", "Wk": "W_k", "bk": "b_k", "Wv": "W_v", "bv": "b_v", "w_g": "w_g", "b_g": "b_g"},
    "L2": {n: n for n in ("W_fc", "b_fc", "w_q", "b_q", "w_k", "b_k")},
    "L3": {**_SAME, "gamma": "gamma", "beta": "beta"},
}


def kernel(**inputs):
    import numpy as _np
    import concourse.bacc as _bacc
    from concourse import mybir as _mybir
    from concourse.bass_utils import run_bass_kernel_spmd as _run

    nc = _bacc.Bacc("TRN2", target_bir_lowering=False, num_devices=1)
    arrays = {}

    def declare(name):
        a = _np.ascontiguousarray(inputs[name])
        a = a.reshape(1, 1) if a.size == 1 and a.ndim == 0 else a
        arrays[f"in_{name}"] = a
        return nc.dram_tensor(f"in_{name}", list(a.shape), _mybir.dt.from_np(a.dtype), kind="ExternalInput").ap()

    x, adj = declare("x"), declare("adj")
    weights = {layer: {own: declare(f"{layer}_gnn_{n}") for own, n in names.items()} for layer, names in _WEIGHTS.items()}
    out = nc.dram_tensor("out", [BATCH, N, D], F32, kind="ExternalOutput").ap()
    program(nc, x, adj, weights, out)
    r = _run(nc, [arrays], core_ids=[0])
    return r.results[0]["out"]
```

```python
import math
from contextlib import ExitStack

import concourse.bass as bass
from concourse import mybir

F32 = mybir.dt.float32
F32R = mybir.dt.float32r
ALU = mybir.AluOpType
ACT = mybir.ActivationFunctionType
AX = mybir.AxisListType

P = 128
BATCH, N, D = 8, 1024, 256
HEADS = 8
HD = D // HEADS
GH = P // HD
G = HEADS // GH
KC = D // P
NC = N // P
HALF = 512
HC = HALF // P
FF = 4 * D
FC = FF // P
LN_EPS = 1e-5
SCALE = float(HD) ** -0.5

STEPS = 2 * NC
MAX_FROM, MAX_TO = 0, 15
MAX_UNITS = GH * NC * 2
POOL_COLS = 128
LAG = 2
P_SLOTS = 3
DMA = 16


def et_job(job):
    return job // 2, job % 2


X_TURNS = {6: ((0, 0), (0, 1)), 11: ((1, 0), (1, 1))}
QK_STEP = 12
CLOSE_STEPS = (7, 9)
WEIGHT_LOADS = {"L0": (8, 8), "L1": (9, 0), "L3": (3, 3)}


def prologue_jobs():
    jobs = []
    for v in range(MAX_UNITS // 2):
        if v in (12, 14, 17, 19, 22, 24, 27, 29):
            jobs.append(("et", sum(what == "et" for what, _ in jobs)))
        jobs.append(("max", v))
    return jobs


def wait_from(eng, sem, count):
    if not isinstance(count, int) or count > 0:
        eng.wait_ge(sem, count)


def p_slot(s):
    return s % P_SLOTS


def edge_jobs(g, s, last):
    if g == 0:
        return [(0, 1, s + 1)] if s < 7 else []
    return [(1, 0, s - 7)] if 7 <= s < 15 and not last else []


def attention_layer(nc, sems, name, x_in, x_out, adj, w, ident, ones, sums_d, recips_d):
    is_l0, is_l1, is_l3 = name == "L0", name == "L1", name == "L3"
    n_bias = 4 if is_l1 else 0
    k_max = 3 * HD + n_bias
    k_all = k_max + 2
    head_dmas = 2 * 3
    last_b = BATCH - 1

    with ExitStack() as ctx:
        def sb(what, shape, dt=F32):
            return ctx.enter_context(nc.sbuf_tensor(f"{name}_{what}", shape, dt))

        def ps(what, shape):
            return ctx.enter_context(nc.psum_tensor(f"{name}_{what}", shape, F32))

        def sem(what):
            sems.append(nc.alloc_semaphore(f"{name}_{what}"))
            return sems[-1]

        qs = [sb(f"q_stack{g}", [P, GH, N], F32R) for g in range(G)]
        ks = [sb(f"k_stack{g}", [P, GH, N], F32R) for g in range(G)]
        et = sb("edge_t", [P, NC, N])
        v_sb = sb("v", [P, NC, D])
        xt = sb("x_t", [P, KC, N])
        xbuf = sb("x_rows", [P, HC, D])
        adj_sb = [sb(f"adj{i}", [P, HALF]) for i in range(2)]
        split_hi = [sb(f"split_hi{i}", [P, N], F32R) for i in range(2)]
        split_lo = [sb(f"split_lo{i}", [P, N], F32R) for i in range(2)]
        probs = sb("probs", [P, P_SLOTS, 2, 2, HALF])
        ot = sb("attended_t", [P, G, N])
        y = [sb(f"y{i}", [P, HC, D]) for i in range(1 if is_l0 else 2)]
        sums = sb("sums", [P, HALF])
        sums_col = sb("sums_col", [P, 16])
        recip_col = sb("recip_col", [P, 16])
        recip_bc = sb("recip_bc", [P, HALF])
        max_part = sb("max_part", [P, GH * NC, 2])
        neg_max = sb("neg_max", [P, GH * NC])
        max_hi = sb("max_hi", [GH * NC, P], F32R)
        max_lo = sb("max_lo", [GH * NC, P], F32R)
        wq, wk, wv = (sb(f"w{c}", [P, KC, D]) for c in "qkv")
        bq, bk = sb("bq", [P, G]), sb("bk", [P, G])
        bv_bc = sb("bv_bc", [P, D])
        if not is_l0:
            res = sb("residual", [P, NC, D])
        if is_l1:
            wg = sb("wg", [P, KC, 2])
            bg = sb("bg", [2, 1])
            adj_floor = sb("adj_floor", [P, 1])
            ca_hi, ca_lo = sb("ca_hi", [2, N], F32R), sb("ca_lo", [2, N], F32R)
        else:
            wo = sb("wo", [P, KC, D])
            bo_bc = sb("bo_bc", [P, D])
            ln_raw, ln_mv = sb("ln_raw", [P, HC, 6]), sb("ln_mv", [P, HC, 2])
            ln_var, ln_rstd = sb("ln_var", [P, HC]), sb("ln_rstd", [P, HC])
            minus_half, ln_eps = sb("minus_half", [P, HC]), sb("ln_eps", [P, HC])
        if is_l0:
            g1, b1, g2, b2 = (sb(c, [P, KC]) for c in ("g1", "b1", "g2", "b2"))
            wf1, wf2 = sb("wf1", [P, KC, FF]), sb("wf2", [P, FC, D])
            bf1, bf2_bc = sb("bf1", [P, FC]), sb("bf2_bc", [P, D])
            edge_exp, edge_bias = sb("edge_exp", [P, HALF]), sb("edge_bias", [P, 1])
            flat = probs[:, :, :, :, :].rearrange("p s t h n -> p (s t h n)")
            hid = flat[:, 0:FC * HALF].rearrange("p (f n) -> p f n", n=HALF)
            xhat = [flat[:, (FC + i * KC) * HALF:(FC + (i + 1) * KC) * HALF].rearrange("p (c d) -> p c d", d=D)
                    for i in range(2)]
            y.insert(0, xbuf)
        if is_l3:
            gamma_bc, beta_bc = sb("gamma_bc", [P, D]), sb("beta_bc", [P, D])

        big = [ps(f"big{i}", [P, N]) for i in range(2)]
        small = [ps(f"small{i}", [P, HALF]) for i in range(2)]
        pv = ps("pv", [P, HALF])
        rowsum = ps("rowsum", [P, HALF])

        late_loaded = sem("late_loaded")
        weights_loaded, w_raw_loaded, w_turned = sem("weights_loaded"), sem("w_raw_loaded"), sem("w_turned")
        w_copied, w_scaled, bg_cleared = sem("w_copied"), sem("w_scaled"), sem("bg_cleared")
        consts_ready = sem("consts_ready")
        x_loaded, stored = sem("x_loaded"), sem("stored")
        res_loaded = [sem(f"res_loaded{j}") for j in range(2 if is_l0 else 1)]
        adj_loaded = [sem(f"adj_loaded{i}") for i in range(2)]
        adj_exp, adj_ready = sem("adj_exp"), sem("adj_ready")
        et_turned, et_ready = sem("et_turned"), sem("et_ready")
        xln_mv, xln_var, xln_rstd, xln_done = (sem(f"xln_{c}") for c in ("mv", "var", "rstd", "done"))
        cln_mv, cln_var, cln_rstd, cln_done = (sem(f"cln_{c}") for c in ("mv", "var", "rstd", "done"))
        x_turned, xt_ready = sem("x_turned"), sem("xt_ready")
        ca_made, ca_copied, ca_hi_ready, ca_ready = sem("ca_made"), sem("ca_copied"), sem("ca_hi_ready"), sem("ca_ready")
        qk_made, split_copied, split_ready = sem("qk_made"), sem("split_copied"), sem("split_ready")
        stack_loaded = [[sem(f"stack_loaded{g}_{h}") for h in range(GH)] for g in range(G)]
        bias_loaded = [sem(f"bias_loaded{g}") for g in range(G)]
        v_made, v_copied, v_ready = sem("v_made"), sem("v_copied"), sem("v_ready")
        max_scored, max_taken = sem("max_scored"), sem("max_taken")
        neg_max_ready, max_turned, max_hi_ready, max_rows_ready = (
            sem(c) for c in ("neg_max_ready", "max_turned", "max_hi_ready", "max_rows_ready"))
        max_loaded = [sem(f"max_loaded{g}") for g in range(G)]
        scored, exp_done, pv_done, pv_copied = sem("scored"), sem("exp_done"), sem("pv_done"), sem("pv_copied")
        probs_ready = [sem(f"probs_ready{t}") for t in range(3)]
        sums_out, sums_in, recip_ready, recip_out, recip_in = (
            sem(c) for c in ("sums_out", "sums_in", "recip_ready", "recip_out", "recip_in"))
        ot_ready = sem("ot_ready")
        c_made, c_copied, c_biased, y_ready, h2_ready, gelu_done, out_ready, out_mid = (
            sem(c) for c in ("c_made", "c_copied", "c_biased", "y_ready", "h2_ready", "gelu_done", "out_ready", "out_mid"))

        def step_no(b, g, s):
            return b * (G * STEPS) + g * STEPS + s

        def unit_no(b, g, u):
            return b * (G * MAX_UNITS) + g * MAX_UNITS + u

        def et_no(b, nh, job):
            return b * 16 + nh * 8 + job

        CLOSE_L0 = ([("wo", 0)] + [("max", 14)] + [("wo", 1)] + [("max", 2)] + [("ln", 0)] + [("f1", 0)] * 4
                    + [("ln", 1)] + [("f2", 0)] + [("f1", 1)] * 4 + [("f2", 1)])
        assert sum(n if what == "max" else {"f1": 4, "f2": 2 * HC}.get(what, 0) for what, n in CLOSE_L0) == MAX_UNITS
        CLOSE_TILES = [item for item in CLOSE_L0 if item[0] != "max"]
        C_TILES = len(CLOSE_TILES) if is_l0 else 2

        def wait_stacks(eng, g, count):
            for h in range(GH):
                wait_from(eng, stack_loaded[g][h], count * (head_dmas * DMA))
            if is_l1:
                wait_from(eng, bias_loaded[g], count * (n_bias * DMA))

        def jobs_at(g, s, first, last):
            maxima, others = [], []
            if g == 0:
                if s < 8:
                    others.append(("et", 0, 1, s))
                nb, ng = 0, 1
            else:
                if last:
                    return maxima, others
                nb, ng = 1, 0
            here = not (is_l0 and g == 0) or first
            span = MAX_TO - MAX_FROM
            if MAX_FROM <= s < MAX_TO and here:
                maxima = [("max", nb, ng, u) for u in range(MAX_UNITS * (s - MAX_FROM) // span,
                                                            MAX_UNITS * (s - MAX_FROM + 1) // span)]
            if g == 1 and s >= 8:
                others.append(("et", 1, 0, s - 8))
            if g == 0 and not last:
                others += [("xt", 1, hf, k) for hf, k in X_TURNS.get(s, ())]
            if is_l1 and (g, s) == (0, QK_STEP) and not last:
                others += [("ca", 1, 0), ("ca", 1, 1)]
            if s == STEPS - 1 and here:
                others.append(("max_rows", nb, ng))
            return maxima, others

        n_weights, n_late = WEIGHT_LOADS[name]
        n_consts = 4 + (1 if is_l1 else 2) + is_l0
        block = ctx.enter_context(nc.Block())

        def rows_of(t, b, hf):
            return t[bass.ds(b, 1), hf * HALF:(hf + 1) * HALF, :].rearrange("o (c p) d -> p (o c) d", p=P)

        @block.sync
        def _(sp):
            n_loads = {weights_loaded: 0, late_loaded: 0}

            def load(dst, src, signal=weights_loaded):
                sp.dma_start(dst, src, allow_slow_non_contiguous=True).then_inc(signal, DMA)
                n_loads[signal] += 1

            def load_x(b, hf):
                if is_l0 and hf == 0 and not (isinstance(b, int) and b < 2):
                    sp.wait_ge(stored, (b - 1) * (2 * DMA))
                else:
                    wait_from(sp, xt_ready, b * 4 + 2 * hf)
                sp.dma_start(xbuf[:, :, :], rows_of(x_in, b, hf)).then_inc(x_loaded, DMA)

            def load_adj(b, nh, job):
                c, mh = et_job(job)
                wait_from(sp, et_ready, et_no(b, nh, job) - 1)
                r0 = (nh * HC + c) * P
                sp.dma_start(adj_sb[job % 2][:, :],
                             adj[bass.ds(b, 1), r0:r0 + P, mh * HALF:(mh + 1) * HALF].rearrange("o p m -> (o p) m")
                             ).then_inc(adj_loaded[job % 2], DMA)

            def stack_biases(b, g):
                if is_l1:
                    for i, part in enumerate((ca_hi, ca_lo)):
                        r = 3 * HD + i
                        sp.dma_start(ks[g][r:r + 1, :, :].bitcast(F32),
                                     part[0:1, None, :].bitcast(F32).to_broadcast([1, GH, N])).then_inc(bias_loaded[g], DMA)
                        sp.dma_start(qs[g][r + 2:r + 3, :, :].bitcast(F32),
                                     part[1:2, None, :].bitcast(F32).to_broadcast([1, GH, N])).then_inc(bias_loaded[g], DMA)

            def stack(b, g, h):
                if h == 0:
                    splits, ca_halves, scores_before = (b * G + g) * 2 + 2, (b + 1) * 2, step_no(b - 1, g, STEPS) * 2
                    sp.wait_ge(split_ready, splits)
                    if is_l1:
                        sp.wait_ge(ca_ready, ca_halves)
                    wait_from(sp, scored, scores_before)
                for which, dst in ((0, qs[g]), (1, ks[g])):
                    hi, lo = split_hi[which], split_lo[which]
                    for i, part in enumerate((hi, hi, lo) if which == 0 else (hi, lo, hi)):
                        sp.dma_start(dst[i * HD:(i + 1) * HD, h, :].bitcast(F32),
                                     part[h * HD:(h + 1) * HD, :].bitcast(F32)).then_inc(stack_loaded[g][h], DMA)

            def max_rows(b, g):
                sp.wait_ge(max_rows_ready, b * G + g + 1)
                for i, part in enumerate((max_hi, max_lo)):
                    sp.dma_start(qs[g][k_max + i:k_max + i + 1, :, :].rearrange("p h (c n) -> p (h c) n", n=P).bitcast(F32),
                                 part[:, :].bitcast(F32)).then_inc(max_loaded[g], DMA)

            def norm_dma(b, q, part):
                n = b * 4 + q
                if part == 0:
                    pv_copies, stores_before = 2 * n + 2, b * (2 * DMA)
                    if q == 2 and not is_l0:
                        wait_from(sp, stored, stores_before)
                    sp.wait_ge(pv_copied, pv_copies)
                    sp.dma_start(sums_d[q, :, :], sums[0:P:HD, :]).then_inc(sums_out, DMA)
                elif part == 1:
                    sp.wait_ge(sums_out, (n + 1) * DMA)
                    sp.dma_start(sums_col[:, :], sums_d[q, :, :].rearrange("h (j f) -> (h j) f", f=16)).then_inc(sums_in, DMA)
                elif part == 2:
                    sp.wait_ge(recip_ready, n + 1)
                    sp.dma_start(recips_d[q, :, :].rearrange("h (j f) -> (h j) f", f=16), recip_col[:, :]).then_inc(recip_out, DMA)
                else:
                    sp.wait_ge(recip_out, (n + 1) * DMA)
                    wait_from(sp, ot_ready, n)
                    sp.dma_start(recip_bc[:, :], recips_d[q, :, None, :].to_broadcast([GH, HD, HALF])).then_inc(recip_in, DMA)

            def load_residual(b):
                sp.dma_start(res[:, :, :], x_in[bass.ds(b, 1), :, :].rearrange("o (c p) d -> p (o c) d", p=P)
                             ).then_inc(res_loaded[0], DMA)

            def store(b, j):
                sp.wait_ge(out_ready, b * 2 + j + 1)
                sp.dma_start(rows_of(x_out, b, j), y[j][:, :, :]).then_inc(stored, DMA)

            def load_residual_l0(b, last):
                stores_before = b * (2 * DMA)
                sp.wait_ge(xt_ready, BATCH * 4 if last else (b + 2) * 4)
                sp.dma_start(xbuf[:, :, :], rows_of(x_in, b, 0)).then_inc(res_loaded[0], DMA)
                wait_from(sp, stored, stores_before)
                sp.dma_start(y[1][:, :, :], rows_of(x_in, b, 1)).then_inc(res_loaded[1], DMA)

            load_x(0, 0)
            for t, n in ((wq, "Wq"), (wk, "Wk"), (wv, "Wv")) if not is_l3 else ():
                load(t[:, :, :], w[n].rearrange("(k p) o -> p k o", p=P))
            for t, n in ((bq, "bq"), (bk, "bk")):
                load(t[:, :], w[n].rearrange("(g p) -> p g", p=P))
            load(bv_bc[:, :], w["bv"][None, :].to_broadcast([P, D]))
            if is_l1:
                load(wg[:, :, 0:1], w["w_g"][D:2 * D].rearrange("(k p o) -> p k o", p=P, o=1))
                load(wg[:, :, 1:2], w["w_g"][0:D].rearrange("(k p o) -> p k o", p=P, o=1))
                sp.wait_ge(bg_cleared, 1)
                load(bg[0:1, :], w["b_g"])
            if is_l0:
                for t, n in ((g1, "g1"), (b1, "b1")):
                    load(t[:, :], w[n].rearrange("(k p) -> p k", p=P))
            if is_l3:
                for i, n in enumerate(("Wq", "Wk", "Wv", "Wo")):
                    sp.dma_start(et[:, i, 0:2 * D].rearrange("p (k o) -> p k o", o=D),
                                 w[n].rearrange("(k p) i -> p k i", p=P)).then_inc(w_raw_loaded, DMA)
            load_adj(0, 0, 0)
            load_adj(0, 0, 1)
            load_x(0, 1)
            if not is_l1:
                load(bo_bc[:, :], w["bo"][None, :].to_broadcast([P, D]), late_loaded)
            if is_l0:
                load(wo[:, :, :], w["Wo"].rearrange("(k p) o -> p k o", p=P), late_loaded)
                for t, n in ((g2, "g2"), (b2, "b2")):
                    load(t[:, :], w[n].rearrange("(k p) -> p k", p=P), late_loaded)
                load(wf1[:, :, :], w["Wf1"].rearrange("(k p) o -> p k o", p=P), late_loaded)
                load(wf2[:, :, :], w["Wf2"].rearrange("(k p) o -> p k o", p=P), late_loaded)
                load(bf1[:, :], w["bf1"].rearrange("(k p) -> p k", p=P), late_loaded)
                load(bf2_bc[:, :], w["bf2"][None, :].to_broadcast([P, D]), late_loaded)
            if is_l3:
                load(gamma_bc[:, :], w["gamma"][None, :].to_broadcast([P, D]), late_loaded)
                load(beta_bc[:, :], w["beta"][None, :].to_broadcast([P, D]), late_loaded)
            assert (n_loads[weights_loaded], n_loads[late_loaded]) == (n_weights, n_late)
            sp.wait_ge(consts_ready, n_consts)
            stack(0, 0, 0)
            stack_biases(0, 0)
            for h in range(1, GH):
                stack(0, 0, h)
            for job in range(2, 8):
                load_adj(0, 0, job)
            load_adj(0, 1, 0)
            load_adj(0, 1, 1)

            def graph(b, first, last):
                here = first or not is_l0
                if here:
                    stack(b, 1, 0)
                    max_rows(b, 0)
                    stack_biases(b, 1)
                    stack(b, 1, 1)
                if not (first or is_l0):
                    norm_dma(b - 1, 3, 0)
                load_adj(b, 1, 2)
                if here:
                    stack(b, 1, 2)
                if not (first or is_l0):
                    norm_dma(b - 1, 3, 1)
                    load_residual(b - 1)
                load_adj(b, 1, 3)
                if here:
                    stack(b, 1, 3)
                if not (first or is_l0):
                    norm_dma(b - 1, 3, 2)
                if not last:
                    load_x(b + 1, 0)
                load_adj(b, 1, 4)
                if not (first or is_l0):
                    norm_dma(b - 1, 3, 3)
                for s in range(5, STEPS):
                    if s < 8:
                        load_adj(b, 1, s)
                    if s == 7 and not last:
                        load_x(b + 1, 1)
                    if s == 11 and not (first or is_l0):
                        store(b - 1, 0)
                    if s in (11, 12):
                        norm_dma(b, 0, s - 11)
                    if s in (14, 15):
                        norm_dma(b, 0, s - 12)
                if not last:
                    stack(b + 1, 0, 0)
                if here:
                    max_rows(b, 1)
                if not last:
                    stack_biases(b + 1, 0)
                    stack(b + 1, 0, 1)
                if not (first or is_l0):
                    store(b - 1, 1)
                norm_dma(b, 1, 0)
                if not last:
                    stack(b + 1, 0, 2)
                norm_dma(b, 1, 1)
                if not last:
                    stack(b + 1, 0, 3)
                    load_adj(b + 1, 0, 0)
                    load_adj(b + 1, 0, 1)
                norm_dma(b, 1, 2)
                norm_dma(b, 1, 3)
                if is_l0:
                    load_residual_l0(b, last)
                for s in range(8, STEPS):
                    if 9 <= s < 15 and not last:
                        load_adj(b + 1, 0, s - 7)
                    if s in (11, 12):
                        norm_dma(b, 2, s - 11)
                    if s in (14, 15):
                        norm_dma(b, 2, s - 12)
                if not last:
                    load_adj(b + 1, 1, 0)
                    load_adj(b + 1, 1, 1)
                if is_l0 and not last:
                    stack(b + 1, 1, 0)
                    max_rows(b + 1, 0)
                    norm_dma(b, 3, 0)
                    stack(b + 1, 1, 1)
                    for part in (1, 2, 3):
                        norm_dma(b, 3, part)
                    stack(b + 1, 1, 2)
                    stack(b + 1, 1, 3)
                elif last:
                    for part in range(4):
                        norm_dma(b, 3, part)
                if is_l0 or last:
                    if not is_l0:
                        load_residual(b)
                    store(b, 0)
                    store(b, 1)
                if is_l0 and not last:
                    max_rows(b + 1, 1)

            graph(0, True, False)
            with sp.Fori(1, last_b) as b:
                graph(b, False, False)
            graph(last_b, False, True)
            sp.wait_ge(stored, BATCH * 2 * DMA)

        @block.tensor
        def _(pe):
            small_hist, big_hist = [None, None], [None, None]
            n_small = n_big = 0

            def small_slot(done_sem, done_value):
                nonlocal n_small
                if small_hist[-2] is not None:
                    pe.wait_ge(*small_hist[-2])
                small_hist.append((done_sem, done_value))
                n_small += 1
                return small[(n_small - 1) % 2]

            def big_slot(done_sem, done_value):
                nonlocal n_big
                if big_hist[-2] is not None:
                    pe.wait_ge(*big_hist[-2])
                big_hist.append((done_sem, done_value))
                n_big += 1
                return big[(n_big - 1) % 2]

            def turn_weights():
                pe.wait_ge(w_raw_loaded, 4 * DMA)
                for i in range(4):
                    tile = small_slot(w_copied, i + 1)
                    for k in range(KC):
                        for o in range(KC):
                            mm = pe.transpose(tile[:, k * D + o * P:k * D + (o + 1) * P],
                                              et[:, i, o * D + k * P:o * D + (k + 1) * P], ident[:, :])
                    mm.then_inc(w_turned, 1)

            def turn_x(b, hf, k):
                if is_l0:
                    pe.wait_ge(xln_done, b * 2 + hf + 1)
                else:
                    pe.wait_ge(x_loaded, (b * 2 + hf + 1) * DMA)
                tile = small_slot(xt_ready, b * 4 + hf * 2 + k + 1)
                for c in range(HC):
                    mm = pe.transpose(tile[:, c * P:(c + 1) * P], xbuf[:, c, k * P:(k + 1) * P], ident[:, :])
                mm.then_inc(x_turned, 1)

            def turn_adj(b, nh, job):
                pe.wait_ge(adj_ready, et_no(b, nh, job) + 1)
                tile = small_slot(et_ready, et_no(b, nh, job) + 1)
                for c in range(HC):
                    mm = pe.transpose(tile[:, c * P:(c + 1) * P], adj_sb[job % 2][:, c * P:(c + 1) * P], ident[:, :])
                mm.then_inc(et_turned, 1)

            def project_ca(b, hf):
                pe.wait_ge(xt_ready, (b + 1) * 4)
                tile = small_slot(ca_ready, b * 2 + hf + 1)
                for k in range(KC):
                    mm = pe.matmul(tile[0:2, :], wg[:, k, :], xt[:, k, hf * HALF:(hf + 1) * HALF],
                                   start=k == 0, stop=k == KC - 1)
                mm.then_inc(ca_made, 1)

            def project_qk(b, g, which):
                pe.wait_ge(xt_ready, (b + 1) * 4)
                tile = big_slot(split_copied, (b * G + g) * 4 + which * 2 + 2)
                wt = wq if which == 0 else wk
                for nh in range(2):
                    for k in range(KC):
                        mm = pe.matmul(tile[:, nh * HALF:(nh + 1) * HALF], wt[:, k, g * P:(g + 1) * P],
                                       xt[:, k, nh * HALF:(nh + 1) * HALF], start=k == 0, stop=k == KC - 1)
                mm.then_inc(qk_made, 1)

            def project_v(b, j):
                pe.wait_ge(xt_ready, (b + 1) * 4)
                tile = big_slot(v_copied, b * 2 + j + 1)
                for c in range(HC):
                    for k in range(KC):
                        mm = pe.matmul(tile[:, c * D:(c + 1) * D], xt[:, k, (j * HC + c) * P:(j * HC + c + 1) * P],
                                       wv[:, k, :], start=k == 0, stop=k == KC - 1)
                mm.then_inc(v_made, 1)

            def score_for_max(b, g, u):
                h, c, mh = u // (2 * NC), u // 2 % NC, u % 2
                if u % (2 * NC) == 0:
                    pe.wait_ge(stack_loaded[g][h], (b + 1) * (head_dmas * DMA))
                if is_l1 and u == 0:
                    pe.wait_ge(bias_loaded[g], (b + 1) * (n_bias * DMA))
                tile = small_slot(max_taken, unit_no(b, g, u) + 1)
                pe.matmul(tile[:, :], qs[g][0:k_max, h, c * P:(c + 1) * P], ks[g][0:k_max, h, mh * HALF:(mh + 1) * HALF],
                          start=True, stop=True).then_inc(max_scored, 1)

            def score_two_for_max(v):
                h, c = v // NC, v % NC
                if c == 0:
                    pe.wait_ge(stack_loaded[0][h], head_dmas * DMA)
                if is_l1 and v == 0:
                    pe.wait_ge(bias_loaded[0], n_bias * DMA)
                tile = big_slot(max_taken, 2 * v + 2)
                for mh in range(2):
                    mm = pe.matmul(tile[:, mh * HALF:(mh + 1) * HALF], qs[0][0:k_max, h, c * P:(c + 1) * P],
                                   ks[0][0:k_max, h, mh * HALF:(mh + 1) * HALF], start=True, stop=True)
                mm.then_inc(max_scored, 2)

            def turn_max(b, g):
                pe.wait_ge(neg_max_ready, b * G + g + 1)
                tile = small_slot(max_rows_ready, b * G + g + 1)
                pe.transpose(tile[0:GH * NC, 0:P], neg_max[:, :], ident[:, :]).then_inc(max_turned, 1)

            def do_job(b, j):
                kind, db, *rest = j
                {"et": turn_adj, "xt": turn_x, "ca": project_ca, "max": score_for_max, "max_rows": turn_max}[kind](b + db, *rest)

            def score(b, g, s, t):
                nh, mc = s // NC, s % NC
                tile = big_slot(exp_done, step_no(b, g, s) * 2 + t + 1)
                for j in range(2):
                    h = 2 * t + j
                    mm = pe.matmul(tile[:, j * HALF:(j + 1) * HALF], ks[g][0:k_all, h, mc * P:(mc + 1) * P],
                                   qs[g][0:k_all, h, nh * HALF:(nh + 1) * HALF], start=True, stop=True)
                mm.then_inc(scored, 1)

            def attend(b, g, s):
                mc = s % NC
                n = step_no(b, g, s)
                if s == 0:
                    pe.wait_ge(v_ready, (b + 1) * 2)
                for ready in probs_ready:
                    pe.wait_ge(ready, n + 1)
                if mc == 0:
                    wait_from(pe, pv_copied, (b * 4 + g * 2 + s // NC) * 2)
                for h in range(GH):
                    pe.matmul(pv[h * HD:(h + 1) * HD, :], v_sb[:, mc, (g * GH + h) * HD:(g * GH + h + 1) * HD],
                              probs[:, p_slot(s), h // 2, h % 2, :], start=mc == 0, stop=mc == NC - 1)

            def sum_probs(b, g, s):
                mc = s % NC
                for h in range(GH):
                    mm = pe.matmul(rowsum[h * HD:(h + 1) * HD, :], ones[:, :], probs[:, p_slot(s), h // 2, h % 2, :],
                                   start=mc == 0, stop=mc == NC - 1)
                mm.then_inc(pv_done, 1)

            def phase(b, g, first, last):
                pe.wait_ge(max_loaded[g], (b + 1) * (2 * DMA))
                for s in range(STEPS):
                    maxima, others = jobs_at(g, s, first, last)
                    score(b, g, s, 0)
                    for j in maxima[0:1]:
                        do_job(b, j)
                    score(b, g, s, 1)
                    for j in maxima[1:2]:
                        do_job(b, j)
                    if s == QK_STEP and not last:
                        project_qk(b + 1, g, 0)
                        project_qk(b + 1, g, 1)
                    if g == 0 and not (first or is_l0) and s in CLOSE_STEPS:
                        close_half(b - 1, CLOSE_STEPS.index(s))
                    if s >= LAG:
                        attend(b, g, s - LAG)
                    for j in maxima[2:4]:
                        do_job(b, j)
                    if s >= LAG:
                        sum_probs(b, g, s - LAG)
                    for j in maxima[4:] + others:
                        do_job(b, j)
                attend(b, g, STEPS - 2)
                sum_probs(b, g, STEPS - 2)
                if g == 1 and not last:
                    project_v(b + 1, 0)
                attend(b, g, STEPS - 1)
                sum_probs(b, g, STEPS - 1)
                if g == 1 and not last:
                    project_v(b + 1, 1)

            def close_half(b, j):
                if j == 0:
                    pe.wait_ge(ot_ready, (b + 1) * 4)
                tile = big_slot(c_copied, b * C_TILES + j + 1)
                for c in range(HC):
                    for g in range(G):
                        o = ot[:, g, (j * HC + c) * P:(j * HC + c + 1) * P]
                        if is_l1:
                            mm = pe.transpose(tile[:, c * D + g * P:c * D + (g + 1) * P], o, ident[:, :])
                        else:
                            mm = pe.matmul(tile[:, c * D:(c + 1) * D], o, wo[:, g, :], start=g == 0, stop=g == G - 1)
                mm.then_inc(c_made, 1)

            def close_l0(b, last):
                u, n_f1 = 0, 0

                def some_maxima(count):
                    nonlocal u
                    if not last:
                        for _ in range(count):
                            score_for_max(b + 1, 1, u)
                            u += 1

                for what, j in CLOSE_L0:
                    if what == "max":
                        some_maxima(j)
                        continue
                    if what == "wo":
                        pe.wait_ge(ot_ready, b * 4 + 3 + j)
                        tile = big_slot(y_ready, b * 2 + j + 1)
                        for c in range(HC):
                            for g in range(G):
                                mm = pe.matmul(tile[:, c * D:(c + 1) * D], ot[:, g, (j * HC + c) * P:(j * HC + c + 1) * P],
                                               wo[:, g, :], start=g == 0, stop=g == G - 1)
                    elif what == "ln":
                        pe.wait_ge(cln_done, b * 2 + j + 1)
                        tile = big_slot(h2_ready, b * 2 + j + 1)
                        for k in range(KC):
                            for c in range(HC):
                                mm = pe.transpose(tile[:, k * HALF + c * P:k * HALF + (c + 1) * P],
                                                  xhat[j][:, c, k * P:(k + 1) * P], ident[:, :])
                    elif what == "f1":
                        i = n_f1 % (FC // 2)
                        n_f1 += 1
                        if i == 0:
                            pe.wait_ge(h2_ready, b * 2 + j + 1)
                        tile = big_slot(gelu_done, b * FC + n_f1)
                        for jj in range(2):
                            f = 2 * i + jj
                            for k in range(KC):
                                mm = pe.matmul(tile[:, jj * HALF:(jj + 1) * HALF], wf1[:, k, f * P:(f + 1) * P],
                                               xt[:, k, j * HALF:(j + 1) * HALF], start=k == 0, stop=k == KC - 1)
                            if jj == 1:
                                mm.then_inc(c_made, 1)
                            some_maxima(2)
                    else:
                        pe.wait_ge(gelu_done, b * FC + n_f1)
                        tile = big_slot(out_ready, b * 2 + j + 1)
                        for c in range(HC):
                            for f in range(FC):
                                mm = pe.matmul(tile[:, c * D:(c + 1) * D], hid[:, f, c * P:(c + 1) * P], wf2[:, f, :],
                                               start=f == 0, stop=f == FC - 1)
                            if c == HC - 1:
                                mm.then_inc(c_made, 1)
                            some_maxima(2)
                    if what in ("wo", "ln"):
                        mm.then_inc(c_made, 1)
                if not last:
                    turn_max(b + 1, 1)

            pe.wait_ge(consts_ready, n_consts)
            if is_l3:
                turn_weights()
                pe.wait_ge(w_copied, 4)
            for hf in range(2):
                for k in range(KC):
                    turn_x(0, hf, k)
            pe.wait_ge(weights_loaded, n_weights * DMA)
            if is_l1:
                project_ca(0, 0)
                project_ca(0, 1)
            project_qk(0, 0, 0)
            project_qk(0, 0, 1)
            project_v(0, 0)
            project_v(0, 1)
            project_qk(0, 1, 0)
            project_qk(0, 1, 1)
            assert n_big % 2 == 0
            for what, i in prologue_jobs():
                if what == "et":
                    turn_adj(0, 0, i)
                else:
                    score_two_for_max(i)
            if n_late:
                pe.wait_ge(late_loaded, n_late * DMA)
            turn_max(0, 0)

            def graph(b, first, last):
                phase(b, 0, first, last)
                phase(b, 1, first, last)
                if is_l0:
                    assert n_big % 2 == 0
                    close_l0(b, last)
                elif last:
                    close_half(b, 0)
                    close_half(b, 1)

            def ring_readers(b):
                if is_l0:
                    small_hist[:] = [(max_taken, unit_no(b, 1, MAX_UNITS - 1) + 1), (max_rows_ready, b * G + 2)]
                    big_hist[:] = [(gelu_done, b * FC), (out_ready, b * 2)]
                else:
                    small_hist[:] = [(et_ready, et_no(b, 0, 7) + 1), (max_rows_ready, b * G + 1)]
                    big_hist[:] = [(v_copied, b * 2 + 1), (v_copied, b * 2 + 2)]

            graph(0, True, False)
            n_small_loop, n_big_loop = n_small, n_big
            with pe.Fori(1, last_b) as b:
                ring_readers(b)
                graph(b, False, False)
            assert (n_small - n_small_loop) % 2 == 0 and (n_big - n_big_loop) % 2 == 0
            ring_readers(last_b)
            graph(last_b, False, True)

        @block.scalar
        def _(act):
            n_big = 0

            def big_slot():
                nonlocal n_big
                n_big += 1
                return big[(n_big - 1) % 2]

            n_small = 0

            def small_slot():
                nonlocal n_small
                n_small += 1
                return small[(n_small - 1) % 2]

            def skip_small(count):
                nonlocal n_small
                n_small += count

            def edge_nat(b, nh, job):
                act.wait_ge(adj_loaded[job % 2], (b * 8 + nh * 4 + job // 2 + 1) * DMA)
                wait_from(act, adj_ready, et_no(b, nh, job))
                act.activation(edge_exp[:, :], adj_sb[job % 2][:, :], ACT.Exp, bias=edge_bias[:, :], scale=2.0
                               ).then_inc(adj_exp, 1)

            def edge_to_t(b, nh, job, read_until):
                c, mh = et_job(job)
                n = et_no(b, nh, job)
                act.wait_ge(et_turned, n + 1)
                if read_until is not None:
                    for ready in probs_ready:
                        wait_from(act, ready, read_until)
                q0 = (nh * HC + c) * P
                act.activation(et[:, mh * HC:(mh + 1) * HC, q0:q0 + P],
                               small_slot()[:, :].rearrange("p (c n) -> p c n", n=P), ACT.Copy).then_inc(et_ready, 1)

            def copy_qk(b, g, which):
                n = (b * G + g) * 2 + which
                act.wait_ge(qk_made, n + 1)
                wait_stacks(act, 1 - g, b + g)
                tile = big_slot()
                scale, bias = (SCALE, bq) if which == 0 else (1.0, bk)
                act.activation(split_lo[which][:, :].bitcast(F32), tile[:, :], ACT.Identity,
                               bias=bias[:, g:g + 1], scale=scale).then_inc(split_copied, 1)
                act.activation(split_hi[which][:, :], tile[:, :], ACT.Identity,
                               bias=bias[:, g:g + 1], scale=scale).then_inc(split_copied, 1)

            def copy_v(b, j):
                act.wait_ge(v_made, b * 2 + j + 1)
                wait_from(act, pv_done, step_no(b, 0, 0))
                act.activation(v_sb[:, j * HC:(j + 1) * HC, :].rearrange("p c d -> p (c d)"), big_slot()[:, :], ACT.Copy
                               ).then_inc(v_copied, 1)

            def exps(b, g, s):
                n = step_no(b, g, s)
                slot = p_slot(s)
                wait_from(act, pv_done, n - (P_SLOTS - 1) if s >= P_SLOTS else step_no(b, g, 0))
                for t in range(2):
                    act.wait_ge(scored, n * 2 + t + 1)
                    act.activation(probs[:, slot, t, :, :].rearrange("p h n -> p (h n)"), big_slot()[:, :], ACT.Exp
                                   ).then_inc(exp_done, 1)

            def copy_pv(b, q):
                n = b * 4 + q
                act.wait_ge(pv_done, (n + 1) * NC)
                wait_from(act, sums_out, n * DMA)
                act.activation(ot[:, q // 2, (q % 2) * HALF:(q % 2 + 1) * HALF], pv[:, :], ACT.Copy).then_inc(pv_copied, 1)
                act.activation(sums[:, :], rowsum[:, :], ACT.Copy).then_inc(pv_copied, 1)

            def phase(b, g, first, last):
                if is_l0 and g == 0:
                    edge_nat(b, 1, 0)
                for s in range(STEPS):
                    exps(b, g, s)
                    if is_l0:
                        for j in edge_jobs(g, s, last):
                            edge_nat(b + j[0], *j[1:])
                    if s == QK_STEP and not last:
                        copy_qk(b + 1, g, 0)
                        copy_qk(b + 1, g, 1)
                    if g == 0 and not (first or is_l0) and s in CLOSE_STEPS:
                        close_half(b - 1, CLOSE_STEPS.index(s))
                    if s == NC + LAG - 1:
                        copy_pv(b, 2 * g)
                    maxima, others = jobs_at(g, s, first, last)
                    skip_small(len(maxima))
                    for kind, db, *rest in others:
                        if kind == "et":
                            edge_to_t(b + db, *rest, step_no(b, 1, 8) if db else step_no(b, 0, 0))
                        else:
                            skip_small(1)
                if g == 1 and not last:
                    copy_v(b + 1, 0)
                copy_pv(b, 2 * g + 1)
                if g == 1 and not last:
                    copy_v(b + 1, 1)

            def close_half(b, j):
                act.wait_ge(c_made, b * C_TILES + j + 1)
                act.activation(y[j][:, :, :].rearrange("p c d -> p (c d)"), big_slot()[:, :], ACT.Copy).then_inc(c_copied, 1)

            def close_l0(b):
                n_f1 = 0
                for i, (what, j) in enumerate(CLOSE_TILES):
                    t = big_slot()
                    if what in ("wo", "f2"):
                        continue
                    act.wait_ge(c_made, b * C_TILES + i + 1)
                    if what == "ln":
                        for k in range(KC):
                            op = act.activation(xt[:, k, j * HALF:(j + 1) * HALF], t[:, k * HALF:(k + 1) * HALF],
                                                ACT.Identity, bias=b2[:, k:k + 1], scale=g2[:, k:k + 1])
                        op.then_inc(h2_ready, 1)
                    else:
                        for jj in range(2):
                            f = 2 * (n_f1 % (FC // 2)) + jj
                            op = act.activation(hid[:, f, :], t[:, jj * HALF:(jj + 1) * HALF], ACT.Gelu, bias=bf1[:, f:f + 1])
                        op.then_inc(gelu_done, 1)
                        n_f1 += 1

            act.wait_ge(consts_ready, n_consts)
            act.wait_ge(weights_loaded, n_weights * DMA)
            act.activation(bq[:, :], bq[:, :], ACT.Copy, scale=SCALE).then_inc(w_scaled, 1)
            act.wait_ge(w_scaled, 1)
            skip_small(4 * is_l3 + 4 + 2 * is_l1)
            copy_qk(0, 0, 0)
            copy_qk(0, 0, 1)
            copy_v(0, 0)
            copy_v(0, 1)
            if is_l0:
                edge_nat(0, 0, 0)
            copy_qk(0, 1, 0)
            copy_qk(0, 1, 1)
            for what, i in prologue_jobs():
                if what == "et":
                    if is_l0 and i < 7:
                        edge_nat(0, 0, i + 1)
                    edge_to_t(0, 0, i, None)
            skip_small(1)
            if n_late:
                act.wait_ge(late_loaded, n_late * DMA)

            def graph(b, first, last):
                phase(b, 0, first, last)
                phase(b, 1, first, last)
                if is_l0:
                    close_l0(b)
                    if not last:
                        skip_small(MAX_UNITS + 1)
                elif last:
                    close_half(b, 0)
                    close_half(b, 1)

            graph(0, True, False)
            with act.Fori(1, last_b) as b:
                graph(b, False, False)
            graph(last_b, False, True)

        @block.vector
        def _(dve):
            n_small = 0

            def small_slot():
                nonlocal n_small
                n_small += 1
                return small[(n_small - 1) % 2]

            def skip_small(count):
                nonlocal n_small
                n_small += count

            def layernorm_stats(src, mv_sem):
                for c in range(HC):
                    dve.bn_stats(ln_raw[:, c, :], src[:, c, :])
                dve.drain()
                for c in range(HC):
                    op = dve.bn_aggr(ln_mv[:, c, :], ln_raw[:, c, :])
                op.then_inc(mv_sem, 1)

            def layernorm_apply(dst, src, rstd_sem, done_sem, n):
                dve.wait_ge(rstd_sem, n + 1)
                for c in range(HC):
                    op = dve.tensor_scalar(dst[:, c, :], src[:, c, :], ln_mv[:, c, 0:1], ln_rstd[:, c:c + 1],
                                           ALU.subtract, ALU.mult)
                op.then_inc(done_sem, 1)

            def x_stats(b, hf):
                dve.wait_ge(x_loaded, (b * 2 + hf + 1) * DMA)
                layernorm_stats(xbuf, xln_mv)

            def x_norm(b, hf):
                layernorm_apply(xbuf, xbuf, xln_rstd, xln_done, b * 2 + hf)

            def x_to_t(b, hf, k):
                tile = small_slot()
                dve.wait_ge(x_turned, b * 4 + hf * 2 + k + 1)
                dst = xt[:, k, hf * HALF:(hf + 1) * HALF]
                if is_l0:
                    op = dve.tensor_scalar(dst, tile[:, :], g1[:, k:k + 1], b1[:, k:k + 1], ALU.mult, ALU.add)
                else:
                    op = dve.tensor_copy(dst, tile[:, :])
                op.then_inc(xt_ready, 1)

            def edge_factor(b, nh, job):
                n = et_no(b, nh, job)
                tile = adj_sb[job % 2][:, :]
                if is_l0:
                    dve.wait_ge(adj_exp, n + 1)
                    op = dve.scalar_tensor_tensor(out=tile, in0=tile, scalar=1.0 / 3.0, in1=edge_exp[:, :],
                                                  op0=ALU.add, op1=ALU.mult)
                else:
                    dve.wait_ge(adj_loaded[job % 2], (b * 8 + nh * 4 + job // 2 + 1) * DMA)
                    op = dve.tensor_scalar(tile, tile, 1e-8, None, ALU.max)
                op.then_inc(adj_ready, 1)

            def take_max(b, g, u):
                h, c, mh = u // (2 * NC), u // 2 % NC, u % 2
                tile = small_slot()
                dve.wait_ge(max_scored, unit_no(b, g, u) + 1)
                dve.tensor_reduce(max_part[:, h * NC + c, mh:mh + 1], tile[:, :], AX.X, ALU.max).then_inc(max_taken, 1)

            def take_two_max(v):
                dve.wait_ge(max_scored, 2 * v + 2)
                dve.tensor_reduce(max_part[:, v, :], big[v % 2][:, :].rearrange("p (m n) -> p m n", n=HALF), AX.X, ALU.max
                                  ).then_inc(max_taken, 2)

            def negate_max(b, g):
                dve.wait_ge(max_taken, unit_no(b, g, MAX_UNITS - 1) + 1)
                dve.tensor_reduce(neg_max[:, :], max_part[:, :, :], AX.X, ALU.max, negate=True).then_inc(neg_max_ready, 1)

            def max_to_rows(b, g):
                n = b * G + g
                tile = small_slot()[0:GH * NC, 0:P]
                dve.wait_ge(max_turned, n + 1)
                wait_from(dve, max_loaded[1 - g], (b + g) * (2 * DMA))
                dve.tensor_copy(max_hi[:, :], tile).then_inc(max_hi_ready, 1)
                dve.wait_ge(max_hi_ready, n + 1)
                dve.tensor_tensor(max_lo[:, :], tile, max_hi[:, :].bitcast(F32), ALU.subtract).then_inc(max_rows_ready, 1)

            def take_ca(b, hf):
                if hf == 0:
                    wait_from(dve, bias_loaded[1], b * (n_bias * DMA))
                n = b * 2 + hf
                tile = small_slot()[0:2, :]
                cols = slice(hf * HALF, (hf + 1) * HALF)
                dve.wait_ge(ca_made, n + 1)
                dve.tensor_scalar(ca_lo[:, cols].bitcast(F32), tile, bg[:, 0:1], None, ALU.add).then_inc(ca_copied, 1)
                dve.tensor_scalar(ca_hi[:, cols], tile, bg[:, 0:1], None, ALU.add).then_inc(ca_hi_ready, 1)
                dve.wait_ge(ca_hi_ready, n + 1)
                dve.wait_ge(ca_copied, n + 1)
                dve.tensor_tensor(ca_lo[:, cols], ca_lo[:, cols].bitcast(F32), ca_hi[:, cols].bitcast(F32),
                                  ALU.subtract).then_inc(ca_ready, 1)

            def split(b, g, which):
                dve.wait_ge(split_copied, (b * G + g) * 4 + which * 2 + 2)
                lo, hi = split_lo[which], split_hi[which]
                dve.tensor_tensor(lo[:, :], lo[:, :].bitcast(F32), hi[:, :].bitcast(F32), ALU.subtract).then_inc(split_ready, 1)

            def weigh(b, g, s):
                n = step_no(b, g, s)
                nh, mc = s // NC, s % NC
                dve.wait_ge(et_ready, et_no(b, nh, 7) + 1)
                dve.wait_ge(exp_done, n * 2 + 2)
                pr = probs[:, p_slot(s), 1, :, POOL_COLS:]
                dve.tensor_tensor(pr, pr, et[:, mc, None, nh * HALF + POOL_COLS:(nh + 1) * HALF].to_broadcast(
                    [P, 2, HALF - POOL_COLS]), ALU.mult).then_inc(probs_ready[1], 1)

            def recip(b, q):
                n = b * 4 + q
                dve.wait_ge(sums_in, (n + 1) * DMA)
                wait_from(dve, recip_out, n * DMA)
                dve.reciprocal(recip_col[:, :], sums_col[:, :]).then_inc(recip_ready, 1)

            def do_job(b, j):
                kind, db, *rest = j
                if kind == "et":
                    skip_small(1)
                else:
                    {"xt": x_to_t, "ca": take_ca, "max": take_max, "max_rows": max_to_rows}[kind](b + db, *rest)

            def phase(b, g, first, last):
                if g == 0 and not is_l1:
                    edge_factor(b, 1, 0)
                for s in range(STEPS):
                    maxima, others = jobs_at(g, s, first, last)
                    if any(j[0] == "max_rows" for j in others):
                        negate_max(b + g, 1 - g)
                    for j in maxima[:2]:
                        do_job(b, j)
                    if s > 0:
                        weigh(b, g, s - 1)
                    if s == 3 and not (first or is_l0 or g == 1):
                        recip(b - 1, 3)
                    for j in maxima[2:] + others:
                        do_job(b, j)
                    if not is_l1:
                        for db, nh, j in edge_jobs(g, s, last):
                            edge_factor(b + db, nh, j)
                    if is_l0 and g == 0 and not last:
                        if s in (4, 9):
                            x_stats(b + 1, s // 9)
                        if s in (5, 10):
                            x_norm(b + 1, s // 10)
                    if s in (QK_STEP + 1, QK_STEP + 2) and not last:
                        split(b + 1, g, s - QK_STEP - 1)
                    if g == 0 and not (first or is_l0):
                        if is_l3 and s - 2 in CLOSE_STEPS:
                            y_stats(b - 1, CLOSE_STEPS.index(s - 2))
                        if is_l3 and s - 3 in CLOSE_STEPS:
                            y_norm(b - 1, CLOSE_STEPS.index(s - 3))
                    if (g, s) == (1, 3):
                        recip(b, 1)
                    if s == 13:
                        recip(b, 2 * g)
                weigh(b, g, STEPS - 1)

            def y_stats(b, j):
                dve.wait_ge(y_ready, b * 2 + j + 1)
                layernorm_stats(y[j], cln_mv)

            def y_norm(b, j):
                layernorm_apply(xhat[j] if is_l0 else y[j], y[j], cln_rstd, cln_done, b * 2 + j)

            def add_tile(b, j, i, ready):
                dve.wait_ge(c_made, b * C_TILES + i + 1)
                flat_y = y[j][:, :, :].rearrange("p c d -> p (c d)")
                dve.tensor_tensor(flat_y, flat_y, big[i % 2][:, :], ALU.add).then_inc(ready, 1)

            def close_l0(b, last):
                u, i = 0, 0

                def some_maxima(count):
                    nonlocal u
                    if not last:
                        for _ in range(count):
                            take_max(b + 1, 1, u)
                            u += 1

                for what, j in CLOSE_L0:
                    if what == "max":
                        if i == 1:
                            some_maxima(2)
                            y_norm(b, 0)
                            some_maxima(3)
                            recip(b, 3)
                            some_maxima(j - 5)
                        elif i == 2:
                            some_maxima(2)
                            y_norm(b, 1)
                            some_maxima(j - 2)
                        else:
                            some_maxima(j)
                        continue
                    if what == "wo":
                        dve.wait_ge(c_biased, b * 2 + j + 1)
                        add_tile(b, j, i, y_ready)
                        y_stats(b, j)
                    elif what == "f1":
                        some_maxima(4)
                    elif what == "f2":
                        some_maxima(2 * HC)
                        dve.wait_ge(out_mid, b * 2 + j + 1)
                        add_tile(b, j, i, out_ready)
                    i += 1
                if not last:
                    negate_max(b + 1, 1)
                    max_to_rows(b + 1, 1)

            for g in range(G):
                dve.memset(ks[g][3 * HD:P, :, :].bitcast(F32), 1.0).then_inc(consts_ready, 1)
            if not is_l1:
                dve.memset(minus_half[:, :], -0.5).then_inc(consts_ready, 1)
                dve.memset(ln_eps[:, :], LN_EPS).then_inc(consts_ready, 1)
            if is_l0:
                dve.memset(edge_bias[:, :], math.log(0.75) - 1.0).then_inc(consts_ready, 1)
            if is_l1:
                dve.memset(adj_floor[:, :], 1e-9).then_inc(consts_ready, 1)
            if is_l1:
                dve.memset(bg[:, :], 0.0).then_inc(bg_cleared, 1)
            dve.wait_ge(consts_ready, n_consts)
            if is_l3:
                for i, t in enumerate((wq, wk, wv, wo)):
                    tile = small_slot()
                    dve.wait_ge(w_turned, i + 1)
                    dve.tensor_copy(t[:, :, :].rearrange("p k o -> p (k o)"), tile[:, :]).then_inc(w_copied, 1)
                dve.wait_ge(w_copied, 4)
            dve.wait_ge(weights_loaded, n_weights * DMA)
            for hf in range(2):
                if is_l0:
                    x_stats(0, hf)
                    x_norm(0, hf)
                for k in range(KC):
                    x_to_t(0, hf, k)
            if is_l1:
                take_ca(0, 0)
                take_ca(0, 1)
            split(0, 0, 0)
            split(0, 0, 1)
            if not is_l1:
                edge_factor(0, 0, 0)
            for what, i in prologue_jobs():
                if what == "et":
                    skip_small(1)
                    if not is_l1 and i < 7:
                        edge_factor(0, 0, i + 1)
                    if i in (2, 3):
                        split(0, 1, i - 2)
                else:
                    take_two_max(i)
            negate_max(0, 0)
            max_to_rows(0, 0)

            def graph(b, first, last):
                phase(b, 0, first, last)
                phase(b, 1, first, last)
                if is_l0:
                    close_l0(b, last)
                elif last:
                    recip(b, 3)
                    for j in range(2 if is_l3 else 0):
                        y_stats(b, j)
                        y_norm(b, j)

            graph(0, True, False)
            with dve.Fori(1, last_b) as b:
                graph(b, False, False)
            graph(last_b, False, True)

        @block.gpsimd
        def _(pool):
            def rstd(mv_sem, var_sem, rstd_sem, n):
                pool.wait_ge(mv_sem, n + 1)
                pool.tensor_tensor(ln_var[:, :], ln_mv[:, :, 1], ln_eps[:, :], ALU.add).then_inc(var_sem, 1)
                pool.wait_ge(var_sem, n + 1)
                pool.tensor_tensor(ln_rstd[:, :], ln_var[:, :], minus_half[:, :], ALU.pow).then_inc(rstd_sem, 1)

            def rows(t):
                return t[:, None, :].to_broadcast([P, HC, D])

            def edge_floor(b, nh, job):
                pool.wait_ge(adj_loaded[job % 2], (b * 8 + nh * 4 + job // 2 + 1) * DMA)
                pool.tensor_tensor(adj_sb[job % 2][:, :], adj_sb[job % 2][:, :], adj_floor[:, :].to_broadcast([P, HALF]),
                                   ALU.add).then_inc(adj_ready, 1)

            def bias_v(b, j):
                pool.wait_ge(v_copied, b * 2 + j + 1)
                part = v_sb[:, j * HC:(j + 1) * HC, :]
                pool.tensor_tensor(part, part, rows(bv_bc), ALU.add).then_inc(v_ready, 1)

            def weigh(b, g, s):
                n = step_no(b, g, s)
                nh, mc = s // NC, s % NC
                pool.wait_ge(et_ready, et_no(b, nh, 7) + 1)
                pool.wait_ge(exp_done, n * 2 + 1)
                pr = probs[:, p_slot(s), 0, :, :]
                pool.tensor_tensor(pr, pr, et[:, mc, None, nh * HALF:(nh + 1) * HALF].to_broadcast([P, 2, HALF]),
                                   ALU.mult).then_inc(probs_ready[0], 1)
                pool.wait_ge(exp_done, n * 2 + 2)
                pr = probs[:, p_slot(s), 1, :, 0:POOL_COLS]
                pool.tensor_tensor(pr, pr, et[:, mc, None, nh * HALF:nh * HALF + POOL_COLS].to_broadcast([P, 2, POOL_COLS]),
                                   ALU.mult).then_inc(probs_ready[2], 1)

            def normalise(b, q):
                pool.wait_ge(recip_in, (b * 4 + q + 1) * DMA)
                part = ot[:, q // 2, (q % 2) * HALF:(q % 2 + 1) * HALF]
                pool.tensor_tensor(part, part, recip_bc[:, :], ALU.mult).then_inc(ot_ready, 1)

            def phase(b, g, first, last):
                if g == 0 and is_l1:
                    edge_floor(b, 1, 0)
                for s in range(STEPS):
                    weigh(b, g, s)
                    if is_l1:
                        for db, nh, job in edge_jobs(g, s, last):
                            edge_floor(b + db, nh, job)
                    if is_l0 and g == 0 and not last and s in (4, 9):
                        rstd(xln_mv, xln_var, xln_rstd, (b + 1) * 2 + s // 9)
                    if g == 0 and not (first or is_l0):
                        if s == 5:
                            normalise(b - 1, 3)
                        if s - 1 in CLOSE_STEPS:
                            add_residual(b - 1, CLOSE_STEPS.index(s - 1))
                        if is_l3 and s - 2 in CLOSE_STEPS:
                            rstd(cln_mv, cln_var, cln_rstd, (b - 1) * 2 + CLOSE_STEPS.index(s - 2))
                        if is_l3 and s - 3 in CLOSE_STEPS:
                            scale_y(b - 1, CLOSE_STEPS.index(s - 3))
                        if is_l3 and s - 4 in CLOSE_STEPS:
                            shift_y(b - 1, CLOSE_STEPS.index(s - 4))
                    if (g, s) == (1, 5):
                        normalise(b, 1)
                    if is_l0 and g == 1 and s in (10, 12):
                        bias_residual_l0(b, (s - 10) // 2)
                normalise(b, 2 * g)

            def add_residual(b, j):
                n = b * 2 + j
                x_res = res[:, j * HC:(j + 1) * HC, :]
                pool.wait_ge(res_loaded[0], (b + 1) * DMA)
                if not is_l1:
                    pool.tensor_tensor(x_res, x_res, rows(bo_bc), ALU.add).then_inc(c_biased, 1)
                    pool.wait_ge(c_biased, n + 1)
                pool.wait_ge(c_copied, n + 1)
                yj = y[j]
                pool.tensor_tensor(yj[:, :, :], yj[:, :, :], x_res, ALU.add).then_inc(out_ready if is_l1 else y_ready, 1)

            def scale_y(b, j):
                pool.wait_ge(cln_done, b * 2 + j + 1)
                pool.tensor_tensor(y[j][:, :, :], y[j][:, :, :], rows(gamma_bc), ALU.mult).then_inc(out_mid, 1)

            def shift_y(b, j):
                pool.wait_ge(out_mid, b * 2 + j + 1)
                pool.tensor_tensor(y[j][:, :, :], y[j][:, :, :], rows(beta_bc), ALU.add).then_inc(out_ready, 1)

            def close_half(b, j):
                add_residual(b, j)
                if is_l3:
                    rstd(cln_mv, cln_var, cln_rstd, b * 2 + j)
                    scale_y(b, j)
                    shift_y(b, j)

            def bias_residual_l0(b, j):
                pool.wait_ge(res_loaded[j], (b + 1) * DMA)
                pool.tensor_tensor(y[j][:, :, :], y[j][:, :, :], rows(bo_bc), ALU.add).then_inc(c_biased, 1)

            def bias_out_l0(b, j):
                pool.wait_ge(cln_done, b * 2 + j + 1)
                pool.tensor_tensor(y[j][:, :, :], y[j][:, :, :], rows(bf2_bc), ALU.add).then_inc(out_mid, 1)

            for g in range(G):
                pool.memset(qs[g][3 * HD:P, :, :].bitcast(F32), 1.0).then_inc(consts_ready, 1)
            pool.wait_ge(consts_ready, n_consts)
            pool.wait_ge(weights_loaded, n_weights * DMA)
            if is_l0:
                for hf in range(2):
                    rstd(xln_mv, xln_var, xln_rstd, hf)
            bias_v(0, 0)
            bias_v(0, 1)
            if is_l1:
                for job in range(8):
                    edge_floor(0, 0, job)
            if n_late:
                pool.wait_ge(late_loaded, n_late * DMA)

            def graph(b, first, last):
                phase(b, 0, first, last)
                phase(b, 1, first, last)
                if not last:
                    bias_v(b + 1, 0)
                    bias_v(b + 1, 1)
                if is_l0:
                    rstd(cln_mv, cln_var, cln_rstd, b * 2)
                    normalise(b, 3)
                    bias_out_l0(b, 0)
                    rstd(cln_mv, cln_var, cln_rstd, b * 2 + 1)
                    bias_out_l0(b, 1)
                elif last:
                    normalise(b, 3)
                    close_half(b, 0)
                    close_half(b, 1)

            graph(0, True, False)
            with pool.Fori(1, last_b) as b:
                graph(b, False, False)
            graph(last_b, False, True)


def constants(nc, sems, ident, ones):
    with ExitStack() as ctx:
        cleared, made = nc.alloc_semaphore("ident_cleared"), nc.alloc_semaphore("ident_made")
        sems.extend((cleared, made))
        block = ctx.enter_context(nc.Block())

        @block.gpsimd
        def _(pool):
            pool.memset(ident[:, :], 0.0).then_inc(cleared, 1)
            pool.wait_ge(cleared, 1)
            pool.affine_select(out=ident[:, :], in_=ident[:, :], compare_op=ALU.not_equal, fill=1.0,
                               base=0, pattern=[[-1, P]], channel_multiplier=1).then_inc(made, 1)
            pool.memset(ones[:, :], 1.0).then_inc(made, 1)
            pool.wait_ge(made, 2)


def single_head_layer(nc, sems, x_in, x_out, adj, w, ident):
    NEG_BIG = -1e9
    SLOPE = 0.01
    X_STEPS, F_STEPS, K_STEP, Q_STEP, K_ROW_STEP = (2, 3), (4, 5), 6, 7, 7
    A_SLOTS = 4

    with ExitStack() as ctx:
        def sb(what, shape, dt=F32):
            return ctx.enter_context(nc.sbuf_tensor(f"L2_{what}", shape, dt))

        def sem(what):
            sems.append(nc.alloc_semaphore(f"L2_{what}"))
            return sems[-1]

        x_rows = [sb(f"x_rows{i}", [P, NC, D]) for i in range(2)]
        feat = [sb(f"feat{i}", [P, NC, D]) for i in range(2)]
        q_col = [sb(f"q_col{i}", [P, NC]) for i in range(2)]
        k_col = [sb(f"k_col{i}", [P, NC]) for i in range(2)]
        k_row = [sb(f"k_row{i}", [P, N]) for i in range(2)]
        xt = sb("x_t", [P, KC, N])
        adj_sb = [sb(f"adj{i}", [P, N]) for i in range(A_SLOTS)]
        logit = [sb(f"logit{i}", [P, N]) for i in range(2)]
        prob = [sb(f"prob{i}", [P, N]) for i in range(2)]
        prob_t = [sb(f"prob_t{i}", [P, NC, P]) for i in range(2)]
        neg_max, total, inv = sb("neg_max", [P, 4]), sb("total", [P, 4]), sb("inv", [P, 4])
        y = [sb(f"y{i}", [P, HC, D]) for i in range(2)]
        wfc, b_bc = sb("wfc", [P, KC, D]), sb("b_bc", [P, D])
        wq_bc, wk_bc, bq, bk = sb("wq_bc", [P, D]), sb("wk_bc", [P, D]), sb("bq", [P, 1]), sb("bk", [P, 1])
        minus_big = sb("minus_big", [P, 1])
        products = sb("products", [P, NC, D])

        turned = [ctx.enter_context(nc.psum_tensor(f"L2_turned{i}", [P, N], F32)) for i in range(2)]
        small = [ctx.enter_context(nc.psum_tensor(f"L2_small{i}", [P, HALF], F32)) for i in range(2)]
        out_ps = [ctx.enter_context(nc.psum_tensor(f"L2_out{i}", [P, HALF], F32)) for i in range(2)]

        weights_loaded, minus_big_ready = sem("weights_loaded"), sem("minus_big_ready")
        x_loaded = [sem(f"x_loaded{i}") for i in range(2)]
        adj_loaded = [sem(f"adj_loaded{i}") for i in range(A_SLOTS)]
        x_turned, xt_ready = sem("x_turned"), sem("xt_ready")
        f_made, f_copied, f_ready = sem("f_made"), sem("f_copied"), sem("f_ready")
        qk_ready, k_row_made, k_row_ready = sem("qk_ready"), sem("k_row_made"), sem("k_row_ready")
        mask_ready, masked, leaked, max_ready = sem("mask_ready"), sem("masked"), sem("leaked"), sem("max_ready")
        exp_done, p_turned, pt_ready = sem("exp_done"), sem("p_turned"), sem("pt_ready")
        attended, inv_ready, y_ready = sem("attended"), sem("inv_ready"), sem("y_ready")
        stored = [sem(f"stored{i}") for i in range(2)]
        n_weights = 6

        block = ctx.enter_context(nc.Block())

        def run(eng, graph):
            graph(0, 0, True, False)
            graph(1, 1, False, False)
            with eng.Fori(2, BATCH - 2, 2) as b:
                graph(b, 0, False, False)
                graph(b + 1, 1, False, False)
            graph(BATCH - 2, 0, False, False)
            graph(BATCH - 1, 1, False, True)

        @block.sync
        def _(sp):
            def load_adj(b, c, skip_wait=False):
                if not skip_wait:
                    sp.wait_ge(masked, b * NC + c - A_SLOTS + 1)
                sp.dma_start(adj_sb[c % A_SLOTS][:, :], adj[bass.ds(b, 1), c * P:(c + 1) * P, :].rearrange("o p m -> (o p) m")
                             ).then_inc(adj_loaded[c % A_SLOTS], DMA)

            def load_x(b, par):
                sp.dma_start(x_rows[par][:, :, :], x_in[bass.ds(b, 1), :, :].rearrange("o (c p) d -> p (o c) d", p=P)
                             ).then_inc(x_loaded[par], DMA)

            load_x(0, 0)
            for dst, src in ((wfc[:, :, :], w["W_fc"].rearrange("(k p) o -> p k o", p=P)),
                             (b_bc[:, :], w["b_fc"][None, :].to_broadcast([P, D])),
                             (wq_bc[:, :], w["w_q"].rearrange("d o -> o d").to_broadcast([P, D])),
                             (wk_bc[:, :], w["w_k"].rearrange("d o -> o d").to_broadcast([P, D])),
                             (bq[:, :], w["b_q"][None, :].to_broadcast([P, 1])),
                             (bk[:, :], w["b_k"][None, :].to_broadcast([P, 1]))):
                sp.dma_start(dst, src, allow_slow_non_contiguous=True).then_inc(weights_loaded, DMA)
            for c in range(A_SLOTS - 1):
                load_adj(0, c, True)

            def graph(b, par, first, last):
                for c in range(NC):
                    ahead = c + A_SLOTS - 1
                    if ahead < NC:
                        load_adj(b, ahead, first and ahead < A_SLOTS)
                    elif not last:
                        load_adj(b + 1, ahead - NC)
                    if c == 1 and not last:
                        if not first:
                            wait_from(sp, y_ready, (b + 1) * NC - NC)
                        load_x(b + 1, 1 - par)
                    if c == 2 and not first:
                        store(b - 1, 1)
                    if c == 6:
                        store(b, 0)
                if last:
                    store(b, 1)

            def store(b, hf):
                sp.wait_ge(y_ready, b * NC + hf * HC + HC)
                sp.dma_start(x_out[bass.ds(b, 1), hf * HALF:(hf + 1) * HALF, :].rearrange("o (c p) d -> p (o c) d", p=P),
                             y[hf][:, :, :]).then_inc(stored[hf], DMA)

            run(sp, graph)
            for hf in range(2):
                sp.wait_ge(stored[hf], BATCH * DMA)

        @block.tensor
        def _(pe):
            hist = [None, None]
            n_small = 0

            def small_slot(done_sem, done_value):
                nonlocal n_small
                if hist[-2] is not None:
                    pe.wait_ge(*hist[-2])
                hist.append((done_sem, done_value))
                n_small += 1
                return small[(n_small - 1) % 2]

            def turn_x(b, par, hf):
                pe.wait_ge(x_loaded[par], (b - par) * (DMA // 2) + DMA)
                for k in range(KC):
                    tile = small_slot(xt_ready, b * 4 + hf * 2 + k + 1)
                    for c in range(HC):
                        mm = pe.transpose(tile[:, c * P:(c + 1) * P], x_rows[par][:, hf * HC + c, k * P:(k + 1) * P], ident[:, :])
                    mm.then_inc(x_turned, 1)

            def project(b, hf):
                pe.wait_ge(xt_ready, (b + 1) * 4)
                for j in range(2):
                    tile = small_slot(f_copied, b * 4 + hf * 2 + j + 1)
                    for i in range(2):
                        c = hf * HC + j * 2 + i
                        for k in range(KC):
                            mm = pe.matmul(tile[:, i * D:(i + 1) * D], xt[:, k, c * P:(c + 1) * P], wfc[:, k, :],
                                           start=k == 0, stop=k == KC - 1)
                    mm.then_inc(f_made, 1)

            def spread_k(b, par):
                pe.wait_ge(qk_ready, b * 2 + 1)
                for hf in range(2):
                    tile = small_slot(k_row_ready, b * 2 + hf + 1)
                    for i in range(HC):
                        c = hf * HC + i
                        mm = pe.matmul(tile[:, i * P:(i + 1) * P], k_col[par][:, c:c + 1].to_broadcast([P, P]), ident[:, :],
                                       start=True, stop=True)
                    mm.then_inc(k_row_made, 1)

            def turn_p(b, c):
                n = b * NC + c
                pe.wait_ge(exp_done, n + 1)
                wait_from(pe, pt_ready, n - 1)
                for m in range(NC):
                    mm = pe.transpose(turned[c % 2][:, m * P:(m + 1) * P], prob[c % 2][:, m * P:(m + 1) * P], ident[:, :])
                mm.then_inc(p_turned, 1)

            def attend(b, par, c):
                n = b * NC + c
                pe.wait_ge(pt_ready, n + 1)
                wait_from(pe, y_ready, n - 1)
                for m in range(NC):
                    mm = pe.matmul(out_ps[c % 2][:, 0:D], prob_t[c % 2][:, m, :], feat[par][:, m, :],
                                   start=m == 0, stop=m == NC - 1)
                mm.then_inc(attended, 1)

            pe.wait_ge(weights_loaded, n_weights * DMA)
            for hf in range(2):
                turn_x(0, 0, hf)
            for hf in range(2):
                project(0, hf)
            spread_k(0, 0)

            def graph(b, par, first, last):
                hist[:] = [(k_row_ready, b * 2 + 1), (k_row_ready, b * 2 + 2)]
                for c in range(NC):
                    turn_p(b, c)
                    if c:
                        attend(b, par, c - 1)
                    elif not first:
                        attend(b - 1, 1 - par, NC - 1)
                    if not last:
                        if c in X_STEPS:
                            turn_x(b + 1, 1 - par, c - X_STEPS[0])
                        if c in F_STEPS:
                            project(b + 1, c - F_STEPS[0])
                        if c == K_ROW_STEP:
                            spread_k(b + 1, 1 - par)
                if last:
                    attend(b, par, NC - 1)

            run(pe, graph)

        @block.scalar
        def _(act):
            n_small = 0

            def small_slot():
                nonlocal n_small
                n_small += 1
                return small[(n_small - 1) % 2]

            def copy_xt(b, hf):
                for k in range(KC):
                    tile = small_slot()
                    act.wait_ge(x_turned, b * 4 + hf * 2 + k + 1)
                    act.activation(xt[:, k, hf * HALF:(hf + 1) * HALF], tile[:, :], ACT.Copy).then_inc(xt_ready, 1)

            def copy_f(b, par, hf):
                for j in range(2):
                    tile = small_slot()
                    c = hf * HC + j * 2
                    act.wait_ge(f_made, b * 4 + hf * 2 + j + 1)
                    act.activation(feat[par][:, c:c + 2, :].rearrange("p c d -> p (c d)"), tile[:, :], ACT.Copy).then_inc(f_copied, 1)

            def copy_k(b, par):
                for hf in range(2):
                    tile = small_slot()
                    act.wait_ge(k_row_made, b * 2 + hf + 1)
                    act.activation(k_row[par][:, hf * HALF:(hf + 1) * HALF], tile[:, :], ACT.Copy).then_inc(k_row_ready, 1)

            def mask(b, c):
                act.wait_ge(adj_loaded[c % A_SLOTS], (b * 2 + c // A_SLOTS + 1) * DMA)
                t = adj_sb[c % A_SLOTS]
                act.activation(t[:, :], t[:, :], ACT.Identity, bias=minus_big[:, :], scale=-NEG_BIG).then_inc(mask_ready, 1)

            def exp(b, c):
                n = b * NC + c
                act.wait_ge(max_ready, n + 1)
                wait_from(act, p_turned, n - 1)
                wait_from(act, inv_ready, n - 3)
                act.activation(prob[c % 2][:, :], logit[c % 2][:, :], ACT.Exp, bias=neg_max[:, c % 4:c % 4 + 1],
                               accum_out=total[:, c % 4:c % 4 + 1]).then_inc(exp_done, 1)

            def copy_pt(b, c):
                n = b * NC + c
                act.wait_ge(p_turned, n + 1)
                wait_from(act, attended, n - 1)
                act.activation(prob_t[c % 2][:, :, :].rearrange("p m n -> p (m n)"), turned[c % 2][:, :], ACT.Copy
                               ).then_inc(pt_ready, 1)

            act.wait_ge(minus_big_ready, 1)
            mask(0, 0)
            mask(0, 1)
            for hf in range(2):
                copy_xt(0, hf)
            for hf in range(2):
                copy_f(0, 0, hf)
            copy_k(0, 0)
            exp(0, 0)

            def graph(b, par, first, last):
                for c in range(NC):
                    if c + 2 < NC:
                        mask(b, c + 2)
                    elif not last:
                        mask(b + 1, c + 2 - NC)
                    copy_pt(b, c)
                    if c < NC - 1:
                        exp(b, c + 1)
                    if not last:
                        if c in X_STEPS:
                            copy_xt(b + 1, c - X_STEPS[0])
                        if c in F_STEPS:
                            copy_f(b + 1, 1 - par, c - F_STEPS[0])
                        if c == K_ROW_STEP:
                            copy_k(b + 1, 1 - par)
                        if c == NC - 1:
                            exp(b + 1, 0)

            run(act, graph)

        @block.vector
        def _(dve):
            def numbers(b, par, i):
                col, wt, bias = ((k_col, wk_bc, bk), (q_col, wq_bc, bq))[i]
                dve.wait_ge(f_ready, (b + 1) * 2)
                wait_from(dve, qk_ready, b * 2 + i)
                for c in range(NC):
                    op = dve.tensor_tensor_reduce(products[:, c, :], feat[par][:, c, :], wt[:, :], 1.0, bias[:, 0:1], ALU.mult, ALU.add,
                                                  col[par][:, c:c + 1])
                op.then_inc(qk_ready, 1)

            def logits(b, par, c):
                n = b * NC + c
                z = logit[c % 2]
                if c == 0:
                    dve.wait_ge(k_row_ready, (b + 1) * 2)
                    dve.wait_ge(qk_ready, (b + 1) * 2)
                dve.wait_ge(mask_ready, n + 1)
                wait_from(dve, exp_done, n - 1)
                dve.scalar_tensor_tensor(out=z[:, :], in0=k_row[par][:, :], scalar=q_col[par][:, c:c + 1],
                                         in1=adj_sb[c % A_SLOTS][:, :], op0=ALU.add, op1=ALU.add).then_inc(masked, 1)
                dve.wait_ge(masked, n + 1)
                dve.scalar_tensor_tensor(out=z[:, :], in0=z[:, :], scalar=SLOPE, in1=z[:, :], op0=ALU.mult, op1=ALU.max
                                         ).then_inc(leaked, 1)
                dve.wait_ge(leaked, n + 1)
                dve.tensor_reduce(neg_max[:, c % 4:c % 4 + 1], z[:, :], AX.X, ALU.max, negate=True).then_inc(max_ready, 1)

            def finish(b, par, c):
                n = b * NC + c
                dve.wait_ge(exp_done, n + 1)
                dve.reciprocal(inv[:, c % 4:c % 4 + 1], total[:, c % 4:c % 4 + 1]).then_inc(inv_ready, 1)
                dve.wait_ge(inv_ready, n + 1)
                dve.wait_ge(attended, n + 1)
                if c % HC == 0:
                    wait_from(dve, stored[c // HC], b * DMA)
                dve.scalar_tensor_tensor(out=y[c // HC][:, c % HC, :], in0=out_ps[c % 2][:, 0:D], scalar=inv[:, c % 4:c % 4 + 1],
                                         in1=x_rows[par][:, c, :], op0=ALU.mult, op1=ALU.add).then_inc(y_ready, 1)

            dve.memset(minus_big[:, :], NEG_BIG).then_inc(minus_big_ready, 1)
            dve.wait_ge(weights_loaded, n_weights * DMA)
            numbers(0, 0, 0)
            numbers(0, 0, 1)

            def graph(b, par, first, last):
                for c in range(NC):
                    logits(b, par, c)
                    if c >= 2:
                        finish(b, par, c - 2)
                    elif not first:
                        finish(b - 1, 1 - par, NC - 2 + c)
                    if c in (K_STEP, Q_STEP) and not last:
                        numbers(b + 1, 1 - par, (K_STEP, Q_STEP).index(c))
                if last:
                    finish(b, par, NC - 2)
                    finish(b, par, NC - 1)

            run(dve, graph)

        @block.gpsimd
        def _(pool):
            def bias_f(b, par):
                for hf in range(2):
                    pool.wait_ge(f_copied, b * 4 + hf * 2 + 2)
                    part = feat[par][:, hf * HC:(hf + 1) * HC, :]
                    pool.tensor_tensor(part, part, b_bc[:, None, :].to_broadcast([P, HC, D]), ALU.add).then_inc(f_ready, 1)

            pool.wait_ge(weights_loaded, n_weights * DMA)
            bias_f(0, 0)

            def graph(b, par, first, last):
                if not last:
                    bias_f(b + 1, 1 - par)

            run(pool, graph)


def clear(nc, sems):
    nc.clear_and_free_semaphores(sems)
    sems.clear()
    with nc.Block():
        pass


def program(nc, x, adj, weights, out):
    between = [nc.dram_tensor(f"x_after_{n}", [BATCH, N, D], F32).ap() for n in ("L0", "L1", "L2")]
    sums_d = nc.dram_tensor("sums_by_row", [4, GH, HALF], F32).ap()
    recips_d = nc.dram_tensor("recips_by_row", [4, GH, HALF], F32).ap()
    with ExitStack() as ctx:
        ident = ctx.enter_context(nc.sbuf_tensor("ident", [P, P], F32))
        ones = ctx.enter_context(nc.sbuf_tensor("ones", [P, HD], F32))
        sems = []
        constants(nc, sems, ident, ones)
        attention_layer(nc, sems, "L0", x, between[0], adj, weights["L0"], ident, ones, sums_d, recips_d)
        clear(nc, sems)
        attention_layer(nc, sems, "L1", between[0], between[1], adj, weights["L1"], ident, ones, sums_d, recips_d)
        clear(nc, sems)
        single_head_layer(nc, sems, between[1], between[2], adj, weights["L2"], ident)
        clear(nc, sems)
        attention_layer(nc, sems, "L3", between[2], out, adj, weights["L3"], ident, ones, sums_d, recips_d)


_SAME = {n: n for n in ("Wq", "bq", "Wk", "bk", "Wv", "bv", "Wo", "bo")}
_WEIGHTS = {
    "L0": {**_SAME, **{n: n for n in ("g1", "b1", "g2", "b2", "Wf1", "bf1", "Wf2", "bf2")}},
    "L1": {"Wq": "W_q", "bq": "b_q", "Wk": "W_k", "bk": "b_k", "Wv": "W_v", "bv": "b_v", "w_g": "w_g", "b_g": "b_g"},
    "L2": {n: n for n in ("W_fc", "b_fc", "w_q", "b_q", "w_k", "b_k")},
    "L3": {**_SAME, "gamma": "gamma", "beta": "beta"},
}


def kernel(**inputs):
    import numpy as _np
    import concourse.bacc as _bacc
    from concourse import mybir as _mybir
    from concourse.bass_utils import run_bass_kernel_spmd as _run

    nc = _bacc.Bacc("TRN2", target_bir_lowering=False, num_devices=1)
    arrays = {}

    def declare(name):
        a = _np.ascontiguousarray(inputs[name])
        a = a.reshape(1, 1) if a.size == 1 and a.ndim == 0 else a
        arrays[f"in_{name}"] = a
        return nc.dram_tensor(f"in_{name}", list(a.shape), _mybir.dt.from_np(a.dtype), kind="ExternalInput").ap()

    x, adj = declare("x"), declare("adj")
    weights = {layer: {own: declare(f"{layer}_gnn_{n}") for own, n in names.items()} for layer, names in _WEIGHTS.items()}
    out = nc.dram_tensor("out", [BATCH, N, D], F32, kind="ExternalOutput").ap()
    program(nc, x, adj, weights, out)
    r = _run(nc, [arrays], core_ids=[0])
    return r.results[0]["out"]
```
